# Optimizing a Trainium2 kernel written in Bass

```python
import numpy as np
import jax
import jax.numpy as jnp

def _softmax(x, axis=-1):
    return jax.nn.softmax(x, axis=axis)

def _gelu(x):
    return jax.nn.gelu(x, approximate=True)

def _silu(x):
    return jax.nn.silu(x)

def _sigmoid(x):
    return jax.nn.sigmoid(x)

def _layernorm(x, axis=-1, eps=1e-05):
    m = jnp.mean(x, axis=axis, keepdims=True)
    v = jnp.var(x, axis=axis, keepdims=True)
    return (x - m) / jnp.sqrt(v + eps)

def _scatter_add(tgt, idx, src, axis=0):
    return tgt.at[idx].add(src)

def _segment_sum(src, seg, n):
    return jax.ops.segment_sum(src, seg, n)
kernel_name = 'mk_pixart_seq_d2_seqx_r4_7b0447'

def setup_inputs(seed: int=0):
    np.random.seed(seed)
    _w = jnp.asarray

    def _rec_inputs():
        import jax
        import jax.numpy as jnp
        _rk = jax.random.key(seed)
        x = -0.0003929 + 0.9999 * jax.random.normal(jax.random.fold_in(_rk, 1), (8, 112, 256), jnp.float32)
        _lenS = 112 - jax.random.randint(jax.random.fold_in(_rk, 7), (8,), 0, max(1, 112 // 4) + 1, jnp.int32)
        _lenS2 = 375 - jax.random.randint(jax.random.fold_in(_rk, 8), (8,), 0, max(1, 375 // 4) + 1, jnp.int32)
        _ctx_1024P = jax.random.normal(jax.random.fold_in(_rk, 11), (8, 16, 256), jnp.float32)
        _ctx_1024c = jax.random.dirichlet(jax.random.fold_in(_rk, 511), 0.3 * jnp.ones((16,), jnp.float32), (8, 375))
        _ctx_1024t = jnp.einsum('bsk,bkd->bsd', _ctx_1024c, _ctx_1024P)
        _ctx_1024t = _ctx_1024t * jax.lax.rsqrt(jnp.mean(jnp.square(_ctx_1024t)) + 1e-12) * 0.953939
        ctx_1024 = -1.39393e-06 + 0.999914 * (_ctx_1024t + 0.3 * jax.random.normal(jax.random.fold_in(_rk, 611), (8, 375, 256), jnp.float32))
        cond_1024 = -0.00920427 + 1.00102 * jax.random.normal(jax.random.fold_in(_rk, 12), (8, 256), jnp.float32)
        return (x, ctx_1024, cond_1024)
    x, ctx_1024, cond_1024 = _rec_inputs()

    def _L0_xcond_setup():
        import jax, jax.numpy as jnp
        import numpy as np
        EPS = 1e-05

        def _ada_ln(x, c, W_ss, b_ss):
            mu = jnp.mean(x, axis=-1, keepdims=True)
            var = jnp.mean((x - mu) ** 2, axis=-1, keepdims=True)
            h = (x - mu) / jnp.sqrt(var + EPS)
            ss = jax.nn.silu(c) @ W_ss + b_ss
            scale, bias = jnp.split(ss, 2, axis=-1)
            return (1.0 + scale)[:, None, :] * h + bias[:, None, :]
        key = jax.random.key(seed)
        ks = jax.random.split(key, 12)
        B, Lq, Lkv, H = (8, 512, 128, 256)
        s = 0.02
        return {'x_q': jax.random.normal(ks[0], (B, Lq, H), jnp.float32), 'x_kv': jax.random.normal(ks[1], (B, Lkv, H), jnp.float32), 't_vec': jax.random.normal(ks[2], (B, H), jnp.float32), 'Wq': jax.random.normal(ks[3], (H, H), jnp.float32) * s, 'bq': jnp.zeros((H,), jnp.float32), 'Wkv': jax.random.normal(ks[4], (H, 2 * H), jnp.float32) * s, 'bkv': jnp.zeros((2 * H,), jnp.float32), 'Wp': jax.random.normal(ks[5], (H, H), jnp.float32) * s, 'bp': jnp.zeros((H,), jnp.float32), 'Wss_q': jax.random.normal(ks[6], (H, 2 * H), jnp.float32) * s, 'bss_q': jnp.zeros((2 * H,), jnp.float32), 'Wss_kv': jax.random.normal(ks[7], (H, 2 * H), jnp.float32) * s, 'bss_kv': jnp.zeros((2 * H,), jnp.float32)}
    _L0_xcond_all = _L0_xcond_setup()
    _L0_xcond_in = {k: v for k, v in _L0_xcond_all.items() if k in ('Wq', 'bq', 'Wkv', 'bkv', 'Wp', 'bp', 'Wss_q', 'bss_q', 'Wss_kv', 'bss_kv')}
    del _L0_xcond_all

    def _L1_xcond_setup():
        import jax, jax.numpy as jnp
        import numpy as np
        EPS = 1e-06
        H = 16

        def layer_norm(x, gamma=None, beta=None):
            x32 = x.astype(jnp.float32)
            mu = jnp.mean(x32, axis=-1, keepdims=True)
            var = jnp.var(x32, axis=-1, keepdims=True)
            y = (x32 - mu) * jax.lax.rsqrt(var + EPS)
            if gamma is not None:
                y = y * gamma + beta
            return y.astype(x.dtype)

        def mha(q, k, v):
            B, Nq, C = q.shape
            d = C // H
            qh = q.reshape(B, Nq, H, d)
            kh = k.reshape(B, k.shape[1], H, d)
            vh = v.reshape(B, v.shape[1], H, d)
            scores = jnp.einsum('bqhd,bkhd->bhqk', qh, kh) / jnp.sqrt(jnp.asarray(d, q.dtype))
            attn = jax.nn.softmax(scores, axis=-1)
            out = jnp.einsum('bhqk,bkhd->bqhd', attn, vh)
            return out.reshape(B, Nq, C)
        key = jax.random.key(seed)
        ks = jax.random.split(key, 24)
        B, N, C, M, Cc = (4, 512, 256, 256, 256)
        hid = 4 * C
        s = 0.02
        return {'x': jax.random.normal(ks[0], (B, N, C), jnp.float32), 'mod': jax.random.normal(ks[1], (B, C), jnp.float32), 'context': jax.random.normal(ks[2], (B, M, Cc), jnp.float32), 'ada_w': jax.random.normal(ks[3], (C, 6 * C), jnp.float32) * s, 'ada_b': jnp.zeros((6 * C,), jnp.float32), 'qkv_w': jax.random.normal(ks[4], (C, 3 * C), jnp.float32) * s, 'qkv_b': jnp.zeros((3 * C,), jnp.float32), 'self_o_w': jax.random.normal(ks[5], (C, C), jnp.float32) * s, 'self_o_b': jnp.zeros((C,), jnp.float32), 'norm2_g': jnp.ones((C,), jnp.float32), 'norm2_b': jnp.zeros((C,), jnp.float32), 'q_w': jax.random.normal(ks[6], (C, C), jnp.float32) * s, 'q_b': jnp.zeros((C,), jnp.float32), 'kv_w': jax.random.normal(ks[7], (Cc, 2 * C), jnp.float32) * s, 'kv_b': jnp.zeros((2 * C,), jnp.float32), 'cross_o_w': jax.random.normal(ks[8], (C, C), jnp.float32) * s, 'cross_o_b': jnp.zeros((C,), jnp.float32), 'mlp_w1': jax.random.normal(ks[9], (C, hid), jnp.float32) * s, 'mlp_b1': jnp.zeros((hid,), jnp.float32), 'mlp_w2': jax.random.normal(ks[10], (hid, C), jnp.float32) * s, 'mlp_b2': jnp.zeros((C,), jnp.float32)}
    _L1_xcond_all = _L1_xcond_setup()
    _L1_xcond_in = {k: v for k, v in _L1_xcond_all.items() if k in ('ada_w', 'ada_b', 'qkv_w', 'qkv_b', 'self_o_w', 'self_o_b', 'norm2_g', 'norm2_b', 'q_w', 'q_b', 'kv_w', 'kv_b', 'cross_o_w', 'cross_o_b', 'mlp_w1', 'mlp_b1', 'mlp_w2', 'mlp_b2')}
    del _L1_xcond_all
    return {'x': x, 'ctx_1024': ctx_1024, 'cond_1024': cond_1024, 'L0_xcond_Wq': _L0_xcond_in['Wq'], 'L0_xcond_bq': _L0_xcond_in['bq'], 'L0_xcond_Wkv': _L0_xcond_in['Wkv'], 'L0_xcond_bkv': _L0_xcond_in['bkv'], 'L0_xcond_Wp': _L0_xcond_in['Wp'], 'L0_xcond_bp': _L0_xcond_in['bp'], 'L0_xcond_Wss_q': _L0_xcond_in['Wss_q'], 'L0_xcond_bss_q': _L0_xcond_in['bss_q'], 'L0_xcond_Wss_kv': _L0_xcond_in['Wss_kv'], 'L0_xcond_bss_kv': _L0_xcond_in['bss_kv'], 'L1_xcond_ada_w': _L1_xcond_in['ada_w'], 'L1_xcond_ada_b': _L1_xcond_in['ada_b'], 'L1_xcond_qkv_w': _L1_xcond_in['qkv_w'], 'L1_xcond_qkv_b': _L1_xcond_in['qkv_b'], 'L1_xcond_self_o_w': _L1_xcond_in['self_o_w'], 'L1_xcond_self_o_b': _L1_xcond_in['self_o_b'], 'L1_xcond_norm2_g': _L1_xcond_in['norm2_g'], 'L1_xcond_norm2_b': _L1_xcond_in['norm2_b'], 'L1_xcond_q_w': _L1_xcond_in['q_w'], 'L1_xcond_q_b': _L1_xcond_in['q_b'], 'L1_xcond_kv_w': _L1_xcond_in['kv_w'], 'L1_xcond_kv_b': _L1_xcond_in['kv_b'], 'L1_xcond_cross_o_w': _L1_xcond_in['cross_o_w'], 'L1_xcond_cross_o_b': _L1_xcond_in['cross_o_b'], 'L1_xcond_mlp_w1': _L1_xcond_in['mlp_w1'], 'L1_xcond_mlp_b1': _L1_xcond_in['mlp_b1'], 'L1_xcond_mlp_w2': _L1_xcond_in['mlp_w2'], 'L1_xcond_mlp_b2': _L1_xcond_in['mlp_b2']}

def reference(x, ctx_1024, cond_1024, L0_xcond_Wq, L0_xcond_bq, L0_xcond_Wkv, L0_xcond_bkv, L0_xcond_Wp, L0_xcond_bp, L0_xcond_Wss_q, L0_xcond_bss_q, L0_xcond_Wss_kv, L0_xcond_bss_kv, L1_xcond_ada_w, L1_xcond_ada_b, L1_xcond_qkv_w, L1_xcond_qkv_b, L1_xcond_self_o_w, L1_xcond_self_o_b, L1_xcond_norm2_g, L1_xcond_norm2_b, L1_xcond_q_w, L1_xcond_q_b, L1_xcond_kv_w, L1_xcond_kv_b, L1_xcond_cross_o_w, L1_xcond_cross_o_b, L1_xcond_mlp_w1, L1_xcond_mlp_b1, L1_xcond_mlp_w2, L1_xcond_mlp_b2):
    import jax
    import jax.numpy as jnp

    def _L0_xcond_ref(x_q, x_kv, t_vec, Wq, bq, Wkv, bkv, Wp, bp, Wss_q, bss_q, Wss_kv, bss_kv):
        import jax, jax.numpy as jnp
        import numpy as np
        EPS = 1e-05

        def _ada_ln(x, c, W_ss, b_ss):
            mu = jnp.mean(x, axis=-1, keepdims=True)
            var = jnp.mean((x - mu) ** 2, axis=-1, keepdims=True)
            h = (x - mu) / jnp.sqrt(var + EPS)
            ss = jax.nn.silu(c) @ W_ss + b_ss
            scale, bias = jnp.split(ss, 2, axis=-1)
            return (1.0 + scale)[:, None, :] * h + bias[:, None, :]
        B, Lq, H = x_q.shape
        Lkv = x_kv.shape[1]
        nh = 16
        dh = H // nh
        xq = _ada_ln(x_q, t_vec, Wss_q, bss_q)
        xkv = _ada_ln(x_kv, t_vec, Wss_kv, bss_kv)
        q = (xq @ Wq + bq).reshape(B, Lq, nh, dh)
        kv = (xkv @ Wkv + bkv).reshape(B, Lkv, 2, nh, dh)
        k = kv[:, :, 0]
        v = kv[:, :, 1]
        scores = jnp.einsum('bqhd,bkhd->bhqk', q, k) / jnp.sqrt(jnp.float32(dh))
        attn = jax.nn.softmax(scores, axis=-1)
        out = jnp.einsum('bhqk,bkhd->bqhd', attn, v).reshape(B, Lq, H)
        return x_q + (out @ Wp + bp)

    def _L1_xcond_ref(x, mod, context, ada_w, ada_b, qkv_w, qkv_b, self_o_w, self_o_b, norm2_g, norm2_b, q_w, q_b, kv_w, kv_b, cross_o_w, cross_o_b, mlp_w1, mlp_b1, mlp_w2, mlp_b2):
        import jax, jax.numpy as jnp
        import numpy as np
        EPS = 1e-06
        H = 16

        def layer_norm(x, gamma=None, beta=None):
            x32 = x.astype(jnp.float32)
            mu = jnp.mean(x32, axis=-1, keepdims=True)
            var = jnp.var(x32, axis=-1, keepdims=True)
            y = (x32 - mu) * jax.lax.rsqrt(var + EPS)
            if gamma is not None:
                y = y * gamma + beta
            return y.astype(x.dtype)

        def mha(q, k, v):
            B, Nq, C = q.shape
            d = C // H
            qh = q.reshape(B, Nq, H, d)
            kh = k.reshape(B, k.shape[1], H, d)
            vh = v.reshape(B, v.shape[1], H, d)
            scores = jnp.einsum('bqhd,bkhd->bhqk', qh, kh) / jnp.sqrt(jnp.asarray(d, q.dtype))
            attn = jax.nn.softmax(scores, axis=-1)
            out = jnp.einsum('bhqk,bkhd->bqhd', attn, vh)
            return out.reshape(B, Nq, C)
        C = x.shape[-1]
        m = jax.nn.silu(mod) @ ada_w + ada_b
        shift_msa, scale_msa, gate_msa, shift_mlp, scale_mlp, gate_mlp = [c[:, None, :] for c in jnp.split(m, 6, axis=-1)]
        h = layer_norm(x)
        h = h * (1.0 + scale_msa) + shift_msa
        qkv = h @ qkv_w + qkv_b
        q, k, v = jnp.split(qkv, 3, axis=-1)
        h = mha(q, k, v) @ self_o_w + self_o_b
        x = x + h * gate_msa
        h = layer_norm(x, norm2_g, norm2_b)
        q = h @ q_w + q_b
        kv = context @ kv_w + kv_b
        k, v = jnp.split(kv, 2, axis=-1)
        h = mha(q, k, v) @ cross_o_w + cross_o_b
        x = x + h
        h = layer_norm(x)
        h = h * (1.0 + scale_mlp) + shift_mlp
        h = jax.nn.gelu(h @ mlp_w1 + mlp_b1) @ mlp_w2 + mlp_b2
        x = x + h * gate_mlp
        return x
    x = _L0_xcond_ref(x, ctx_1024, cond_1024, L0_xcond_Wq, L0_xcond_bq, L0_xcond_Wkv, L0_xcond_bkv, L0_xcond_Wp, L0_xcond_bp, L0_xcond_Wss_q, L0_xcond_bss_q, L0_xcond_Wss_kv, L0_xcond_bss_kv)
    x = _L1_xcond_ref(x, cond_1024, ctx_1024, L1_xcond_ada_w, L1_xcond_ada_b, L1_xcond_qkv_w, L1_xcond_qkv_b, L1_xcond_self_o_w, L1_xcond_self_o_b, L1_xcond_norm2_g, L1_xcond_norm2_b, L1_xcond_q_w, L1_xcond_q_b, L1_xcond_kv_w, L1_xcond_kv_b, L1_xcond_cross_o_w, L1_xcond_cross_o_b, L1_xcond_mlp_w1, L1_xcond_mlp_b1, L1_xcond_mlp_w2, L1_xcond_mlp_b2)
    return x

_drawn_inputs = setup_inputs


def setup_inputs(seed=0):
    import zlib

    import numpy as np

    out = dict(_drawn_inputs(seed))
    spreads = {'L0_xcond_bq': (0.0, 2.0),
     'L0_xcond_bkv': (0.0, 0.1),
     'L0_xcond_bp': (0.0, 0.1),
     'L0_xcond_bss_q': (0.0, 0.8),
     'L0_xcond_bss_kv': (0.0, 0.65),
     'L1_xcond_ada_b': (0.0, 0.387),
     'L1_xcond_qkv_b': (0.0, 0.8),
     'L1_xcond_self_o_b': (0.0, 0.372),
     'L1_xcond_norm2_g': (1.0, 0.6),
     'L1_xcond_norm2_b': (0.0, 2.0),
     'L1_xcond_q_b': (0.0, 2.0),
     'L1_xcond_kv_b': (0.0, 0.281),
     'L1_xcond_cross_o_b': (0.0, 0.1),
     'L1_xcond_mlp_b1': (0.0, 0.8),
     'L1_xcond_mlp_b2': (0.0, 0.38)}
    factors = {'L0_xcond_Wq': 8.0,
     'L0_xcond_Wss_q': 8.0,
     'L1_xcond_qkv_w': 8.0,
     'L1_xcond_self_o_w': 5.924,
     'L1_xcond_q_w': 33.404}
    for name, (base, spread) in spreads.items():
        noise = np.random.default_rng([zlib.crc32(name.encode()), seed]).standard_normal(out[name].shape)
        drawn = base * np.exp(spread * noise) if base else spread * noise
        out[name] = jnp.asarray(drawn.astype(out[name].dtype))
    for name, factor in factors.items():
        out[name] = (out[name] * factor).astype(out[name].dtype)
    return out
```

```python
from contextlib import ExitStack

import concourse.bass as bass
from concourse import mybir

F32 = mybir.dt.float32
BF16 = mybir.dt.bfloat16
ALU = mybir.AluOpType
ACT = mybir.ActivationFunctionType
AX_X = mybir.AxisListType.X

P = 128
B, T, L, C = 8, 112, 375, 256
H, D = 16, 16
CH = C // P
HC = P // D
HID = 4 * C
KEYS = [min(P, L - k) for k in range(0, L, P)]
NT = len(KEYS)
PAIRS = B // 2
SCALE = float(D) ** -0.5

TERMS_K = [0, 1, 0, 1, 2, 0]
TERMS_Q = [0, 0, 1, 1, 0, 2]
NTERM = len(TERMS_K)
DEEP = NTERM * D
AUG = DEEP + 3

MODS = ["q_scale", "q_bias", "kv_scale", "kv_bias", "shift_msa", "scale_msa", "shift_mlp", "scale_mlp"]


def wait(eng, sem, count):
    if isinstance(count, int) and count <= 0:
        return
    eng.wait_ge(sem, count)


class Semaphores:

    def __init__(self, nc):
        self.nc, self.all = nc, []

    def new(self, name):
        self.all.append(self.nc.alloc_semaphore(name))
        return self.all[-1]

    def __enter__(self):
        return self

    def __exit__(self, *_):
        self.nc.clear_and_free_semaphores(self.all)
        self.nc.all_engine_barrier()


class Shared:
    pass


def allocate(nc, ctx, dram):
    sh = Shared()

    def sb(name, shape, dt=F32):
        return ctx.enter_context(nc.sbuf_tensor(name, shape, dt))

    sh.dram = dram
    sh.bank = [ctx.enter_context(nc.psum_tensor(f"bank{i}", [P, 512], F32)) for i in range(8)]
    sh.ident = sb("ident", [P, P])
    sh.ident_bf = sb("ident_bf", [P, P], BF16)
    sh.x = sb("x_tokens", [T, B, C])
    sh.ctx = sb("ctx_tokens", [P, B, NT, C])
    sh.ctx_mean = sb("ctx_mean", [P, B, NT])
    sh.ctx_rstd = sb("ctx_rstd", [P, B, NT])
    sh.zero = sb("zero", [P, CH * 2 * T])
    sh.mod = sb("mod", [P, len(MODS), CH, B])
    sh.gate = sb("gate", [T, 2, B, C])
    sh.wq0 = sb("wq0", [P, CH, C])
    sh.wkv0 = sb("wkv0", [P, CH, 2 * C])
    sh.wo0 = sb("wo0", [P, CH, C])
    sh.wqkv1 = sb("wqkv1", [P, CH, 3 * C])
    sh.wo1 = sb("wo1", [P, CH, C])
    sh.wq2 = sb("wq2", [P, CH, C])
    sh.wkv2 = sb("wkv2", [P, CH, 2 * C])
    sh.wo2 = sb("wo2", [P, CH, C])
    sh.bcol = sb("bias_columns", [P, 9, CH])
    sh.bhid = sb("bias_hidden", [P, HID // P])
    sh.brow = sb("bias_rows", [P, 7, C])
    sh.q_all = sb("q_stack_all", [DEEP, B, H, T], BF16)
    k_space = sb("k_stack_all", [P, B, H, T], BF16)
    sh.k_all = k_space[0:DEEP]
    mod_w = k_space[:, :, :, :].rearrange("p b h n -> p (b h n)").bitcast(F32)
    sh.wss = mod_w[:, 0:CH * 4 * C].rearrange("p (k n) -> p k n", k=CH)
    sh.ctx_t = [mod_w[:, i * CH * L:(i + 1) * CH * L].rearrange("p (c n) -> p c n", c=CH) for i in range(4)]
    at = 4 * CH * L
    sh.w1 = mod_w[:, at:at + CH * HID].rearrange("p (k n) -> p k n", k=CH)
    sh.w2 = mod_w[:, at + CH * HID:at + 2 * CH * HID].rearrange("p (k n) -> p k n", n=C)
    sh.wada = mod_w[:, CH * 4 * C:CH * 10 * C].rearrange("p (k n) -> p k n", k=CH)
    sh.v_all = sb("v_all", [T, B, H, D + 1])
    sh.q_st = [sb(f"q_stack{i}", [AUG, H, T], BF16) for i in range(2)]
    sh.k_st = [sb(f"k_stack{i}", [AUG, H, NT * P], BF16) for i in range(2)]
    sh.v_sb = [sb(f"v_tokens{i}", [P, NT, H, D + 1]) for i in range(2)]
    return sh


BIAS_COLS = ["bq0", "bk0", "bq1", "bk1", "g2", "b2", "bq2", "bk2", "spare"]
BIAS_ROWS = ["bv0", "bp0", "bv1", "bo1", "bv2", "bo2", "bmlp2"]


def phase_load(nc, sh, ins):
    with ExitStack() as ctx:
        semaphores = ctx.enter_context(Semaphores(nc))

        def sb(name, shape, dt=F32):
            return ctx.enter_context(nc.sbuf_tensor(name, shape, dt))

        def sem(name):
            return semaphores.new(name)

        wss, wada = sh.wss, sh.wada
        bmod = sb("bmod", [P, len(MODS), CH])
        bgate = sb("bgate", [B, 2, C])
        cond = sb("cond", [B, C])
        e = sb("cond_exp", [B, C])
        den = sb("cond_den", [B, C])
        sig = sb("cond_sig", [B, C])
        silu = sb("cond_silu", [B, C])
        silu_t = sb("cond_silu_t", [P, CH, B])
        gates = sb("gates", [B, 2, C])
        stats = sb("ctx_stats", [P, B, NT, 6])
        mv = sb("ctx_mv", [P, B, NT, 2])
        veps = sb("ctx_veps", [P, B, NT])
        half = sb("ctx_half", [P, B, NT])

        cond_in, x_in, ctx_in, mod_in, w_in = (sem(n) for n in ("cond_in", "x_in", "ctx_in", "mod_in", "w_in"))
        zeroed, ident_set, half_set, ctx_zero = (sem(n) for n in ("zeroed", "ident_set", "half_set", "ctx_zero"))
        exp_done, silu_step, silu_ready, silu_t_psum, silu_t_ready = (
            sem(n) for n in ("exp_done", "silu_step", "silu_ready", "silu_t_psum", "silu_t_ready"))
        mod_psum, gate_psum, mod_step, gates_ready, gate_dram, gate_in = (
            sem(n) for n in ("mod_psum", "gate_psum", "mod_step", "gates_ready", "gate_dram", "gate_in"))
        stats_done, aggr_done, veps_done, rstd_done, ones_set = (
            sem(n) for n in ("stats_done", "aggr_done", "veps_done", "rstd_done", "ones_set"))
        where = [(wss, 0), (wss, C), (wss, 2 * C), (wss, 3 * C), (wada, 0), (wada, C), (wada, 3 * C), (wada, 4 * C)]
        gate_at = [2 * C, 5 * C]
        n_w = [0]

        with nc.Block() as block:
            @block.sync
            def _(sp):
                def chunks(w):
                    return w.rearrange("(k p) n -> p k n", p=P)

                def col(v):
                    return v.rearrange("(k p) -> p k", p=P)

                sp.dma_start(cond[:, :], ins["cond_1024"]).then_inc(cond_in, 16)
                sp.wait_ge(ctx_zero, 1)
                sp.dma_start(sh.ctx[:, :, 0, :], ins["ctx_1024"][:, 0:P, :].rearrange("b p c -> p b c")).then_inc(ctx_in, 16)
                sp.dma_start(sh.ctx[:, :, 1, :], ins["ctx_1024"][:, P:2 * P, :].rearrange("b p c -> p b c")).then_inc(ctx_in, 16)
                sp.dma_start(sh.ctx[0:KEYS[2], :, 2, :], ins["ctx_1024"][:, 2 * P:L, :].rearrange("b p c -> p b c")).then_inc(ctx_in, 16)
                sp.dma_start(wss[:, :, 0:2 * C], chunks(ins["L0_xcond_Wss_q"])).then_inc(mod_in, 16)
                sp.dma_start(wss[:, :, 2 * C:4 * C], chunks(ins["L0_xcond_Wss_kv"])).then_inc(mod_in, 16)
                sp.dma_start(wada[:, :, :], chunks(ins["L1_xcond_ada_w"])).then_inc(mod_in, 16)
                ada_b = ins["L1_xcond_ada_b"]
                with nc.allow_non_contiguous_dma(reason="biases, a few KB in all"):
                    for m, v in enumerate([ins["L0_xcond_bss_q"][0:C], ins["L0_xcond_bss_q"][C:2 * C],
                                           ins["L0_xcond_bss_kv"][0:C], ins["L0_xcond_bss_kv"][C:2 * C],
                                           ada_b[0:C], ada_b[C:2 * C], ada_b[3 * C:4 * C], ada_b[4 * C:5 * C]]):
                        sp.dma_start(bmod[:, m, :], col(v)).then_inc(mod_in, 16)
                    for g in range(2):
                        sp.dma_start(bgate[:, g, :], ada_b[gate_at[g]:gate_at[g] + C].partition_broadcast(B)).then_inc(mod_in, 16)
                    for i, v in enumerate([ins["L0_xcond_bq"], ins["L0_xcond_bkv"][0:C], ins["L1_xcond_qkv_b"][0:C],
                                           ins["L1_xcond_qkv_b"][C:2 * C], ins["L1_xcond_norm2_g"], ins["L1_xcond_norm2_b"],
                                           ins["L1_xcond_q_b"], ins["L1_xcond_kv_b"][0:C]]):
                        sp.dma_start(sh.bcol[:, i, :], col(v)).then_inc(w_in, 16)
                        n_w[0] += 16
                    sp.dma_start(sh.bhid[:, :], col(ins["L1_xcond_mlp_b1"])).then_inc(w_in, 16)
                    n_w[0] += 16
                for w, name in ((sh.wq0, "L0_xcond_Wq"), (sh.wkv0, "L0_xcond_Wkv"), (sh.wo0, "L0_xcond_Wp"),
                                (sh.wqkv1, "L1_xcond_qkv_w"), (sh.wo1, "L1_xcond_self_o_w"), (sh.wq2, "L1_xcond_q_w"),
                                (sh.wkv2, "L1_xcond_kv_w"), (sh.wo2, "L1_xcond_cross_o_w")):
                    sp.dma_start(w[:, :, :], chunks(ins[name])).then_inc(w_in, 16)
                    n_w[0] += 16
                for i, v in enumerate([ins["L0_xcond_bkv"][C:2 * C], ins["L0_xcond_bp"], ins["L1_xcond_qkv_b"][2 * C:3 * C],
                                       ins["L1_xcond_self_o_b"], ins["L1_xcond_kv_b"][C:2 * C], ins["L1_xcond_cross_o_b"],
                                       ins["L1_xcond_mlp_b2"]]):
                    sp.dma_start(sh.brow[:, i, :], v.partition_broadcast(P)).then_inc(w_in, 16)
                    n_w[0] += 16
                sp.dma_start(sh.x[:, :, :], ins["x"].rearrange("b n c -> n b c")).then_inc(x_in, 16)
                sp.wait_ge(gates_ready, 2)
                sp.dma_start(sh.dram["gate"], gates[:, :, :]).then_inc(gate_dram, 16)
                sp.wait_ge(gate_dram, 16)
                for g in range(2):
                    sp.dma_start(sh.gate[:, g, :, :], sh.dram["gate"][:, g, :].partition_broadcast(T)).then_inc(gate_in, 16)
                sp.wait_ge(gate_in, 32)
                sp.wait_ge(x_in, 16)
                sp.wait_ge(w_in, n_w[0])

            @block.gpsimd
            def _(pool):
                pool.memset(sh.ident[:, :], 0.0).then_inc(zeroed, 1)
                pool.memset(sh.ident_bf[:, :], 0.0).then_inc(zeroed, 1)
                pool.wait_ge(zeroed, 2)
                for m in (sh.ident, sh.ident_bf):
                    pool.affine_select(out=m[:, :], in_=m[:, :], compare_op=ALU.not_equal, fill=1.0,
                                       base=0, pattern=[[-1, P]], channel_multiplier=1).then_inc(ident_set, 1)
                pool.memset(sh.zero[:, :], 0.0)
                pool.memset(half[:, :, :], -0.5).then_inc(half_set, 1)
                for s in range(2):
                    pool.memset(sh.k_st[s][:, :, :], 0.0).then_inc(ones_set, 1)
                    pool.memset(sh.v_sb[s][:, :, :, D:D + 1], 1.0)
                pool.memset(sh.v_all[:, :, :, D:D + 1], 1.0)
                pool.wait_ge(half_set, 1)
                pool.wait_ge(veps_done, 1)
                pool.tensor_tensor(sh.ctx_rstd[:, :, :], veps[:, :, :], half[:, :, :], ALU.pow).then_inc(rstd_done, 1)

            @block.scalar
            def _(act):
                act.wait_ge(cond_in, 16)
                act.activation(e[:, :], cond[:, :], ACT.Exp, scale=-1.0).then_inc(exp_done, 1)

            @block.vector
            def _(dve):
                dve.memset(sh.ctx[96:P, :, NT - 1, :], 0.0).then_inc(ctx_zero, 1)
                dve.wait_ge(ones_set, 2)
                for s in range(2):
                    dve.memset(sh.k_st[s][DEEP:AUG, :, :], 1.0)
                dve.memset(sh.bank[4][:, :], 0.0)
                dve.wait_ge(exp_done, 1)
                dve.tensor_scalar(den[:, :], e[:, :], 1.0, None, ALU.add).then_inc(silu_step, 1)
                dve.wait_ge(silu_step, 1)
                dve.reciprocal(sig[:, :], den[:, :]).then_inc(silu_step, 1)
                dve.wait_ge(silu_step, 2)
                dve.tensor_tensor(silu[:, :], cond[:, :], sig[:, :], ALU.mult).then_inc(silu_ready, 1)
                dve.wait_ge(silu_t_psum, 1)
                dve.tensor_copy(silu_t[:, :, :], sh.bank[0][:, 0:CH * B].rearrange("p (k b) -> p k b", b=B)).then_inc(silu_t_ready, 1)
                dve.wait_ge(ctx_in, 48)
                for b in range(B):
                    for t in range(NT):
                        dve.bn_stats(stats[:, b, t, :], sh.ctx[:, b, t, :]).then_inc(stats_done, 1)
                dve.wait_ge(stats_done, B * NT)
                for b in range(B):
                    for t in range(NT):
                        dve.bn_aggr(mv[:, b, t, :], stats[:, b, t, :]).then_inc(aggr_done, 1)
                dve.wait_ge(aggr_done, B * NT)
                dve.tensor_scalar(veps[:, :, :], mv[:, :, :, 1], 1e-5, None, ALU.add).then_inc(veps_done, 1)
                dve.tensor_copy(sh.ctx_mean[:, :, :], mv[:, :, :, 0])
                dve.wait_ge(mod_psum, 1)
                mp = sh.bank[1][:, 0:len(MODS) * CH * B].rearrange("p (m k b) -> p m k b", k=CH, b=B)
                for m, name in enumerate(MODS):
                    plus = 1.0 if "scale" in name else 0.0
                    for k in range(CH):
                        dve.tensor_scalar(sh.mod[:, m, k, :], mp[:, m, k, :], bmod[:, m, k:k + 1], plus, ALU.add, ALU.add)
                dve.wait_ge(gate_psum, 1)
                for g in range(2):
                    dve.tensor_tensor(gates[:, g, :], sh.bank[2][0:B, g * C:(g + 1) * C], bgate[:, g, :], ALU.add).then_inc(gates_ready, 1)

            @block.tensor
            def _(pe):
                pe.wait_ge(silu_ready, 1)
                pe.wait_ge(ident_set, 2)
                for k in range(CH):
                    ins_ = pe.transpose(sh.bank[0][:, k * B:(k + 1) * B], silu[:, k * P:(k + 1) * P], sh.ident[0:B, 0:B])
                ins_.then_inc(silu_t_psum, 1)
                pe.wait_ge(silu_t_ready, 1)
                pe.wait_ge(mod_in, 16 * 13)
                for m in range(len(MODS)):
                    w, at = where[m]
                    for k in range(CH):
                        o = (m * CH + k) * B
                        for kk in range(CH):
                            ins_ = pe.matmul(sh.bank[1][:, o:o + B], w[:, kk, at + k * P:at + (k + 1) * P], silu_t[:, kk, :],
                                             start=kk == 0, stop=kk == CH - 1)
                ins_.then_inc(mod_psum, 1)
                for g in range(2):
                    for kk in range(CH):
                        ins_ = pe.matmul(sh.bank[2][0:B, g * C:(g + 1) * C], silu_t[:, kk, :],
                                         wada[:, kk, gate_at[g]:gate_at[g] + C], start=kk == 0, stop=kk == CH - 1)
                ins_.then_inc(gate_psum, 1)


def phase_project(nc, sh, name, eps, scale_of, bias_of, wq, bq, qkv):
    N2 = 2 * T
    with ExitStack() as ctx:
        semaphores = ctx.enter_context(Semaphores(nc))

        def sb(n, shape, dt=F32):
            return ctx.enter_context(nc.sbuf_tensor(f"{name}_{n}", shape, dt))

        def sem(n):
            return semaphores.new(f"{name}_{n}")

        stats, mv, veps, half, rstd, pause = sb("stats", [T, 2, 6]), sb("mv", [T, 2, 2]), sb("veps", [T, 2]), sb("half", [T, 2]), sb("rstd", [T, 2]), sb("pause", [T, 1])
        xn = sb("xn", [T, 2, C])
        xt = sb("xt", [P, CH, N2])
        kinds = ["q", "k"] if qkv else ["q"]
        full = {k: sb(f"{k}_full", [P, CH, N2]) for k in kinds}
        rest = {k: sb(f"{k}_rest", [P, CH, N2]) for k in kinds}
        part = {k: sb(f"{k}_part", [P, 3, CH, N2], BF16) for k in kinds}
        qb = sb("qb", [P, CH])
        zero = sh.zero[:, :].rearrange("p (c n) -> p c n", c=CH)
        half_set, qb_set, stats_done, aggr_done, veps_done, rstd_done, xn_done = (
            sem(n) for n in ("half_set", "qb_set", "stats_done", "aggr_done", "veps_done", "rstd_done", "xn_done"))
        xt_psum, xt_done, proj_psum, v_psum, full_done, v_done, split = (
            sem(n) for n in ("xt_psum", "xt_done", "proj_psum", "v_psum", "full_done", "v_done", "split"))
        written = {k: sem(f"{k}_written") for k in kinds}
        stacked = sem("stacked")
        NK = len(kinds)
        all_of = {"q": sh.q_all, "k": sh.k_all}
        bank_of = {"q": sh.bank[1], "k": sh.bank[2]}
        bias_col = {"q": qb, "k": sh.bcol[:, 3, :]}
        terms = {"q": TERMS_Q, "k": TERMS_K}

        with nc.Block() as block:
            @block.vector
            def _(dve):
                dve.tensor_scalar(qb[:, :], bq, SCALE, None, ALU.mult).then_inc(qb_set, 1)
                with dve.Fori(0, PAIRS) as p:
                    for j in range(2):
                        dve.bn_stats(stats[:, j, :], sh.x[:, bass.ds(2 * p + j, 1), :]).then_inc(stats_done, 1)
                    dve.wait_ge(stats_done, 2 * p + 2)
                    dve.memset(pause[:, :], 0.0)
                    for j in range(2):
                        dve.bn_aggr(mv[:, j, :], stats[:, j, :]).then_inc(aggr_done, 1)
                    dve.wait_ge(aggr_done, 2 * p + 2)
                    dve.tensor_scalar(veps[:, :], mv[:, :, 1], eps, None, ALU.add).then_inc(veps_done, 1)
                    dve.wait_ge(rstd_done, p + 1)
                    dve.wait_ge(xt_psum, p + 0)
                    for j in range(2):
                        dve.tensor_scalar(xn[:, j, :], sh.x[:, bass.ds(2 * p + j, 1), :], mv[:, j, 0:1], rstd[:, j:j + 1],
                                          ALU.subtract, ALU.mult).then_inc(xn_done, 1)
                    if qkv:
                        dve.wait_ge(v_psum, p + 1)
                        dve.tensor_tensor(sh.v_all[:, bass.ds(2 * p, 2), :, 0:D],
                                          sh.bank[3][0:T, :].rearrange("t (j h d) -> t j h d", j=2, d=D),
                                          sh.brow[0:T, 2:3, :].rearrange("t o (h d) -> t o h d", d=D).broadcast_to([T, 2, H, D]),
                                          ALU.add).then_inc(v_done, 1)

            @block.gpsimd
            def _(pool):
                pool.memset(half[:, :], -0.5).then_inc(half_set, 1)
                pool.wait_ge(half_set, 1)
                with pool.Fori(0, PAIRS) as p:
                    pool.wait_ge(veps_done, p + 1)
                    pool.tensor_tensor(rstd[:, :], veps[:, :], half[:, :], ALU.pow).then_inc(rstd_done, 1)
                    for i, k in enumerate(kinds):
                        n = 4 * (NK * p + i)
                        pool.wait_ge(full_done, CH * (NK * p + i + 1))
                        pool.wait_ge(written[k], 16 * p)
                        pool.tensor_tensor(part[k][:, 0, :, :], full[k][:, :, :], zero[:, :, :], ALU.add).then_inc(split, 1)
                        pool.wait_ge(split, n + 1)
                        pool.tensor_tensor(rest[k][:, :, :], full[k][:, :, :], part[k][:, 0, :, :], ALU.subtract).then_inc(split, 1)
                        pool.wait_ge(split, n + 2)
                        pool.tensor_tensor(part[k][:, 1, :, :], rest[k][:, :, :], zero[:, :, :], ALU.add).then_inc(split, 1)
                        pool.wait_ge(split, n + 3)
                        pool.tensor_tensor(part[k][:, 2, :, :], rest[k][:, :, :], part[k][:, 1, :, :], ALU.subtract).then_inc(split, 1)

            @block.scalar
            def _(act):
                act.wait_ge(qb_set, 1)
                with act.Fori(0, PAIRS) as p:
                    act.wait_ge(xt_psum, p + 1)
                    act.wait_ge(proj_psum, NK * p)
                    if qkv:
                        act.wait_ge(v_psum, p + 0)
                    for c in range(CH):
                        for j in range(2):
                            o = (c * 2 + j) * T
                            act.activation(xt[:, c, j * T:(j + 1) * T], sh.bank[0][:, o:o + T], ACT.Identity,
                                           bias=bias_of(c, 2 * p + j), scale=scale_of(c, 2 * p + j)).then_inc(xt_done, 1)
                    for i, k in enumerate(kinds):
                        act.wait_ge(proj_psum, NK * p + i + 1)
                        act.wait_ge(split, 4 * (NK * p + i) - 4 * (NK - 1) if NK == 1 else 4 * NK * p)
                        for m in range(CH):
                            act.activation(full[k][:, m, :], bank_of[k][:, m * N2:(m + 1) * N2], ACT.Identity,
                                           bias=bias_col[k][:, m:m + 1], scale=SCALE if k == "q" else 1.0).then_inc(full_done, 1)

            @block.tensor
            def _(pe):
                with pe.Fori(0, PAIRS) as p:
                    pe.wait_ge(xn_done, 2 * p + 2)
                    pe.wait_ge(xt_done, 4 * p)
                    for c in range(CH):
                        for j in range(2):
                            o = (c * 2 + j) * T
                            ins_ = pe.transpose(sh.bank[0][:, o:o + T], xn[:, j, c * P:(c + 1) * P], sh.ident[0:T, 0:T])
                    ins_.then_inc(xt_psum, 1)
                    pe.wait_ge(xt_done, 4 * p + 4)
                    for i, k in enumerate(kinds):
                        pe.wait_ge(full_done, CH * NK * p)
                        for m in range(CH):
                            for c in range(CH):
                                ins_ = pe.matmul(bank_of[k][:, m * N2:(m + 1) * N2],
                                                 wq[:, c, i * C + m * P:i * C + (m + 1) * P], xt[:, c, :],
                                                 start=c == 0, stop=c == CH - 1)
                        ins_.then_inc(proj_psum, 1)
                    if qkv:
                        pe.wait_ge(v_done, p + 0)
                        for j in range(2):
                            for c in range(CH):
                                ins_ = pe.matmul(sh.bank[3][0:T, j * C:(j + 1) * C], xt[:, c, j * T:(j + 1) * T],
                                                 wq[:, c, 2 * C:3 * C], start=c == 0, stop=c == CH - 1)
                        ins_.then_inc(v_psum, 1)

            @block.sync
            def _(sp):
                with sp.Fori(0, PAIRS) as p:
                    for i, k in enumerate(kinds):
                        sp.wait_ge(split, 4 * (NK * p + i + 1))
                        d = sh.dram[f"{k}_parts"]
                        sp.dma_start(d[bass.ds(p, 1)].rearrange("o t c p n -> p (o t) c n"), part[k][:, :, :, :]).then_inc(written[k], 16)
                        sp.wait_ge(qb_set, 1)
                        sp.wait_ge(written[k], 16 * p + 16)
                        for s, w in enumerate(terms[k]):
                            for j in range(2):
                                sp.dma_start(all_of[k][s * D:(s + 1) * D, bass.ds(2 * p + j, 1), :, :],
                                             d[bass.ds(p, 1), w, :, :, j * T:(j + 1) * T].rearrange("o c (h d) n -> d o (c h) n", d=D)
                                             ).then_inc(stacked, 16)
                sp.wait_ge(stacked, 16 * NTERM * 2 * NK * PAIRS)


def phase_attend(nc, sh, name, cross, ln, wkv, bk, bv_row, wo, bo_row, gate):
    keys = KEYS if cross else [T]
    nt = len(keys)
    nk = sum(keys)
    GH = 4
    NG = H // GH
    NU = NG * nt
    HS = 1 if cross else 4
    NS = H // HS
    S_AT = [(NS * (u + 1)) // (NU + 1) for u in range(-1, NU + 1)]
    FILLS = ["T0", "T1", "K0", "K1", "V0", "V1"]
    FILL_AT = {0: 0, 1: 1, 3: 2, 5: 3, 7: 4, 9: 5}
    TAIL_AT = {1: 0, 3: 1, 5: 2} if cross else {1: 0, 2: 1, 3: 2}

    with ExitStack() as ctx:
        semaphores = ctx.enter_context(Semaphores(nc))

        def sb(n, shape, dt=F32):
            return ctx.enter_context(nc.sbuf_tensor(f"{name}_{n}", shape, dt))

        def sem(n):
            return semaphores.new(f"{name}_{n}")

        score, score_t, pv, cx, ta, tb = [sh.bank[0], sh.bank[1]], [sh.bank[2], sh.bank[3]], sh.bank[4], sh.bank[5], sh.bank[6], sh.bank[7]
        prob = [sb(f"prob{i}", [P, GH * T]) for i in range(2)]
        nmax, nrest, nparts = sb("nmax", [T, H]), sb("nrest", [T, H]), sb("nparts", [T, P // H, H], BF16)
        nm_t = sb("nm_t", [3 * H, T], BF16)
        pv_sb = sb("pv_sb", [P, NG * T])
        rden = sb("rden", [T, H])
        on = sb("on", [T, C])
        ot = sb("ot", [P, CH, T])
        zero = sh.zero[:, 0:L]
        gated = sb("gated", [T, C])
        bog = sb("bog", [T, C])
        if cross:
            xn = sb("xn", [P, NT, C])
            ct, kf, kr = sh.ctx_t[0:2], sh.ctx_t[2], sh.ctx_t[3]
            kp = sb("kp", [P, 3, CH, L], BF16)
        xn_done, fill_psum, fill_read, split = (sem(n) for n in ("xn_done", "fill_psum", "fill_read", "split"))
        k_written = [sem(f"k_written{c}") for c in range(CH)]
        stacked = [[sem(f"stacked{s}{c}") for c in range(CH)] for s in range(2)]
        v_loaded = [sem(f"v_loaded{s}") for s in range(2)]
        s_psum, max_done, nm_step, nm_psum, nm_done = (sem(n) for n in ("s_psum", "max_done", "nm_step", "nm_psum", "nm_done"))
        nm_written = sem("nm_written")
        nparts_set = sem("nparts_set")
        nm_in = [sem(f"nm_in{s}") for s in range(2)]
        st_psum, exp_done, pv_psum, pv_read = (sem(n) for n in ("st_psum", "exp_done", "pv_psum", "pv_read"))
        tail1, rden_done, on_done, tail2, ot_done, tail3, fin, base_done, bog_done, gated_done = (
            sem(n) for n in ("tail1", "rden_done", "on_done", "tail2", "ot_done", "tail3", "fin", "base_done", "bog_done", "gated_done"))

        def fill_no(slot, k):
            if isinstance(slot, int):
                if slot == -2:
                    return k
                if slot == 6:
                    return 6 * 6 + 10 + k - 4
            return 6 * slot + 10 + k

        def has_fill(slot, k):
            if not cross:
                return False
            b = slot + 2 if k < 4 else slot + 1
            return not isinstance(slot, int) or 0 <= b < B

        def times(b):
            return b // 2 + 1 if isinstance(b, int) else b[1]


        def pe_fill(pe, slot, k, par):
            n = fill_no(slot, k)
            wait(pe, fill_read, n)
            c_t = ct[par] if k < 4 else ct[1 - par]
            if k < 2:
                if k == 0:
                    wait(pe, xn_done, NT * (slot + 3))
                for t, rows in enumerate(keys):
                    ins_ = pe.transpose(cx[:, t * P:t * P + rows], xn[0:rows, t, k * P:(k + 1) * P], sh.ident[0:rows, 0:rows])
            elif k < 4:
                m = k - 2
                for c in range(CH):
                    ins_ = pe.matmul(cx[:, 0:L], wkv[:, c, m * P:(m + 1) * P], c_t[:, c, :], start=c == 0, stop=c == CH - 1)
            else:
                for t in ((0, 1) if k == 4 else (2,)):
                    rows = keys[t]
                    for c in range(CH):
                        ins_ = pe.matmul(cx[0:rows, (t % 2) * C:(t % 2 + 1) * C], c_t[:, c, t * P:t * P + rows], wkv[:, c, C:2 * C],
                                         start=c == 0, stop=c == CH - 1)
            ins_.then_inc(fill_psum, 1)

        def pe_scores(pe, b, par, lo, hi, cnt):
            for i in range(lo, hi):
                if i == 0:
                    pe.wait_ge(stacked[par][0], cnt * (16 * (NTERM + 1) if cross else 32))
                if i * HS == HC:
                    pe.wait_ge(stacked[par][1], cnt * (16 * (NTERM + 1) if cross else 32))
                wait(pe, max_done, NS * b + i - 1)
                for h in range(i * HS, (i + 1) * HS):
                    o = (h - i * HS) * T
                    w = L if cross else T
                    ins_ = pe.matmul(score[i % 2][0:T, o:o + w], sh.q_st[par][0:DEEP, h, :], sh.k_st[par][0:DEEP, h, 0:w],
                                     start=True, stop=True)
                ins_.then_inc(s_psum, 1)

        def pe_max_t(pe, b):
            pe.wait_ge(nm_step, 4 * b + 4)
            wait(pe, ot_done, b - 1)
            pe.transpose(tb[:, CH * T:CH * T + T // 2].bitcast(BF16), nparts[:, :, :].rearrange("t a h -> t (a h)"),
                         sh.ident_bf[0:T, 0:T]).then_inc(nm_psum, 1)

        def pe_scores_t(pe, b, par, u, cnt):
            g, t = u // nt, u % nt
            if u == 0:
                pe.wait_ge(nm_in[par], 16 * cnt)
            wait(pe, exp_done, NU * b + u - 1)
            for j in range(GH):
                h = g * GH + j
                ins_ = pe.matmul(score_t[u % 2][:, j * T:(j + 1) * T], sh.k_st[par][0:AUG, h, t * P:(t + 1) * P],
                                 sh.q_st[par][0:AUG, h, :], start=True, stop=True)
            ins_.then_inc(st_psum, 1)

        def pe_values(pe, b, slot, par, u, cnt):
            g, t = u // nt, u % nt
            if u == 0:
                wait(pe, pv_read, b)
                if cross:
                    wait(pe, fill_read, fill_no(slot - 1, 5) + 1)
                else:
                    pe.wait_ge(v_loaded[par], 16 * cnt)
            pe.wait_ge(exp_done, NU * b + u + 1)
            rows = keys[t]
            for j in range(GH):
                h = g * GH + j
                ins_ = pe.matmul(pv[32 * j:32 * j + D + 1, g * T:(g + 1) * T], sh.v_sb[par][0:rows, t, h, :],
                                 prob[u % 2][0:rows, j * T:(j + 1) * T], start=t == 0, stop=t == nt - 1)
            ins_.then_inc(pv_psum, 1)

        def pe_tail(pe, b, step, last):
            if step == 0:
                pe.wait_ge(pv_read, b + 1)
                wait(pe, fin, b)
                for g in range(NG):
                    ins_ = pe.transpose(ta[0:T, g * P:(g + 1) * P], pv_sb[:, g * T:(g + 1) * T], sh.ident[:, :])
                ins_.then_inc(tail1, 1)
            elif step == 1:
                pe.wait_ge(on_done, b + 1)
                pe.wait_ge(nm_done, B if last else b + 2)
                for c in range(CH):
                    ins_ = pe.transpose(tb[:, c * T:(c + 1) * T], on[:, c * P:(c + 1) * P], sh.ident[0:T, 0:T])
                ins_.then_inc(tail2, 1)
            else:
                pe.wait_ge(ot_done, b + 1)
                for c in range(CH):
                    ins_ = pe.matmul(ta[0:T, 0:C], ot[:, c, :], wo[:, c, :], start=c == 0, stop=c == CH - 1)
                ins_.then_inc(tail3, 1)

        def pe_slot(pe, b, par, cnt, has_e, has_s, has_tail, tail_last=False):
            for u in range(NU + 1):
                if has_e and u < NU:
                    pe_scores_t(pe, b, par, u, cnt[0])
                if has_tail and u in TAIL_AT:
                    pe_tail(pe, b - 1, TAIL_AT[u], tail_last)
                if u in FILL_AT and has_fill(b, FILL_AT[u]):
                    pe_fill(pe, b, FILL_AT[u], par)
                if has_s:
                    pe_scores(pe, b + 1, 1 - par, S_AT[u], S_AT[u + 1], cnt[1])
                if has_e and u > 0:
                    pe_values(pe, b, b, par, u - 1, cnt[0])
            if has_s:
                pe_max_t(pe, b + 1)

        def act_slot(act, b, par, has_e, has_tail):
            for u in range(NU + 1):
                if has_e and u < NU:
                    rows = keys[u % nt]
                    act.wait_ge(st_psum, NU * b + u + 1)
                    wait(act, pv_psum, NU * b + u - 1)
                    act.activation(prob[u % 2][0:rows, :], score_t[u % 2][0:rows, 0:GH * T], ACT.Exp).then_inc(exp_done, 1)
                if has_tail and TAIL_AT.get(u) == 1:
                    act.wait_ge(tail2, b)
                    wait(act, tail3, b - 1)
                    act.activation(ot[:, :, :], tb[:, 0:CH * T].rearrange("p (c n) -> p c n", c=CH), ACT.Copy).then_inc(ot_done, 1)
                if u in FILL_AT and FILL_AT[u] < 4 and has_fill(b, FILL_AT[u]):
                    k = FILL_AT[u]
                    act.wait_ge(fill_psum, fill_no(b, k) + 1)
                    if k < 2:
                        if ln:
                            act.activation(ct[par][:, k, :], cx[:, 0:L], ACT.Identity, bias=sh.mod[:, 3, k, bass.ds(b + 2, 1)],
                                           scale=sh.mod[:, 2, k, bass.ds(b + 2, 1)]).then_inc(fill_read, 1)
                        else:
                            act.activation(ct[par][:, k, :], cx[:, 0:L], ACT.Copy).then_inc(fill_read, 1)
                    else:
                        m = k - 2
                        wait(act, split, 8 * (b + 1) + 4 * m + 4)
                        act.activation(kf[:, m, :], cx[:, 0:L], ACT.Identity, bias=bk[:, m:m + 1]).then_inc(fill_read, 1)
            if has_e:
                act.wait_ge(pv_psum, NU * b + NU)
                wait(act, tail1, b)
                act.activation(pv_sb[:, :], pv[:, 0:NG * T], ACT.Copy).then_inc(pv_read, 1)

        def dve_norm_context(dve, b):
            wait(dve, fill_psum, fill_no(b - 3, 1) + 1) if not (isinstance(b, int) and b == 0) else None
            for t in range(NT):
                x_in = sh.ctx[:, bass.ds(b, 1), t, :]
                if ln:
                    dve.tensor_scalar(xn[:, t, :], x_in, sh.ctx_mean[:, bass.ds(b, 1), t], sh.ctx_rstd[:, bass.ds(b, 1), t],
                                      ALU.subtract, ALU.mult).then_inc(xn_done, 1)
                else:
                    dve.tensor_copy(xn[:, t, :], x_in).then_inc(xn_done, 1)

        def dve_slot(dve, b, par, has_e, has_s, has_tail, norm_next):
            for u in range(NU + 1):
                if has_tail and TAIL_AT.get(u) == 0:
                    dve.wait_ge(tail1, b)
                    tp = ta[0:T, :].rearrange("t (h e) -> t h e", e=32)
                    dve.reciprocal(rden[:, :], tp[:, :, D]).then_inc(rden_done, 1)
                    dve.wait_ge(rden_done, b)
                    wait(dve, tail2, b - 1)
                    dve.tensor_tensor(on[:, :].rearrange("t (h d) -> t h d", d=D), tp[:, :, 0:D],
                                      rden[:, :].rearrange("t (h o) -> t h o", o=1).broadcast_to([T, H, D]), ALU.mult).then_inc(on_done, 1)
                if has_tail and TAIL_AT.get(u) == 2:
                    xb = sh.x[:, bass.ds(b - 1, 1), :].rearrange("t o c -> t (o c)")
                    dve.wait_ge(tail3, b)
                    dve.wait_ge(base_done, b)
                    if gate is None:
                        dve.tensor_tensor(xb, ta[0:T, 0:C], xb, ALU.add).then_inc(fin, 1)
                    else:
                        dve.tensor_tensor(gated[:, :], ta[0:T, 0:C], sh.gate[:, gate, bass.ds(b - 1, 1), :].rearrange("t o c -> t (o c)"),
                                          ALU.mult).then_inc(gated_done, 1)
                        dve.wait_ge(gated_done, b)
                        dve.tensor_tensor(xb, gated[:, :], xb, ALU.add).then_inc(fin, 1)
                if u in FILL_AT and FILL_AT[u] >= 4 and has_fill(b, FILL_AT[u]):
                    k = FILL_AT[u]
                    dve.wait_ge(fill_psum, fill_no(b, k) + 1)
                    wait(dve, pv_psum, NU * b)
                    for t in ((0, 1) if k == 4 else (2,)):
                        rows = keys[t]
                        ins_ = dve.tensor_tensor(sh.v_sb[1 - par][0:rows, t, :, 0:D],
                                                 cx[0:rows, (t % 2) * C:(t % 2 + 1) * C].rearrange("p (h d) -> p h d", d=D),
                                                 sh.brow[0:rows, bv_row, :].rearrange("p (h d) -> p h d", d=D), ALU.add)
                    ins_.then_inc(fill_read, 1)
                if norm_next and u == 6:
                    dve_norm_context(dve, b + 3)
                if has_s:
                    for i in range(S_AT[u], S_AT[u + 1]):
                        dve.wait_ge(s_psum, NS * (b + 1) + i + 1)
                        if i == 0:
                            wait(dve, nm_step, 4 * (b + 1))
                        w = L if cross else T
                        dve.tensor_reduce(nmax[:, i * HS:(i + 1) * HS], score[i % 2][0:T, 0:HS * w].rearrange("t (h k) -> t h k", k=w),
                                          AX_X, ALU.max, negate=True).then_inc(max_done, 1)
            if has_s:
                n = 4 * (b + 1)
                dve.wait_ge(max_done, NS * (b + 2))
                wait(dve, nm_psum, b + 1)
                dve.tensor_copy(nparts[:, 0, :], nmax[:, :]).then_inc(nm_step, 1)
                dve.wait_ge(nm_step, n + 1)
                dve.tensor_tensor(nrest[:, :], nmax[:, :], nparts[:, 0, :], ALU.subtract).then_inc(nm_step, 1)
                dve.wait_ge(nm_step, n + 2)
                dve.tensor_copy(nparts[:, 1, :], nrest[:, :]).then_inc(nm_step, 1)
                dve.wait_ge(nm_step, n + 3)
                dve.tensor_tensor(nparts[:, 2, :], nrest[:, :], nparts[:, 1, :], ALU.subtract).then_inc(nm_step, 1)
                dve.wait_ge(nm_psum, b + 2)
                wait(dve, nm_written, 16 * (b + 1))
                dve.tensor_copy(nm_t[:, :], tb[0:3 * H, CH * T:CH * T + T // 2].bitcast(BF16)).then_inc(nm_done, 1)

        def pool_slot(pool, b, has_e):
            if has_e:
                xb = sh.x[:, bass.ds(b, 1), :].rearrange("t o c -> t (o c)")
                if gate is None:
                    pool.tensor_tensor(xb, xb, sh.brow[0:T, bo_row, :], ALU.add).then_inc(base_done, 1)
                else:
                    wait(pool, base_done, b)
                    pool.tensor_tensor(bog[:, :], sh.gate[:, gate, bass.ds(b, 1), :].rearrange("t o c -> t (o c)"),
                                       sh.brow[0:T, bo_row, :], ALU.mult).then_inc(bog_done, 1)
                    pool.wait_ge(bog_done, b + 1)
                    pool.tensor_tensor(xb, xb, bog[:, :], ALU.add).then_inc(base_done, 1)
            if has_fill(b, 2):
                for m in range(CH):
                    n = 8 * (b + 2) + 4 * m
                    pool.wait_ge(fill_read, fill_no(b, 2 + m) + 1)
                    wait(pool, k_written[m], 16 * (b + 2))
                    pool.tensor_tensor(kp[:, 0, m, :], kf[:, m, :], zero, ALU.add).then_inc(split, 1)
                    pool.wait_ge(split, n + 1)
                    pool.tensor_tensor(kr[:, m, :], kf[:, m, :], kp[:, 0, m, :], ALU.subtract).then_inc(split, 1)
                    pool.wait_ge(split, n + 2)
                    pool.tensor_tensor(kp[:, 1, m, :], kr[:, m, :], zero, ALU.add).then_inc(split, 1)
                    pool.wait_ge(split, n + 3)
                    pool.tensor_tensor(kp[:, 2, m, :], kr[:, m, :], kp[:, 1, m, :], ALU.subtract).then_inc(split, 1)

        def sp_write_keys(sp, b, par, m):
            sp.wait_ge(split, 8 * b + 4 * m + 4)
            sp.dma_start(sh.dram["ctx_k"][par, :, m, :, :].rearrange("t p n -> p t n"), kp[:, :, m, :]).then_inc(k_written[m], 16)

        def sp_load_half(sp, b, par, c):
            wait(sp, st_psum, NU * (b - 2) + (NU // 2) * (c + 1))
            if cross:
                sp.wait_ge(k_written[c], 16 * (b + 1))
                for s, w in enumerate(TERMS_K):
                    sp.dma_start(sh.k_st[par][s * D:(s + 1) * D, c * HC:(c + 1) * HC, 0:L],
                                 sh.dram["ctx_k"][par, w, c, :, :].rearrange("(h d) n -> d h n", d=D)).then_inc(stacked[par][c], 16)
            else:
                sp.dma_start(sh.k_st[par][0:DEEP, c * HC:(c + 1) * HC, 0:T],
                             sh.k_all[:, bass.ds(b, 1), c * HC:(c + 1) * HC, :]).then_inc(stacked[par][c], 16)
            sp.dma_start(sh.q_st[par][0:DEEP, c * HC:(c + 1) * HC, :],
                         sh.q_all[:, bass.ds(b, 1), c * HC:(c + 1) * HC, :]).then_inc(stacked[par][c], 16)

        def sp_load_max(sp, b, par):
            sp.wait_ge(nm_done, b + 1)
            sp.dma_start(sh.dram["nmax"][par], nm_t[:, :]).then_inc(nm_written, 16)
            sp.wait_ge(nm_written, 16 * (b + 1))
            sp.dma_start(sh.q_st[par][DEEP:AUG, :, :], sh.dram["nmax"][par].rearrange("(a h) n -> a h n", a=3)).then_inc(nm_in[par], 16)

        def sp_slot(sp, b, par, has_s, has_load):
            if has_load and cross:
                sp_write_keys(sp, b + 2, par, 0)
                sp_load_half(sp, b + 2, par, 0)
                sp_write_keys(sp, b + 2, par, 1)
            elif has_load:
                sp_load_half(sp, b + 2, par, 0)
            if has_s:
                sp_load_max(sp, b + 1, 1 - par)
            if has_load:
                sp_load_half(sp, b + 2, par, 1)
                if not cross:
                    wait(sp, pv_psum, NU * (b + 1))
                    sp.dma_start(sh.v_sb[par][0:T, 0, :, :], sh.v_all[:, bass.ds(b + 2, 1), :, :]).then_inc(v_loaded[par], 16)

        def pipeline(eng, slot):
            for b in (-2, -1, 0):
                slot(b, b % 2, (b // 2 + 1, (b + 1) // 2 + 1))
            with eng.Fori(0, 2) as i:
                slot(2 * i + 1, 1, (i + 1, i + 2))
                slot(2 * i + 2, 0, (i + 2, i + 2))
            for b in (5, 6, 7, 8):
                slot(b, b % 2, (b // 2 + 1, (b + 1) // 2 + 1))

        def within(b, ahead):
            return not isinstance(b, int) or 0 <= b + ahead < B

        with nc.Block() as block:
            @block.tensor
            def _(pe):
                pe.wait_ge(nparts_set, 1)
                pipeline(pe, lambda b, par, cnt: pe_slot(pe, b, par, cnt, within(b, 0), within(b, 1), within(b, -1),
                                                         isinstance(b, int) and b + 1 >= B))

            @block.scalar
            def _(act):
                pipeline(act, lambda b, par, cnt: act_slot(act, b, par, within(b, 0), within(b, -1)))

            @block.vector
            def _(dve):
                dve.memset(nparts[:, 3:, :], 0.0).then_inc(nparts_set, 1)
                if cross:
                    dve_norm_context(dve, 0)
                pipeline(dve, lambda b, par, cnt: dve_slot(dve, b, par, within(b, 0), within(b, 1), within(b, -1),
                                                           cross and within(b, 3)))

            @block.gpsimd
            def _(pool):
                pipeline(pool, lambda b, par, cnt: pool_slot(pool, b, within(b, 0)))

            @block.sync
            def _(sp):
                pipeline(sp, lambda b, par, cnt: sp_slot(sp, b, par, within(b, 1), within(b, 2)))


def phase_mlp(nc, sh, ins, out):
    N2 = 2 * T
    NH = HID // P
    with ExitStack() as ctx:
        semaphores = ctx.enter_context(Semaphores(nc))

        def sb(n, shape, dt=F32):
            return ctx.enter_context(nc.sbuf_tensor(f"mlp_{n}", shape, dt))

        def sem(n):
            return semaphores.new(f"mlp_{n}")

        w1, w2 = sh.w1, sh.w2
        stats, mv, veps, half, rstd, pause = sb("stats", [T, 2, 6]), sb("mv", [T, 2, 2]), sb("veps", [T, 2]), sb("half", [T, 2]), sb("rstd", [T, 2]), sb("pause", [T, 1])
        xn = sb("xn", [T, 2, C])
        xt = sb("xt", [P, CH, N2])
        hid = sb("hid", [P, NH, N2])
        y, yg, yo = sb("y", [T, 2, C]), sb("yg", [T, 2, C]), sb("yo", [T, 2, C])
        w_in, half_set, stats_done, aggr_done, veps_done, rstd_done, xn_done = (
            sem(n) for n in ("w_in", "half_set", "stats_done", "aggr_done", "veps_done", "rstd_done", "xn_done"))
        xt_psum, xt_done, h_psum, hid_done, y_psum, y_step, stored = (
            sem(n) for n in ("xt_psum", "xt_done", "h_psum", "hid_done", "y_psum", "y_step", "stored"))
        y_bank = sh.bank[7]

        with nc.Block() as block:
            @block.sync
            def _(sp):
                sp.dma_start(w1[:, :, :], ins["L1_xcond_mlp_w1"].rearrange("(k p) n -> p k n", p=P)).then_inc(w_in, 16)
                sp.dma_start(w2[:, :, :], ins["L1_xcond_mlp_w2"].rearrange("(k p) n -> p k n", p=P)).then_inc(w_in, 16)
                with sp.Fori(0, PAIRS) as p:
                    sp.wait_ge(y_step, 3 * p + 3)
                    sp.dma_start(out[bass.ds(2 * p, 2)].rearrange("j n c -> n j c"), yo[:, :, :]).then_inc(stored, 16)
                sp.wait_ge(stored, 16 * PAIRS)

            @block.gpsimd
            def _(pool):
                pool.memset(half[:, :], -0.5).then_inc(half_set, 1)
                pool.wait_ge(half_set, 1)
                with pool.Fori(0, PAIRS) as p:
                    pool.wait_ge(veps_done, p + 1)
                    pool.tensor_tensor(rstd[:, :], veps[:, :], half[:, :], ALU.pow).then_inc(rstd_done, 1)

            @block.vector
            def _(dve):
                with dve.Fori(0, PAIRS) as p:
                    for j in range(2):
                        dve.bn_stats(stats[:, j, :], sh.x[:, bass.ds(2 * p + j, 1), :]).then_inc(stats_done, 1)
                    dve.wait_ge(stats_done, 2 * p + 2)
                    dve.memset(pause[:, :], 0.0)
                    for j in range(2):
                        dve.bn_aggr(mv[:, j, :], stats[:, j, :]).then_inc(aggr_done, 1)
                    dve.wait_ge(aggr_done, 2 * p + 2)
                    dve.tensor_scalar(veps[:, :], mv[:, :, 1], 1e-6, None, ALU.add).then_inc(veps_done, 1)
                    dve.wait_ge(rstd_done, p + 1)
                    dve.wait_ge(xt_psum, p + 0)
                    for j in range(2):
                        dve.tensor_scalar(xn[:, j, :], sh.x[:, bass.ds(2 * p + j, 1), :], mv[:, j, 0:1], rstd[:, j:j + 1],
                                          ALU.subtract, ALU.mult).then_inc(xn_done, 1)
                    dve.wait_ge(y_psum, p + 1)
                    dve.tensor_tensor(y[:, :, :], y_bank[0:T, :].rearrange("t (j c) -> t j c", j=2),
                                      sh.brow[0:T, 6:7, :].broadcast_to([T, 2, C]), ALU.add).then_inc(y_step, 1)
                    dve.wait_ge(y_step, 3 * p + 1)
                    dve.tensor_tensor(yg[:, :, :], y[:, :, :], sh.gate[:, 1, bass.ds(2 * p, 2), :], ALU.mult).then_inc(y_step, 1)
                    dve.wait_ge(y_step, 3 * p + 2)
                    dve.wait_ge(stored, 16 * p)
                    dve.tensor_tensor(yo[:, :, :], yg[:, :, :], sh.x[:, bass.ds(2 * p, 2), :], ALU.add).then_inc(y_step, 1)

            @block.scalar
            def _(act):
                with act.Fori(0, PAIRS) as p:
                    act.wait_ge(xt_psum, p + 1)
                    for c in range(CH):
                        for j in range(2):
                            o = (c * 2 + j) * T
                            act.activation(xt[:, c, j * T:(j + 1) * T], sh.bank[0][:, o:o + T], ACT.Identity,
                                           bias=sh.mod[:, 6, c, bass.ds(2 * p + j, 1)],
                                           scale=sh.mod[:, 7, c, bass.ds(2 * p + j, 1)]).then_inc(xt_done, 1)
                    for m in range(NH):
                        act.wait_ge(h_psum, NH * p + m + 1)
                        if m == 0:
                            act.wait_ge(y_psum, p + 0)
                        act.activation(hid[:, m, :], sh.bank[1 + m % 4][:, 0:N2], ACT.Gelu_apprx_tanh,
                                       bias=sh.bhid[:, m:m + 1]).then_inc(hid_done, 1)

            @block.tensor
            def _(pe):
                with pe.Fori(0, PAIRS) as p:
                    pe.wait_ge(xn_done, 2 * p + 2)
                    for c in range(CH):
                        for j in range(2):
                            o = (c * 2 + j) * T
                            ins_ = pe.transpose(sh.bank[0][:, o:o + T], xn[:, j, c * P:(c + 1) * P], sh.ident[0:T, 0:T])
                    ins_.then_inc(xt_psum, 1)
                    pe.wait_ge(xt_done, 4 * p + 4)
                    pe.wait_ge(w_in, 32)
                    for m in range(NH):
                        if m >= 4:
                            pe.wait_ge(hid_done, NH * p + m - 3)
                        for c in range(CH):
                            ins_ = pe.matmul(sh.bank[1 + m % 4][:, 0:N2], w1[:, c, m * P:(m + 1) * P], xt[:, c, :],
                                             start=c == 0, stop=c == CH - 1)
                        ins_.then_inc(h_psum, 1)
                    pe.wait_ge(hid_done, NH * p + NH)
                    pe.wait_ge(y_step, 3 * p)
                    for j in range(2):
                        for m in range(NH):
                            ins_ = pe.matmul(y_bank[0:T, j * C:(j + 1) * C], hid[:, m, j * T:(j + 1) * T], w2[:, m, :],
                                             start=m == 0, stop=m == NH - 1)
                    ins_.then_inc(y_psum, 1)


def build(nc, ins, out):
    dram = {
        "gate": nc.dram_tensor("gate_rows", (B, 2, C), F32, kind="Internal").ap(),
        "q_parts": nc.dram_tensor("q_parts", (PAIRS, 3, CH, P, 2 * T), BF16, kind="Internal").ap(),
        "k_parts": nc.dram_tensor("k_parts", (PAIRS, 3, CH, P, 2 * T), BF16, kind="Internal").ap(),
        "ctx_k": nc.dram_tensor("ctx_k_parts", (2, 3, CH, P, L), BF16, kind="Internal").ap(),
        "nmax": nc.dram_tensor("nmax_parts", (2, 3 * H, T), BF16, kind="Internal").ap(),
    }
    with ExitStack() as ctx:
        sh = allocate(nc, ctx, dram)
        phase_load(nc, sh, ins)

        def mod(m):
            return lambda c, b: sh.mod[:, m, c, bass.ds(b, 1)]

        phase_project(nc, sh, "p0", 1e-5, mod(0), mod(1), sh.wq0, sh.bcol[:, 0, :], False)
        phase_attend(nc, sh, "a0", True, True, sh.wkv0, sh.bcol[:, 1, :], 0, sh.wo0, 1, None)
        phase_project(nc, sh, "p1", 1e-6, mod(5), mod(4), sh.wqkv1, sh.bcol[:, 2, :], True)
        phase_attend(nc, sh, "a1", False, False, None, None, 2, sh.wo1, 3, 0)
        phase_project(nc, sh, "p2", 1e-6, lambda c, b: sh.bcol[:, 4, c:c + 1], lambda c, b: sh.bcol[:, 5, c:c + 1],
                      sh.wq2, sh.bcol[:, 6, :], False)
        phase_attend(nc, sh, "a2", True, False, sh.wkv2, sh.bcol[:, 7, :], 4, sh.wo2, 5, None)
        phase_mlp(nc, sh, ins, out)


_OUT = ((B, T, C), "float32")


def kernel(**inputs):
    import numpy as _np
    import concourse.bacc as _bacc
    from concourse import mybir as _mybir
    from concourse.bass_utils import run_bass_kernel_spmd as _run

    nc = _bacc.Bacc("TRN2", target_bir_lowering=False, num_devices=1)
    arrays, ins = {}, {}
    for name, value in inputs.items():
        a = _np.ascontiguousarray(value)
        arrays[f"in_{name}_dram"] = a
        ins[name] = nc.dram_tensor(f"in_{name}_dram", a.shape, _mybir.dt.from_np(a.dtype), kind="ExternalInput").ap()
    out = nc.dram_tensor("out_0_dram", _OUT[0], _mybir.dt.from_np(_np.dtype(_OUT[1])), kind="ExternalOutput").ap()
    build(nc, ins, out)
    r = _run(nc, [arrays], core_ids=[0])
    return r.results[0]["out_0_dram"]
```

```python
from contextlib import ExitStack

import numpy as np

import concourse.bass as bass
from concourse import mybir

F32 = mybir.dt.float32
BF16 = mybir.dt.bfloat16
ALU = mybir.AluOpType
ACT = mybir.ActivationFunctionType
AX_X = mybir.AxisListType.X

P = 128
B, T, L, C = 8, 112, 375, 256
H, D = 16, 16
CH = C // P
HC = P // D
HID = 4 * C
KEYS = [min(P, L - k) for k in range(0, L, P)]
NT = len(KEYS)
PAIRS = B // 2
SCALE = float(D) ** -0.5

TERMS_K = [0, 1, 0, 1, 2, 0]
TERMS_Q = [0, 0, 1, 1, 0, 2]
NTERM = len(TERMS_K)
WIDE = B * T + P - T
QUAD = 4
DEEP = NTERM * D
AUG = DEEP + 3

MODS = [("q_scale", 1.0), ("q_bias", 0.0), ("kv_scale", 1.0), ("kv_bias", 0.0),
        ("shift_msa", 0.0), ("scale_msa", 1.0), ("shift_mlp", 0.0), ("scale_mlp", 1.0)]


def wait(eng, sem, count):
    if isinstance(count, int) and count <= 0:
        return
    eng.wait_ge(sem, count)


def wait_all(eng, pairs):
    for sem, count in pairs:
        eng.wait_ge(sem, count)


class Parts:

    def __init__(self, tensor, vector, scalar, gpsimd, sync, **more):
        self.tensor, self.vector, self.scalar, self.gpsimd, self.sync = tensor, vector, scalar, gpsimd, sync
        self.more = more


class Room:

    def __init__(self, space):
        self.space, self.at = space, 0

    def take(self, shape, dt=F32):
        words = int(np.prod(shape[1:])) * (2 if dt == BF16 else 4) // 4
        view = self.space[0:shape[0], self.at:self.at + words]
        self.at += words
        if dt == BF16:
            view = view.bitcast(BF16)
        names = "abcd"[:len(shape) - 1]
        if len(names) == 1:
            return view
        return view.rearrange(f"p ({' '.join(names)}) -> p {' '.join(names)}", **dict(zip(names[1:], shape[2:])))


class Semaphores:

    def __init__(self, nc):
        self.nc, self.all = nc, []

    def new(self, name):
        self.all.append(self.nc.alloc_semaphore(name))
        return self.all[-1]

    def __enter__(self):
        return self

    def __exit__(self, *_):
        self.nc.clear_and_free_semaphores(self.all)
        self.nc.all_engine_barrier()


class Shared:
    pass


def allocate(nc, ctx, dram):
    sh = Shared()

    def sb(name, shape, dt=F32):
        return ctx.enter_context(nc.sbuf_tensor(name, shape, dt))

    sh.dram = dram
    sh.bank = [ctx.enter_context(nc.psum_tensor(f"bank{i}", [P, 512], F32)) for i in range(8)]
    sh.ident = sb("ident", [P, P])
    sh.ident_bf = sb("ident_bf", [P, P], BF16)
    sh.x = sb("x_tokens", [T, B, C])
    sh.ctx = sb("ctx_tokens", [P, B, NT, C])
    sh.ctx_mean = sb("ctx_mean", [P, B, NT])
    sh.ctx_rstd = sb("ctx_rstd", [P, B, NT])
    sh.silu_t = sb("silu_t", [P, CH, B])
    sh.mod = sb("mod", [P, len(MODS), CH, B])
    gates = [sb(f"gate{g}", [P, B * C]) for g in range(2)]
    sh.gate_space = gates
    sh.gate = [g[0:T, :].rearrange("t (b c) -> t b c", c=C) for g in gates]
    sh.wq0 = sb("wq0", [P, CH, C])
    sh.wkv0 = sb("wkv0", [P, CH, 2 * C])
    sh.wo0 = sb("wo0", [P, CH, C])
    sh.wqkv1 = sb("wqkv1", [P, CH, 3 * C])
    sh.wo1 = sb("wo1", [P, CH, C])
    sh.wq2 = sb("wq2", [P, CH, C])
    sh.wkv2 = sb("wkv2", [P, CH, 2 * C])
    sh.wo2 = sb("wo2", [P, CH, C])
    sh.bcol = sb("bias_columns", [P, 9, CH])
    sh.bhid = sb("bias_hidden", [P, HID // P])
    sh.brow = sb("bias_rows", [P, 7, C])
    sh.q_all = sb("q_stack_all", [AUG, H, WIDE], BF16)
    k_space = sb("k_stack_all", [P, H, WIDE], BF16)
    sh.k_all = k_space[0:AUG]
    mod_w = k_space[:, :, :].rearrange("p h n -> p (h n)").bitcast(F32)
    sh.wss = mod_w[:, 0:CH * 4 * C].rearrange("p (k n) -> p k n", k=CH)
    sh.ctx_t = [mod_w[:, i * CH * L:(i + 1) * CH * L].rearrange("p (c n) -> p c n", c=CH) for i in range(4)]
    at = 4 * CH * L
    sh.w1 = mod_w[:, at:at + CH * HID].rearrange("p (k n) -> p k n", k=CH)
    sh.w2 = mod_w[:, at + CH * HID:at + 2 * CH * HID].rearrange("p (k n) -> p k n", n=C)
    sh.wada = mod_w[:, at:at + CH * 6 * C].rearrange("p (k n) -> p k n", k=CH)
    sh.v_space = sb("v_all", [P, B * H * (D + 1)])
    sh.v_all = sh.v_space[0:T, :].rearrange("t (b h e) -> t b h e", b=B, h=H)
    sh.k_space = sb("k_stack", [P, 2 * H * NT * P // 2])
    stack = Room(sh.k_space)
    sh.k_st = [stack.take([AUG, H, NT * P], BF16) for i in range(2)]
    sh.v_sb = [sb(f"v_tokens{i}", [P, NT, H, D + 1]) for i in range(2)]
    return sh


BIAS_COLS = ["bq0", "bk0", "bq1", "bk1", "g2", "b2", "bq2", "bk2", "spare"]
BIAS_ROWS = ["bv0", "bp0", "bv1", "bo1", "bv2", "bo2", "bmlp2"]


def load(nc, sh, ctx, sems, ins):
    def sb(name, shape, dt=F32):
        return ctx.enter_context(nc.sbuf_tensor(name, shape, dt))

    cond, e, den, sig, silu = (sb(n, [B, C]) for n in ("cond", "cond_exp", "cond_den", "cond_sig", "cond_silu"))
    stats = sb("ctx_stats", [P, B, NT, 6])
    mv = sb("ctx_mv", [P, B, NT, 2])
    veps = sb("ctx_veps", [P, B, NT])
    half = sb("ctx_half", [P, B, NT])
    bmod = sb("bmod0", [P, 4, CH])

    cond_in, ctx_zero, zeroed, ident_set, half_set = (
        sems.new(n) for n in ("cond_in", "ctx_zero", "zeroed", "ident_set", "half_set"))
    exp_done, silu_step, silu_ready, silu_t_psum, silu_t_ready, mod_psum = (
        sems.new(n) for n in ("exp_done", "silu_step", "silu_ready", "silu_t_psum", "silu_t_ready", "mod_psum"))
    stats_done, aggr_done, veps_done = (sems.new(n) for n in ("stats_done", "aggr_done", "veps_done"))
    sh.mod_in = sems.new("mod_in")
    sh.x_in = sems.new("x_in")
    sh.wq_in = sems.new("wq_in")
    sh.ctx_in = sems.new("ctx_in")
    sh.w_in = sems.new("w_in")
    sh.late_in = sems.new("late_in")
    sh.mod_done = sems.new("mod_done")
    sh.ctx_stats_done = sems.new("ctx_stats_done")
    sh.consts_done = sems.new("consts_done")

    def chunks(w):
        return w.rearrange("(k p) n -> p k n", p=P)

    def col(v):
        return v.rearrange("(k p) -> p k", p=P)

    def sync(sp):
        sp.dma_start(cond[:, :], ins["cond_1024"]).then_inc(cond_in, 16)
        sp.dma_start(sh.wss[:, :, 0:2 * C], chunks(ins["L0_xcond_Wss_q"])).then_inc(sh.mod_in, 16)
        sp.dma_start(sh.x[:, 0:QUAD, :], ins["x"][0:QUAD].rearrange("b n c -> n b c")).then_inc(sh.x_in, 16)
        sp.dma_start(sh.x[:, QUAD:B, :], ins["x"][QUAD:B].rearrange("b n c -> n b c")).then_inc(sh.x_in, 16)
        sp.dma_start(sh.wss[:, :, 2 * C:4 * C], chunks(ins["L0_xcond_Wss_kv"])).then_inc(sh.mod_in, 16)
        with nc.allow_non_contiguous_dma(reason="biases, a few KB in all"):
            for m, v in enumerate([ins["L0_xcond_bss_q"][0:C], ins["L0_xcond_bss_q"][C:2 * C],
                                   ins["L0_xcond_bss_kv"][0:C], ins["L0_xcond_bss_kv"][C:2 * C]]):
                sp.dma_start(bmod[:, m, :], col(v)).then_inc(sh.mod_in, 16)
            sp.dma_start(sh.wq0[:, :, :], chunks(ins["L0_xcond_Wq"])).then_inc(sh.wq_in, 16)
            for n, v in (("bq0", ins["L0_xcond_bq"]), ("bq1", ins["L1_xcond_qkv_b"][0:C]), ("bk1", ins["L1_xcond_qkv_b"][C:2 * C]),
                         ("g2", ins["L1_xcond_norm2_g"]), ("b2", ins["L1_xcond_norm2_b"]), ("bq2", ins["L1_xcond_q_b"])):
                sp.dma_start(sh.bcol[:, BIAS_COLS.index(n), :], col(v)).then_inc(sh.wq_in, 16)
            sp.dma_start(sh.bhid[:, :], col(ins["L1_xcond_mlp_b1"])).then_inc(sh.wq_in, 16)
        sp.wait_ge(ctx_zero, 1)
        for t, rows in enumerate(KEYS):
            sp.dma_start(sh.ctx[0:rows, :, t, :],
                         ins["ctx_1024"][:, t * P:t * P + rows, :].rearrange("b p c -> p b c")).then_inc(sh.ctx_in, 16)
        sp.dma_start(sh.wkv0[:, :, :], chunks(ins["L0_xcond_Wkv"])).then_inc(sh.w_in, 16)
        sp.dma_start(sh.wo0[:, :, :], chunks(ins["L0_xcond_Wp"])).then_inc(sh.w_in, 16)
        for i, v in enumerate([ins["L0_xcond_bkv"][C:2 * C], ins["L0_xcond_bp"], ins["L1_xcond_qkv_b"][2 * C:3 * C],
                               ins["L1_xcond_self_o_b"], ins["L1_xcond_kv_b"][C:2 * C], ins["L1_xcond_cross_o_b"],
                               ins["L1_xcond_mlp_b2"]]):
            sp.dma_start(sh.brow[:, i, :], v.partition_broadcast(P)).then_inc(sh.w_in, 16)
        with nc.allow_non_contiguous_dma(reason="biases, a few KB in all"):
            for n, v in (("bk0", ins["L0_xcond_bkv"]), ("bk2", ins["L1_xcond_kv_b"])):
                for k in range(CH):
                    sp.dma_start(sh.bcol[:, BIAS_COLS.index(n), k:k + 1],
                                 v[k * P:(k + 1) * P].rearrange("(h d) -> d h", d=D)).then_inc(sh.w_in, 16)
        for w, name in ((sh.wada, "L1_xcond_ada_w"), (sh.wqkv1, "L1_xcond_qkv_w"), (sh.wo1, "L1_xcond_self_o_w"),
                        (sh.wq2, "L1_xcond_q_w"), (sh.wkv2, "L1_xcond_kv_w"), (sh.wo2, "L1_xcond_cross_o_w")):
            sp.dma_start(w[:, :, :], chunks(ins[name])).then_inc(sh.late_in, 16)

    def gpsimd(pool):
        pool.memset(sh.ident[:, :], 0.0).then_inc(zeroed, 1)
        pool.memset(sh.ident_bf[:, :], 0.0).then_inc(zeroed, 1)
        pool.wait_ge(zeroed, 2)
        for m in (sh.ident, sh.ident_bf):
            pool.affine_select(out=m[:, :], in_=m[:, :], compare_op=ALU.not_equal, fill=1.0,
                               base=0, pattern=[[-1, P]], channel_multiplier=1).then_inc(ident_set, 1)
        pool.memset(half[:, :, :], -0.5).then_inc(half_set, 1)

    def gpsimd_late(pool):
        for s in range(2):
            pool.memset(sh.v_sb[s][:, :, :, D:D + 1], 1.0).then_inc(sh.consts_done, 1)
        pool.memset(sh.q_all[:, :, B * T:], 0.0).then_inc(sh.consts_done, 1)
        pool.wait_ge(half_set, 1)
        pool.wait_ge(veps_done, 1)
        pool.tensor_tensor(sh.ctx_rstd[:, :, :], veps[:, :, :], half[:, :, :], ALU.pow).then_inc(sh.ctx_stats_done, 1)

    def scalar(act):
        act.wait_ge(cond_in, 16)
        act.activation(e[:, :], cond[:, :], ACT.Exp, scale=-1.0).then_inc(exp_done, 1)

    def vector(dve):
        dve.memset(sh.ctx[96:P, :, NT - 1, :], 0.0).then_inc(ctx_zero, 1)
        dve.wait_ge(exp_done, 1)
        dve.tensor_scalar(den[:, :], e[:, :], 1.0, None, ALU.add).then_inc(silu_step, 1)
        dve.wait_ge(silu_step, 1)
        dve.reciprocal(sig[:, :], den[:, :]).then_inc(silu_step, 1)
        dve.wait_ge(silu_step, 2)
        dve.tensor_tensor(silu[:, :], cond[:, :], sig[:, :], ALU.mult).then_inc(silu_ready, 1)
        dve.wait_ge(silu_t_psum, 1)
        dve.tensor_copy(sh.silu_t[:, :, :], sh.bank[6][:, 0:CH * B].rearrange("p (k b) -> p k b", b=B)).then_inc(silu_t_ready, 1)

    def vector_mod(dve):
        dve.wait_ge(mod_psum, 1)
        mp = sh.bank[7][:, 0:4 * CH * B].rearrange("p (m k b) -> p m k b", k=CH, b=B)
        for m in range(4):
            for k in range(CH):
                dve.tensor_scalar(sh.mod[:, m, k, :], mp[:, m, k, :], bmod[:, m, k:k + 1], MODS[m][1], ALU.add, ALU.add).then_inc(sh.mod_done, 1)

    def vector_late(dve):
        dve.memset(sh.bank[4][:, :], 0.0).then_inc(sh.consts_done, 1)
        dve.wait_ge(sh.ctx_in, 16 * NT)
        for b in range(B):
            for t in range(NT):
                dve.bn_stats(stats[:, b, t, :], sh.ctx[:, b, t, :]).then_inc(stats_done, 1)
        dve.wait_ge(stats_done, B * NT)
        for b in range(B):
            for t in range(NT):
                dve.bn_aggr(mv[:, b, t, :], stats[:, b, t, :]).then_inc(aggr_done, 1)
        dve.wait_ge(aggr_done, B * NT)
        dve.tensor_scalar(veps[:, :, :], mv[:, :, :, 1], 1e-5, None, ALU.add).then_inc(veps_done, 1)
        dve.tensor_copy(sh.ctx_mean[:, :, :], mv[:, :, :, 0]).then_inc(sh.ctx_stats_done, 1)

    def tensor(pe):
        pe.wait_ge(silu_ready, 1)
        pe.wait_ge(ident_set, 2)
        for k in range(CH):
            last = pe.transpose(sh.bank[6][:, k * B:(k + 1) * B], silu[:, k * P:(k + 1) * P], sh.ident[0:B, 0:B])
        last.then_inc(silu_t_psum, 1)
        pe.wait_ge(silu_t_ready, 1)
        pe.wait_ge(sh.mod_in, 16 * 6)
        for m in range(4):
            for k in range(CH):
                o = (m * CH + k) * B
                for kk in range(CH):
                    last = pe.matmul(sh.bank[7][:, o:o + B], sh.wss[:, kk, m * C + k * P:m * C + (k + 1) * P],
                                     sh.silu_t[:, kk, :], start=kk == 0, stop=kk == CH - 1)
        last.then_inc(mod_psum, 1)

    return Parts(tensor, vector, scalar, gpsimd, sync, gpsimd_late=gpsimd_late, vector_mod=vector_mod, vector_late=vector_late)


def modulate_second(nc, sh, ctx, sems, ins):
    def sb(name, shape, dt=F32):
        return ctx.enter_context(nc.sbuf_tensor(name, shape, dt))

    bmod = sb("bmod1", [P, 4, CH])
    bgate = sb("bgate", [B, 2, C])
    gates = sb("gates", [B, 2, C])
    bias_in, mod_psum, gate_psum, gates_ready, gate_dram = (
        sems.new(n) for n in ("ada_bias_in", "ada_mod_psum", "gate_psum", "gates_ready", "gate_dram"))
    sh.gate_in = sems.new("gate_in")
    sh.mod1_done = sems.new("mod1_done")
    ada_b = ins["L1_xcond_ada_b"]
    part_at = [0, C, 3 * C, 4 * C]
    gate_at = [2 * C, 5 * C]

    def sync(sp):
        with nc.allow_non_contiguous_dma(reason="biases, a few KB in all"):
            for m, at in enumerate(part_at):
                sp.dma_start(bmod[:, m, :], ada_b[at:at + C].rearrange("(k p) -> p k", p=P)).then_inc(bias_in, 16)
            for g, at in enumerate(gate_at):
                sp.dma_start(bgate[:, g, :], ada_b[at:at + C].partition_broadcast(B)).then_inc(bias_in, 16)
        sp.wait_ge(gates_ready, 2)
        sp.dma_start(sh.dram["gate"], gates[:, :, :]).then_inc(gate_dram, 16)
        sp.wait_ge(gate_dram, 16)
        for g in range(2):
            sp.dma_start(sh.gate[g], sh.dram["gate"][:, g, :].partition_broadcast(T)).then_inc(sh.gate_in, 16)

    def vector(dve):
        dve.wait_ge(bias_in, 16 * 6)
        dve.wait_ge(mod_psum, 1)
        mp = sh.bank[6][:, 0:4 * CH * B].rearrange("p (m k b) -> p m k b", k=CH, b=B)
        for m in range(4):
            for k in range(CH):
                dve.tensor_scalar(sh.mod[:, 4 + m, k, :], mp[:, m, k, :], bmod[:, m, k:k + 1], MODS[4 + m][1], ALU.add, ALU.add).then_inc(sh.mod1_done, 1)
        dve.wait_ge(gate_psum, 1)
        for g in range(2):
            dve.tensor_tensor(gates[:, g, :], sh.bank[7][0:B, g * C:(g + 1) * C], bgate[:, g, :], ALU.add).then_inc(gates_ready, 1)

    def tensor(pe):
        for m in range(4):
            for k in range(CH):
                o = (m * CH + k) * B
                for kk in range(CH):
                    last = pe.matmul(sh.bank[6][:, o:o + B], sh.wada[:, kk, part_at[m] + k * P:part_at[m] + (k + 1) * P],
                                     sh.silu_t[:, kk, :], start=kk == 0, stop=kk == CH - 1)
        last.then_inc(mod_psum, 1)
        for g in range(2):
            for kk in range(CH):
                last = pe.matmul(sh.bank[7][0:B, g * C:(g + 1) * C], sh.silu_t[:, kk, :],
                                 sh.wada[:, kk, gate_at[g]:gate_at[g] + C], start=kk == 0, stop=kk == CH - 1)
        last.then_inc(gate_psum, 1)

    return Parts(tensor, vector, None, None, sync, gate_psum=gate_psum, gates_ready=gates_ready)


def project(nc, sh, ctx, sems, name, eps, scale_of, bias_of, wq, bq, qkv, rooms, tensor_first=(), scalar_first=(), k_first=(), v_first=()):
    N4 = QUAD * T
    QUADS = B // QUAD

    def sb(n, shape, dt=F32):
        return ctx.enter_context(nc.sbuf_tensor(f"{name}_{n}", shape, dt))

    def sem(n):
        return sems.new(f"{name}_{n}")

    stats, mv = sb("stats", [T, B, 6]), sb("mv", [T, B, 2])
    veps, half, rstd = (sb(n, [T, B]) for n in ("veps", "half", "rstd"))
    def place(n, shape, dt=F32):
        room = rooms.get(n.split("_")[-1].rstrip("01"))
        return room.take(shape, dt) if room else sb(n, shape, dt)

    xn = place("xn", [T, B, C])
    xt = [place(f"xt{i}", [P, CH, N4]) for i in range(QUADS)]
    kinds = ["q", "k"] if qkv else ["q"]
    NK = len(kinds)
    full = {k: place(f"{k}_full", [P, CH, N4]) for k in kinds}
    rest = place("rest", [P, CH, N4])
    part = {k: place(f"{k}_part", [P, 3, CH, N4], BF16) for k in kinds}
    qb = sb("qb", [P, CH])
    half_set, qb_set, stats_done, aggr_done, veps_done, rstd_done, xn_done = (
        sem(n) for n in ("half_set", "qb_set", "stats_done", "aggr_done", "veps_done", "rstd_done", "xn_done"))
    xt_psum, xt_done, proj_psum, v_psum, full_done, v_done, split = (
        sem(n) for n in ("xt_psum", "xt_done", "proj_psum", "v_psum", "full_done", "v_done", "split"))
    written = sem("written")
    stacked = [sem(f"stacked{i}") for i in range(QUADS)]
    all_of = {"q": sh.q_all, "k": sh.k_all}
    banks_of = {"q": sh.bank[2:4], "k": sh.bank[4:6]}
    bias_col = {"q": qb, "k": sh.bcol[:, 3, :]}
    terms = {"q": TERMS_Q, "k": TERMS_K}

    def vector_norm(dve, first=()):
        wait_all(dve, first)
        for b in range(B):
            if b in (0, QUAD) and name == "p0":
                dve.wait_ge(sh.x_in, 32)
            dve.bn_stats(stats[:, b, :], sh.x[:, b, :]).then_inc(stats_done, 1)
        dve.wait_ge(stats_done, B)
        for b in range(B):
            dve.bn_aggr(mv[:, b, :], stats[:, b, :]).then_inc(aggr_done, 1)
        dve.wait_ge(aggr_done, B)
        dve.tensor_scalar(veps[:, :], mv[:, :, 1], eps, None, ALU.add).then_inc(veps_done, 1)
        dve.tensor_scalar(qb[:, :], bq, SCALE, None, ALU.mult).then_inc(qb_set, 1)
        dve.wait_ge(rstd_done, 1)
        for b in range(B):
            dve.tensor_scalar(xn[:, b, :], sh.x[:, b, :], mv[:, b, 0:1], rstd[:, b:b + 1],
                              ALU.subtract, ALU.mult).then_inc(xn_done, 1)

    def vector(dve):
        for i in range(QUADS):
            for n, k in enumerate(kinds):
                at = NK * i + n
                dve.wait_ge(full_done, CH * (at + 1))
                wait(dve, written, 16 * (at - NK + 1))
                dve.tensor_copy(part[k][:, 0, :, :], full[k][:, :, :]).then_inc(split, 1)
                dve.wait_ge(split, 4 * at + 1)
                dve.tensor_tensor(rest[:, :, :], full[k][:, :, :], part[k][:, 0, :, :], ALU.subtract).then_inc(split, 1)
                dve.wait_ge(split, 4 * at + 2)
                dve.tensor_copy(part[k][:, 1, :, :], rest[:, :, :]).then_inc(split, 1)
                dve.wait_ge(split, 4 * at + 3)
                dve.tensor_tensor(part[k][:, 2, :, :], rest[:, :, :], part[k][:, 1, :, :], ALU.subtract).then_inc(split, 1)
            if qkv:
                for j in range(0, QUAD, 2):
                    n = 2 * i + j // 2
                    dve.wait_ge(v_psum, n + 1)
                    b = QUAD * i + j
                    dve.tensor_tensor(sh.v_all[:, b:b + 2, :, 0:D],
                                      sh.bank[6 + j // 2][0:T, :].rearrange("t (j h d) -> t j h d", j=2, d=D),
                                      sh.brow[0:T, 2:3, :].rearrange("t o (h d) -> t o h d", d=D).broadcast_to([T, 2, H, D]),
                                      ALU.add).then_inc(v_done, 1)

    def gpsimd(pool):
        pool.memset(half[:, :], -0.5).then_inc(half_set, 1)
        pool.wait_ge(half_set, 1)
        pool.wait_ge(veps_done, 1)
        pool.tensor_tensor(rstd[:, :], veps[:, :], half[:, :], ALU.pow).then_inc(rstd_done, 1)

    def scalar(act):
        act.wait_ge(qb_set, 1)
        wait_all(act, scalar_first)
        for i in range(QUADS):
            for c in range(CH):
                act.wait_ge(xt_psum, CH * i + c + 1)
                for j in range(QUAD):
                    b = QUAD * i + j
                    act.activation(xt[i][:, c, j * T:(j + 1) * T], sh.bank[c][:, j * T:(j + 1) * T], ACT.Identity,
                                   bias=bias_of(c, b), scale=scale_of(c, b)).then_inc(xt_done, 1)
            for n, k in enumerate(kinds):
                at = NK * i + n
                wait(act, split, 4 * (at - NK + 1))
                for m in range(CH):
                    act.wait_ge(proj_psum, CH * at + m + 1)
                    act.activation(full[k][:, m, :], banks_of[k][m][:, 0:N4], ACT.Identity,
                                   bias=bias_col[k][:, m:m + 1], scale=SCALE if k == "q" else 1.0).then_inc(full_done, 1)

    def tensor(pe):
        for i in range(QUADS):
            pe.wait_ge(xn_done, QUAD * (i + 1))
            wait(pe, xt_done, CH * QUAD * i)
            for c in range(CH):
                for j in range(QUAD):
                    last = pe.transpose(sh.bank[c][:, j * T:(j + 1) * T], xn[:, QUAD * i + j, c * P:(c + 1) * P], sh.ident[0:T, 0:T])
                last.then_inc(xt_psum, 1)
            if i == 0:
                wait_all(pe, tensor_first)
            pe.wait_ge(xt_done, CH * QUAD * (i + 1))
            for n, k in enumerate(kinds):
                for m in range(CH):
                    wait(pe, full_done, CH * (NK * (i - 1) + n) + m + 1)
                    for c in range(CH):
                        last = pe.matmul(banks_of[k][m][:, 0:N4], wq[:, c, n * C + m * P:n * C + (m + 1) * P], xt[i][:, c, :],
                                         start=c == 0, stop=c == CH - 1)
                    last.then_inc(proj_psum, 1)
            if qkv:
                if i == 0:
                    wait_all(pe, v_first)
                for j in range(0, QUAD, 2):
                    wait(pe, v_done, 2 * (i - 1) + j // 2 + 1)
                    for jj in (j, j + 1):
                        for c in range(CH):
                            last = pe.matmul(sh.bank[6 + j // 2][0:T, (jj - j) * C:(jj - j + 1) * C], xt[i][:, c, jj * T:(jj + 1) * T],
                                             wq[:, c, 2 * C:3 * C], start=c == 0, stop=c == CH - 1)
                    last.then_inc(v_psum, 1)

    def sync(sp):
        for i in range(QUADS):
            for n, k in enumerate(kinds):
                at = NK * i + n
                sp.wait_ge(split, 4 * (at + 1))
                d = sh.dram[f"{k}_parts"]
                sp.dma_start(d[i].rearrange("t c p n -> p t c n"), part[k][:, :, :, :]).then_inc(written, 16)
                sp.wait_ge(written, 16 * (at + 1))
                if k == "k" and i == 0:
                    wait_all(sp, k_first)
                for s, w in enumerate(terms[k]):
                    sp.dma_start(all_of[k][s * D:(s + 1) * D, :, i * N4:(i + 1) * N4],
                                 d[i, w].rearrange("c (h d) n -> d (c h) n", d=D)).then_inc(stacked[i], 16)

    return Parts(tensor, vector, scalar, gpsimd, sync, vector_norm=vector_norm,
                 stacked=stacked, stacked_count=16 * NTERM * NK,
                 banks_read=[(full_done, CH * NK * QUADS)] + ([(v_done, 2 * QUADS)] if qkv else []),
                 x_read=[(xn_done, B)])


def attend(nc, sh, ctx, sems, name, cross, ln, wkv, bk, bv_row, wo, bo_row, gate, stacks, first, ahead=None):
    keys = KEYS if cross else [T]
    nt = len(keys)
    nk = sum(keys)
    GH = 4
    NG = H // GH
    NU = NG * nt
    HS = 1 if cross else 4
    NS = H // HS
    LAG = 1 if cross else 2
    S_AT = [0, 3, 6, 8, 11, 14, 16, 16, 16, 16, 16, 16, 16, 16] if cross else [0, 2, 4, 4, 4, 4]
    K0, K1, V0, V1, T0, T1 = range(6)
    FILL_AT = {0: K0, 2: K1, 7: V0, 9: V1, 10: T0, 12: T1} if cross else {}
    MID_AT = {3: 0, 5: 1}
    LOAD_MAX_AT = 8
    MAX_AT = 7 if cross else 3
    TAIL_AT = {1: 0, 3: 1, 5: 2} if cross else {0: 0, 2: 1, 4: 2}

    def sb(n, shape, dt=F32):
        return ctx.enter_context(nc.sbuf_tensor(f"{name}_{n}", shape, dt))

    def sem(n):
        return sems.new(f"{name}_{n}")

    score, score_t, pv, cx, tb = [sh.bank[0], sh.bank[1], sh.bank[7]], [sh.bank[2], sh.bank[3]], sh.bank[4], sh.bank[5], sh.bank[6]
    nm_bank = (tb if cross else cx)[:, CH * T:CH * T + T // 2].bitcast(BF16)
    prob = [sb(f"prob{i}", [P, GH * T]) for i in range(2)]
    nmax, nrest, nparts = sb("nmax", [T, H]), sb("nrest", [T, H]), sb("nparts", [T, P // H, H], BF16)
    nm_t = [sb(f"nm_t{i}", [3 * H, T], BF16) for i in range(2)]
    pv_sb = sb("pv_sb", [P, NG * T])
    rden = sb("rden", [T, H])
    on = sb("on", [T, C])
    ot = sb("ot", [P, CH, T])
    if gate is not None:
        gated, bog = sb("gated", [T, C]), sb("bog", [T, C])
    if cross:
        xn = sb("xn", [P, NT, C])
        ct, kf, kr = sh.ctx_t[0:2], sh.ctx_t[2], sh.ctx_t[3]
        kp = [sb("kp", [P, 3, CH, L], BF16), Room(sh.v_space).take([P, 3, CH, L], BF16)]
    xn_done, fill_psum, fill_read, rest_done, mid_done = (
        sem(n) for n in ("xn_done", "fill_psum", "fill_read", "rest_done", "mid_done"))
    split = [sem(f"split{c}") for c in range(CH)]
    stacked = [[sem(f"stacked{s}{c}") for c in range(CH)] for s in range(2)]
    v_done, w_copied, w_ordered = sem("v_done"), sem("w_copied"), sem("w_ordered")
    v_loaded = [sem(f"v_loaded{s}") for s in range(2)]
    s_psum, max_done, nm_step, nm_psum, nm_done = (sem(n) for n in ("s_psum", "max_done", "nm_step", "nm_psum", "nm_done"))
    nparts_set, pad_set, ones_set = sem("nparts_set"), sem("pad_set"), sem("ones_set")
    nm_in = [sem(f"nm_in{s}") for s in range(2)]
    st_psum, exp_done, pv_psum, pv_read = (sem(n) for n in ("st_psum", "exp_done", "pv_psum", "pv_read"))
    tail1, rden_done, on_done, tail2, ot_done, tail3, tb_free, base_done, bog_done, gated_done = (
        sem(n) for n in ("tail1", "rden_done", "on_done", "tail2", "ot_done", "tail3", "tb_free", "base_done", "bog_done", "gated_done"))

    def has_fill(slot, k):
        b = slot + (2 if k in (K0, K1) else 1 if k in (V0, V1) else 3)
        return not isinstance(slot, int) or 0 <= b < B

    def fill_no(slot, k):
        if isinstance(slot, int):
            return sum(has_fill(s, j) for s in range(-3, slot) for j in range(6)) + sum(has_fill(slot, j) for j in range(k))
        return 6 * slot + 12 + k


    def pe_fill(pe, slot, k, par):
        wait(pe, fill_read, fill_no(slot, k))
        if k in (K0, K1):
            m = k - K0
            for c in range(CH):
                ins_ = pe.matmul(cx[:, 0:L], wkv[:, c, m * P:(m + 1) * P], ct[par][:, c, :], start=c == 0, stop=c == CH - 1)
        elif k in (V0, V1):
            for t in ((0, 1) if k == V0 else (2,)):
                rows = keys[t]
                for c in range(CH):
                    ins_ = pe.matmul(cx[0:rows, (t % 2) * C:(t % 2 + 1) * C], ct[1 - par][:, c, t * P:t * P + rows], wkv[:, c, C:2 * C],
                                     start=c == 0, stop=c == CH - 1)
        else:
            c = k - T0
            if c == 0:
                wait(pe, xn_done, NT * (slot + 4))
            for t, rows in enumerate(keys):
                ins_ = pe.transpose(cx[:, t * P:t * P + rows], xn[0:rows, t, c * P:(c + 1) * P], sh.ident[0:rows, 0:rows])
        ins_.then_inc(fill_psum, 1)

    def pe_scores(pe, b, par, lo, hi, cnt):
        for i in range(lo, hi):
            if i == 0 and isinstance(b, int) and b == 0:
                pe.wait_ge(stacks.more["stacked"][0], stacks.more["stacked_count"])
            if cross and i == 0:
                pe.wait_ge(stacked[par][0], cnt * 16 * NTERM)
            if cross and i * HS == HC:
                pe.wait_ge(stacked[par][1], cnt * 16 * NTERM)
            wait(pe, max_done, NS * b + (i - 2 if i else 0))
            for h in range(i * HS, (i + 1) * HS):
                o = (h - i * HS) * T
                w = L if cross else T
                keys_h = sh.k_st[par][0:DEEP, h, 0:w] if cross else sh.k_all[0:DEEP, h, bass.ds(b * T, T)]
                ins_ = pe.matmul(score[i % 3][:, o:o + w], sh.q_all[0:DEEP, h, bass.ds(b * T, P)], keys_h, start=True, stop=True)
            ins_.then_inc(s_psum, 1)

    def pe_max_t(pe, b):
        pe.wait_ge(nm_step, 4 * b + 4)
        wait(pe, nm_done, b)
        pe.transpose(nm_bank, nparts[:, :, :].rearrange("t a h -> t (a h)"),
                     sh.ident_bf[0:T, 0:T]).then_inc(nm_psum, 1)

    def pe_scores_t(pe, b, par, u, cnt):
        g, t = u // nt, u % nt
        if u == 0:
            pe.wait_ge(nm_in[par], 16 * cnt)
        wait(pe, exp_done, NU * b + u - 1)
        for j in range(GH):
            h = g * GH + j
            keys_h = sh.k_st[par][0:AUG, h, t * P:(t + 1) * P] if cross else sh.k_all[0:AUG, h, bass.ds(b * T, P)]
            ins_ = pe.matmul(score_t[u % 2][:, j * T:(j + 1) * T], keys_h, sh.q_all[0:AUG, h, bass.ds(b * T, T)],
                             start=True, stop=True)
        ins_.then_inc(st_psum, 1)

    def pe_values(pe, b, slot, par, u, cnt):
        g, t = u // nt, u % nt
        if u == 0:
            wait(pe, pv_read, b)
            if cross:
                pe.wait_ge(v_done, NT * (b + 1))
            else:
                pe.wait_ge(v_loaded[par], 16 * cnt)
        pe.wait_ge(exp_done, NU * b + u + 1)
        rows = keys[t]
        for j in range(GH):
            h = g * GH + j
            ins_ = pe.matmul(pv[32 * j:32 * j + D + 1, g * T:(g + 1) * T], sh.v_sb[par][0:rows, t, h, :],
                             prob[u % 2][0:rows, j * T:(j + 1) * T], start=t == 0, stop=t == nt - 1)
        ins_.then_inc(pv_psum, 1)

    def pe_tail(pe, b, step):
        if step == 0:
            pe.wait_ge(pv_read, b + 1)
            pe.wait_ge(tb_free, b + 1)
            if cross:
                pe.wait_ge(nm_done, min(b + 2, B) if isinstance(b, int) else b + 2)
            for g in range(NG):
                ins_ = pe.transpose(tb[0:T, g * P:(g + 1) * P], pv_sb[:, g * T:(g + 1) * T], sh.ident[:, :])
            ins_.then_inc(tail1, 1)
        elif step == 1:
            pe.wait_ge(on_done, b + 1)
            for c in range(CH):
                ins_ = pe.transpose(tb[:, c * T:(c + 1) * T], on[:, c * P:(c + 1) * P], sh.ident[0:T, 0:T])
            ins_.then_inc(tail2, 1)
        else:
            pe.wait_ge(ot_done, b + 1)
            for c in range(CH):
                ins_ = pe.matmul(tb[0:T, 0:C], ot[:, c, :], wo[:, c, :], start=c == 0, stop=c == CH - 1)
            ins_.then_inc(tail3, 1)

    def pe_slot(pe, b, par, cnt, has_e, has_s, has_tail):
        for u in range(NU + 1):
            if has_e and u < NU:
                pe_scores_t(pe, b, par, u, cnt[0])
            if has_tail and u in TAIL_AT:
                pe_tail(pe, b - 1, TAIL_AT[u])
            if u in FILL_AT and has_fill(b, FILL_AT[u]):
                pe_fill(pe, b, FILL_AT[u], par)
            if has_s:
                pe_scores(pe, b + LAG, (par + LAG) % 2, S_AT[u], S_AT[u + 1], cnt[1])
                if u == MAX_AT:
                    pe_max_t(pe, b + LAG)
            if has_e and u > 0:
                pe_values(pe, b, b, par, u - 1, cnt[0])

    def act_slot(act, b, par, cnt, has_e, has_s, has_tail):
        for u in range(NU + 1):
            if has_e and u < NU:
                rows = keys[u % nt]
                act.wait_ge(st_psum, NU * b + u + 1)
                wait(act, pv_psum, NU * b + u - 1)
                act.activation(prob[u % 2][0:rows, :], score_t[u % 2][0:rows, 0:GH * T], ACT.Exp).then_inc(exp_done, 1)
            if has_s and cross and u == LOAD_MAX_AT:
                load_max(act, b + LAG, (par + LAG) % 2)
            if has_tail and TAIL_AT.get(u) == 1:
                act.wait_ge(tail2, b)
                act.activation(ot[:, :, :], tb[:, 0:CH * T].rearrange("p (c n) -> p c n", c=CH), ACT.Copy).then_inc(ot_done, 1)
            if FILL_AT.get(u) in (K0, K1) and has_fill(b, K0):
                m = FILL_AT[u] - K0
                act.wait_ge(fill_psum, fill_no(b, K0 + m) + 1)
                act.activation(kf[:, m, :], cx[:, 0:L], ACT.Identity, bias=bk[:, m:m + 1])
                wait(act, stacked[par][m], 16 * NTERM * cnt[0])
                act.activation(kp[par][:, 0, m, :], cx[:, 0:L], ACT.Identity, bias=bk[:, m:m + 1]).then_inc(fill_read, 1)
            if cross and u in MID_AT and has_fill(b, K0):
                m = MID_AT[u]
                act.wait_ge(rest_done, CH * (b + 2) + m + 1)
                act.activation(kp[par][:, 1, m, :], kr[:, m, :], ACT.Copy).then_inc(mid_done, 1)
            if FILL_AT.get(u) in (V0, V1) and has_fill(b, V0):
                k = FILL_AT[u]
                act.wait_ge(fill_psum, fill_no(b, k) + 1)
                wait(act, pv_psum, NU * b)
                for t in ((0, 1) if k == V0 else (2,)):
                    rows = keys[t]
                    last = act.activation(sh.v_sb[1 - par][0:rows, t, :, 0:D],
                                          cx[0:rows, (t % 2) * C:(t % 2 + 1) * C].rearrange("p (h d) -> p h d", d=D), ACT.Copy)
                last.then_inc(fill_read, 1)
            if FILL_AT.get(u) in (T0, T1) and has_fill(b, T0):
                c = FILL_AT[u] - T0
                act.wait_ge(fill_psum, fill_no(b, T0 + c) + 1)
                if ln:
                    act.activation(ct[1 - par][:, c, :], cx[:, 0:L], ACT.Identity, bias=sh.mod[:, 3, c, bass.ds(b + 3, 1)],
                                   scale=sh.mod[:, 2, c, bass.ds(b + 3, 1)]).then_inc(fill_read, 1)
                else:
                    act.activation(ct[1 - par][:, c, :], cx[:, 0:L], ACT.Copy).then_inc(fill_read, 1)
        if has_e:
            act.wait_ge(pv_psum, NU * b + NU)
            wait(act, tail1, b)
            act.activation(pv_sb[:, :], pv[:, 0:NG * T], ACT.Copy).then_inc(pv_read, 1)

    def dve_norm_context(dve, b):
        if not isinstance(b, int) or b > 0:
            dve.wait_ge(fill_psum, fill_no(b - 4, T1) + 1)
        for t in range(NT):
            x_in = sh.ctx[:, bass.ds(b, 1), t, :]
            if ln:
                dve.tensor_scalar(xn[:, t, :], x_in, sh.ctx_mean[:, bass.ds(b, 1), t], sh.ctx_rstd[:, bass.ds(b, 1), t],
                                  ALU.subtract, ALU.mult).then_inc(xn_done, 1)
            else:
                dve.tensor_copy(xn[:, t, :], x_in).then_inc(xn_done, 1)

    def dve_slot(dve, b, par, cnt, has_e, has_s, has_tail, norm_next):
        for u in range(NU + 1):
            if has_tail and TAIL_AT.get(u) == 0:
                dve.wait_ge(tail1, b)
                tp = tb[0:T, :].rearrange("t (h e) -> t h e", e=32)
                dve.reciprocal(rden[:, :], tp[:, :, D]).then_inc(rden_done, 1)
                dve.wait_ge(rden_done, b)
                dve.tensor_tensor(on[:, :].rearrange("t (h d) -> t h d", d=D), tp[:, :, 0:D],
                                  rden[:, :].rearrange("t (h o) -> t h o", o=1).broadcast_to([T, H, D]), ALU.mult).then_inc(on_done, 1)
            if has_tail and TAIL_AT.get(u) == 2:
                xb = sh.x[:, bass.ds(b - 1, 1), :].rearrange("t o c -> t (o c)")
                dve.wait_ge(tail3, b)
                dve.wait_ge(base_done, b)
                if gate is None:
                    dve.tensor_tensor(xb, tb[0:T, 0:C], xb, ALU.add).then_inc(tb_free, 1)
                else:
                    dve.tensor_tensor(gated[:, :], tb[0:T, 0:C], sh.gate[gate][:, bass.ds(b - 1, 1), :].rearrange("t o c -> t (o c)"),
                                      ALU.mult).then_inc(gated_done, 1)
                    dve.wait_ge(gated_done, b)
                    dve.tensor_tensor(xb, gated[:, :], xb, ALU.add).then_inc(tb_free, 1)
            if has_s:
                n = b + LAG
                for i in range(S_AT[u], S_AT[u + 1]):
                    dve.wait_ge(s_psum, NS * n + i + 1)
                    if i == 0:
                        wait(dve, nm_step, 4 * n)
                    w = L if cross else T
                    dve.tensor_reduce(nmax[:, i * HS:(i + 1) * HS], score[i % 3][0:T, 0:HS * w].rearrange("t (h k) -> t h k", k=w),
                                      AX_X, ALU.max, negate=True).then_inc(max_done, 1)
            if has_s and u == MAX_AT:
                dve.wait_ge(max_done, NS * (n + 1))
                wait(dve, nm_psum, n)
                dve.tensor_copy(nparts[:, 0, :], nmax[:, :]).then_inc(nm_step, 1)
                dve.wait_ge(nm_step, 4 * n + 1)
                dve.tensor_tensor(nrest[:, :], nmax[:, :], nparts[:, 0, :], ALU.subtract).then_inc(nm_step, 1)
                dve.wait_ge(nm_step, 4 * n + 2)
                dve.tensor_copy(nparts[:, 1, :], nrest[:, :]).then_inc(nm_step, 1)
                dve.wait_ge(nm_step, 4 * n + 3)
                dve.tensor_tensor(nparts[:, 2, :], nrest[:, :], nparts[:, 1, :], ALU.subtract).then_inc(nm_step, 1)
                dve.wait_ge(nm_psum, n + 1)
                wait(dve, nm_in[(par + LAG) % 2], 16 * (cnt[1] - 1))
                dve.tensor_copy(nm_t[(par + LAG) % 2][:, :], nm_bank[0:3 * H, :]).then_inc(nm_done, 1)
            if norm_next and u == MAX_AT:
                dve_norm_context(dve, b + 3)

    def pool_slot(pool, b, par, has_e):
        if has_e:
            xb = sh.x[:, bass.ds(b, 1), :].rearrange("t o c -> t (o c)")
            if gate is None:
                pool.tensor_tensor(xb, xb, sh.brow[0:T, bo_row, :], ALU.add).then_inc(base_done, 1)
            else:
                wait(pool, base_done, b)
                pool.tensor_tensor(bog[:, :], sh.gate[gate][:, bass.ds(b, 1), :].rearrange("t o c -> t (o c)"),
                                   sh.brow[0:T, bo_row, :], ALU.mult).then_inc(bog_done, 1)
                pool.wait_ge(bog_done, b + 1)
                pool.tensor_tensor(xb, xb, bog[:, :], ALU.add).then_inc(base_done, 1)
        if cross and has_fill(b, K0):
            for m in range(CH):
                n = CH * (b + 2) + m
                pool.wait_ge(fill_read, fill_no(b, K0 + m) + 1)
                pool.tensor_tensor(kr[:, m, :], kf[:, m, :], kp[par][:, 0, m, :], ALU.subtract).then_inc(rest_done, 1)
                pool.wait_ge(mid_done, n + 1)
                pool.tensor_tensor(kp[par][:, 2, m, :], kr[:, m, :], kp[par][:, 1, m, :], ALU.subtract).then_inc(split[m], 3)
        if cross and has_fill(b, V0):
            for t, k in enumerate((V0, V0, V1)):
                if t != 1:
                    pool.wait_ge(fill_read, fill_no(b, k) + 1)
                v = sh.v_sb[1 - par][0:keys[t], t, :, 0:D]
                pool.tensor_tensor(v, v, sh.brow[0:keys[t], bv_row, :].rearrange("p (h d) -> p h d", d=D), ALU.add).then_inc(v_done, 1)

    def sp_load_half(sp, b, par, c):
        wait(sp, st_psum, NU * (b - 2) + (NU // 2) * (c + 1))
        sp.wait_ge(split[c], 3 * (b + 1))
        for s, w in enumerate(TERMS_K):
            sp.dma_start(sh.k_st[par][s * D:(s + 1) * D, c * HC:(c + 1) * HC, 0:L], kp[par][:, w, c, :]).then_inc(stacked[par][c], 16)

    def load_max(eng, b, par):
        eng.wait_ge(nm_done, b + 1)
        eng.dma_start(sh.q_all[DEEP:AUG, :, bass.ds(b * T, T)], nm_t[par][:, :]).then_inc(nm_in[par], 16)

    def sp_load_values(sp, b, par):
        wait(sp, pv_psum, NU * (b - 1))
        sp.dma_start(sh.v_sb[par][0:T, 0, :, :], sh.v_all[:, bass.ds(b, 1), :, :]).then_inc(v_loaded[par], 16)

    def sp_slot(sp, b, par, cnt, has_s, has_load):
        if has_load and cross:
            sp_load_half(sp, b + 2, par, 0)
        elif has_load:
            sp_load_values(sp, b + 2, par)
        if has_s and not cross:
            load_max(sp, b + LAG, (par + LAG) % 2)
        if has_load and cross:
            sp_load_half(sp, b + 2, par, 1)

    AHEAD = (-3, -2) if cross else ()

    def within(b, ahead):
        return not isinstance(b, int) or 0 <= b + ahead < B

    def run(slot, slots):
        for b in slots:
            slot(b, b % 2, (b // 2 + 1, (b + LAG) // 2 + 1))

    def run_main(eng, slot, before_loop=()):
        run(slot, range(-1 if cross else -2, 1))
        wait_all(eng, before_loop)
        with eng.Fori(0, 2) as i:
            slot(2 * i + 1, 1, (i + 1, i + 2))
            slot(2 * i + 2, 0, (i + 2, i + 1 + LAG))
        run(slot, range(5, B + 1))

    def on_tensor(pe):
        return lambda b, par, cnt: pe_slot(pe, b, par, cnt, within(b, 0), within(b, LAG), within(b, -1))

    def on_scalar(act):
        return lambda b, par, cnt: act_slot(act, b, par, cnt, within(b, 0), within(b, LAG), within(b, -1))

    def on_vector(dve):
        return lambda b, par, cnt: dve_slot(dve, b, par, cnt, within(b, 0), within(b, LAG), within(b, -1), cross and within(b, 3))

    def on_gpsimd(pool):
        return lambda b, par, cnt: pool_slot(pool, b, par, within(b, 0))

    def on_sync(sp):
        return lambda b, par, cnt: sp_slot(sp, b, par, cnt, within(b, LAG), within(b, 2))


    def tensor_ahead(pe):
        wait_all(pe, ahead["tensor"])
        pe.wait_ge(w_ordered, CH)
        run(on_tensor(pe), AHEAD)

    def scalar_ahead(act):
        wait_all(act, ahead["scalar"])
        run(on_scalar(act), AHEAD)

    def vector_ahead(dve):
        wait_all(dve, ahead["vector"])
        w_heads = kr[:, :, 0:C]
        dve.tensor_copy(w_heads, wkv[:, :, 0:C]).then_inc(w_copied, 1)
        dve.wait_ge(w_copied, 1)
        for c in range(CH):
            dve.tensor_copy(wkv[:, c, 0:C].rearrange("p (m d h) -> p m d h", m=CH, h=HC),
                            w_heads[:, c, :].rearrange("p (m h d) -> p m d h", m=CH, d=D)).then_inc(w_ordered, 1)
        run(on_vector(dve), AHEAD)

    def gpsimd_pads(pool):
        for s in range(2):
            pool.memset(sh.k_st[s][:, :, L:], 0.0).then_inc(pad_set, 1)
        pool.wait_ge(pad_set, 2)

    def gpsimd_ones(pool, behind=None):
        if behind is not None:
            pool.wait_ge(split[behind], 3)
        for s in range(2):
            pool.memset(sh.k_st[s][DEEP:AUG, :, :], 1.0).then_inc(ones_set, 1)
        pool.wait_ge(ones_set, 2)

    def gpsimd_ahead(pool):
        run(on_gpsimd(pool), AHEAD)

    def sync_ahead(sp):
        sp.wait_ge(pad_set, 2)
        run(on_sync(sp), AHEAD)


    def tensor(pe):
        wait_all(pe, first["tensor"])
        pe.wait_ge(nparts_set, 1)
        if cross:
            pe.wait_ge(ones_set, 2)
        run_main(pe, on_tensor(pe), [(stacks.more["stacked"][1], stacks.more["stacked_count"])])

    def scalar(act):
        run_main(act, on_scalar(act))

    def vector(dve):
        dve.memset(nparts[:, 3:5, :], 0.0).then_inc(nparts_set, 1)
        dve.memset(nparts[:, 5:, :], 0.0).then_inc(tb_free, 1)
        run_main(dve, on_vector(dve))

    def gpsimd(pool):
        wait_all(pool, first["gpsimd"])
        run_main(pool, on_gpsimd(pool))

    def sync(sp):
        wait_all(sp, first["sync"])
        run_main(sp, on_sync(sp))

    return Parts(tensor, vector, scalar, gpsimd, sync, tensor_ahead=tensor_ahead, vector_ahead=vector_ahead,
                 scalar_ahead=scalar_ahead, gpsimd_ahead=gpsimd_ahead, sync_ahead=sync_ahead,
                 gpsimd_pads=gpsimd_pads, gpsimd_ones=gpsimd_ones)


def phase_mlp(nc, sh, ins, out):
    N2 = 2 * T
    NH = HID // P
    with ExitStack() as ctx:
        semaphores = ctx.enter_context(Semaphores(nc))

        def sb(n, shape, dt=F32):
            return ctx.enter_context(nc.sbuf_tensor(f"mlp_{n}", shape, dt))

        def sem(n):
            return semaphores.new(f"mlp_{n}")

        w1, w2 = sh.w1, sh.w2
        stats, mv, veps, half, rstd, pause = sb("stats", [T, 2, 6]), sb("mv", [T, 2, 2]), sb("veps", [T, 2]), sb("half", [T, 2]), sb("rstd", [T, 2]), sb("pause", [T, 1])
        xn = sb("xn", [T, 2, C])
        xt = sb("xt", [P, CH, N2])
        hid = sb("hid", [P, NH, N2])
        y, yg, yo = sb("y", [T, 2, C]), sb("yg", [T, 2, C]), sb("yo", [T, 2, C])
        half_set, stats_done, aggr_done, veps_done, rstd_done, xn_done = (
            sem(n) for n in ("half_set", "stats_done", "aggr_done", "veps_done", "rstd_done", "xn_done"))
        xt_psum, xt_done, h_psum, hid_done, y_psum, y_step, stored = (
            sem(n) for n in ("xt_psum", "xt_done", "h_psum", "hid_done", "y_psum", "y_step", "stored"))
        xt_bank, y_bank = sh.bank[0], sh.bank[7]

        def norm(dve, p):
            for j in range(2):
                dve.bn_stats(stats[:, j, :], sh.x[:, bass.ds(2 * p + j, 1), :]).then_inc(stats_done, 1)
            dve.wait_ge(stats_done, 2 * p + 2)
            dve.memset(pause[:, :], 0.0)
            for j in range(2):
                dve.bn_aggr(mv[:, j, :], stats[:, j, :]).then_inc(aggr_done, 1)
            dve.wait_ge(aggr_done, 2 * p + 2)
            dve.tensor_scalar(veps[:, :], mv[:, :, 1], 1e-6, None, ALU.add).then_inc(veps_done, 1)
            dve.wait_ge(rstd_done, p + 1)
            wait(dve, xt_psum, p)
            for j in range(2):
                dve.tensor_scalar(xn[:, j, :], sh.x[:, bass.ds(2 * p + j, 1), :], mv[:, j, 0:1], rstd[:, j:j + 1],
                                  ALU.subtract, ALU.mult).then_inc(xn_done, 1)

        def modulate(dve, p):
            dve.wait_ge(xt_psum, p + 1)
            for c in range(CH):
                for j in range(2):
                    o = (c * 2 + j) * T
                    dve.tensor_scalar(xt[:, c, j * T:(j + 1) * T], xt_bank[:, o:o + T], sh.mod[:, 7, c, bass.ds(2 * p + j, 1)],
                                      sh.mod[:, 6, c, bass.ds(2 * p + j, 1)], ALU.mult, ALU.add).then_inc(xt_done, 1)

        def finish(dve, p):
            dve.wait_ge(y_psum, p + 1)
            dve.tensor_tensor(y[:, :, :], y_bank[0:T, :].rearrange("t (j c) -> t j c", j=2),
                              sh.brow[0:T, 6:7, :].broadcast_to([T, 2, C]), ALU.add).then_inc(y_step, 1)
            dve.wait_ge(y_step, 3 * p + 1)
            dve.tensor_tensor(yg[:, :, :], y[:, :, :], sh.gate[1][:, bass.ds(2 * p, 2), :], ALU.mult).then_inc(y_step, 1)
            dve.wait_ge(y_step, 3 * p + 2)
            wait(dve, stored, 16 * p)
            dve.tensor_tensor(yo[:, :, :], yg[:, :, :], sh.x[:, bass.ds(2 * p, 2), :], ALU.add).then_inc(y_step, 1)

        def transposes(pe, p):
            pe.wait_ge(xn_done, 2 * p + 2)
            wait(pe, xt_done, 4 * p)
            for c in range(CH):
                for j in range(2):
                    o = (c * 2 + j) * T
                    last = pe.transpose(xt_bank[:, o:o + T], xn[:, j, c * P:(c + 1) * P], sh.ident[0:T, 0:T])
            last.then_inc(xt_psum, 1)

        def first_matmuls(pe, p):
            pe.wait_ge(xt_done, 4 * p + 4)
            for m in range(NH):
                wait(pe, hid_done, NH * p + m - 3)
                for c in range(CH):
                    last = pe.matmul(sh.bank[1 + m % 4][:, 0:N2], w1[:, c, m * P:(m + 1) * P], xt[:, c, :],
                                     start=c == 0, stop=c == CH - 1)
                last.then_inc(h_psum, 1)

        def second_matmuls(pe, p):
            wait(pe, y_step, 3 * p - 2)
            for j in range(2):
                for m in range(NH):
                    if j == 0:
                        pe.wait_ge(hid_done, NH * p + m + 1)
                    last = pe.matmul(y_bank[0:T, j * C:(j + 1) * C], hid[:, m, j * T:(j + 1) * T], w2[:, m, :],
                                     start=m == 0, stop=m == NH - 1)
            last.then_inc(y_psum, 1)

        with nc.Block() as block:
            @block.sync
            def _(sp):
                with sp.Fori(0, PAIRS) as p:
                    sp.wait_ge(y_step, 3 * p + 3)
                    sp.dma_start(out[bass.ds(2 * p, 2)].rearrange("j n c -> n j c"), yo[:, :, :]).then_inc(stored, 16)
                sp.wait_ge(stored, 16 * PAIRS)

            @block.gpsimd
            def _(pool):
                pool.memset(half[:, :], -0.5).then_inc(half_set, 1)
                pool.wait_ge(half_set, 1)
                with pool.Fori(0, PAIRS) as p:
                    pool.wait_ge(veps_done, p + 1)
                    pool.tensor_tensor(rstd[:, :], veps[:, :], half[:, :], ALU.pow).then_inc(rstd_done, 1)

            @block.vector
            def _(dve):
                norm(dve, 0)
                modulate(dve, 0)
                norm(dve, 1)
                modulate(dve, 1)
                finish(dve, 0)
                with dve.Fori(1, PAIRS - 1) as p:
                    norm(dve, p + 1)
                    modulate(dve, p + 1)
                    finish(dve, p)
                finish(dve, PAIRS - 1)

            @block.scalar
            def _(act):
                def hidden(p):
                    for m in range(NH):
                        act.wait_ge(h_psum, NH * p + m + 1)
                        if m == 0:
                            wait(act, y_psum, p)
                        act.activation(hid[:, m, :], sh.bank[1 + m % 4][:, 0:N2], ACT.Gelu_apprx_tanh,
                                       bias=sh.bhid[:, m:m + 1]).then_inc(hid_done, 1)
                hidden(0)
                with act.Fori(1, PAIRS) as p:
                    hidden(p)

            @block.tensor
            def _(pe):
                transposes(pe, 0)
                first_matmuls(pe, 0)
                transposes(pe, 1)
                second_matmuls(pe, 0)
                with pe.Fori(1, PAIRS - 1) as p:
                    first_matmuls(pe, p)
                    transposes(pe, p + 1)
                    second_matmuls(pe, p)
                first_matmuls(pe, PAIRS - 1)
                second_matmuls(pe, PAIRS - 1)


def modulation(sh, m):
    return lambda c, b: sh.mod[:, m, c, b:b + 1]


def first_layer(nc, sh, ins):
    with ExitStack() as ctx:
        sems = ctx.enter_context(Semaphores(nc))
        ld = load(nc, sh, ctx, sems, ins)
        NM = 4 * CH
        pj = project(nc, sh, ctx, sems, "p0", 1e-5, modulation(sh, 0), modulation(sh, 1), sh.wq0, sh.bcol[:, 0, :], False,
                     {"xn": Room(sh.v_space), "xt": Room(sh.gate_space[0]), "full": Room(sh.gate_space[1]), "rest": Room(sh.gate_space[1][:, 1024:])},
                     tensor_first=[(sh.wq_in, 16 * 8)], scalar_first=[(sh.mod_done, NM)])
        w_all = 16 * 13
        at = attend(nc, sh, ctx, sems, "a0", True, True, sh.wkv0, sh.bcol[:, 1, :], 0, sh.wo0, 1, None, pj, {
            "tensor": pj.more["banks_read"] + [(sh.consts_done, 4)],
            "gpsimd": pj.more["x_read"], "sync": []}, {
            "tensor": [(sh.w_in, w_all), (sh.mod_done, NM)], "scalar": [(sh.mod_done, NM), (sh.w_in, w_all)],
            "vector": [(sh.ctx_stats_done, 2), (sh.w_in, w_all)]})
        block = ctx.enter_context(nc.Block())

        @block.sync
        def _(sp):
            ld.sync(sp)
            pj.sync(sp)
            at.more["sync_ahead"](sp)
            at.sync(sp)
            sp.wait_ge(sh.late_in, 16 * 6)

        @block.gpsimd
        def _(pool):
            ld.gpsimd(pool)
            at.more["gpsimd_pads"](pool)
            at.more["gpsimd_ones"](pool)
            pj.gpsimd(pool)
            ld.more["gpsimd_late"](pool)
            at.more["gpsimd_ahead"](pool)
            at.gpsimd(pool)

        @block.scalar
        def _(act):
            ld.scalar(act)
            pj.scalar(act)
            at.more["scalar_ahead"](act)
            at.scalar(act)

        @block.vector
        def _(dve):
            ld.vector(dve)
            pj.more["vector_norm"](dve, [(sh.wq_in, 16 * 8)])
            ld.more["vector_mod"](dve)
            ld.more["vector_late"](dve)
            pj.vector(dve)
            at.more["vector_ahead"](dve)
            at.vector(dve)

        @block.tensor
        def _(pe):
            ld.tensor(pe)
            pj.tensor(pe)
            at.more["tensor_ahead"](pe)
            at.tensor(pe)


def self_attention(nc, sh, ins):
    with ExitStack() as ctx:
        sems = ctx.enter_context(Semaphores(nc))
        md = modulate_second(nc, sh, ctx, sems, ins)
        stack = Room(sh.k_space)
        pj = project(nc, sh, ctx, sems, "p1", 1e-6, modulation(sh, 5), modulation(sh, 4), sh.wqkv1, sh.bcol[:, 2, :], True,
                     {n: stack for n in ("full", "rest", "part")},
                     scalar_first=[(sh.mod1_done, 4 * CH)], k_first=[(md.more["gate_psum"], 1)],
                     v_first=[(sh.mod1_done, 4 * CH), (md.more["gates_ready"], 2)])
        sh.pad_set = sems.new("pad_set")
        at = attend(nc, sh, ctx, sems, "a1", False, False, None, None, 2, sh.wo1, 3, 0, pj, {
            "tensor": pj.more["banks_read"], "gpsimd": pj.more["x_read"] + [(sh.gate_in, 32)],
            "sync": pj.more["banks_read"] + [(sh.pad_set, 3)]})
        block = ctx.enter_context(nc.Block())

        @block.sync
        def _(sp):
            md.sync(sp)
            pj.sync(sp)
            at.sync(sp)

        @block.gpsimd
        def _(pool):
            pj.gpsimd(pool)
            pool.wait_ge(md.more["gate_psum"], 1)
            pool.memset(sh.k_all[:, :, B * T:], 0.0).then_inc(sh.pad_set, 1)
            pool.memset(sh.v_all[:, :, :, D:D + 1], 1.0).then_inc(sh.pad_set, 1)
            pool.wait_ge(sh.pad_set, 2)
            pool.memset(sh.k_all[96:AUG, :, :], 1.0).then_inc(sh.pad_set, 1)
            pool.wait_ge(sh.pad_set, 3)
            at.gpsimd(pool)

        @block.scalar
        def _(act):
            pj.scalar(act)
            at.scalar(act)

        @block.vector
        def _(dve):
            pj.more["vector_norm"](dve)
            md.vector(dve)
            pj.vector(dve)
            at.vector(dve)

        @block.tensor
        def _(pe):
            md.tensor(pe)
            pj.tensor(pe)
            pe.wait_ge(sh.pad_set, 3)
            at.tensor(pe)


def cross_attention(nc, sh, ins):
    with ExitStack() as ctx:
        sems = ctx.enter_context(Semaphores(nc))
        mlp_in = sems.new("mlp_in")
        pj = project(nc, sh, ctx, sems, "p2", 1e-6, lambda c, b: sh.bcol[:, 4, c:c + 1], lambda c, b: sh.bcol[:, 5, c:c + 1],
                     sh.wq2, sh.bcol[:, 6, :], False, {"xn": Room(sh.v_space), "xt": Room(sh.gate_space[0])})
        at = attend(nc, sh, ctx, sems, "a2", True, False, sh.wkv2, sh.bcol[:, 7, :], 4, sh.wo2, 5, None, pj, {
            "tensor": pj.more["banks_read"], "gpsimd": pj.more["x_read"], "sync": []}, {"tensor": [], "scalar": [], "vector": []})
        block = ctx.enter_context(nc.Block())

        @block.sync
        def _(sp):
            sp.dma_start(sh.w1, ins["L1_xcond_mlp_w1"].rearrange("(k p) n -> p k n", p=P)).then_inc(mlp_in, 16)
            sp.dma_start(sh.w2, ins["L1_xcond_mlp_w2"].rearrange("(k p) n -> p k n", p=P)).then_inc(mlp_in, 16)
            at.more["sync_ahead"](sp)
            pj.sync(sp)
            at.sync(sp)
            sp.wait_ge(mlp_in, 32)

        @block.gpsimd
        def _(pool):
            at.more["gpsimd_pads"](pool)
            pj.gpsimd(pool)
            at.more["gpsimd_ahead"](pool)
            at.more["gpsimd_ones"](pool, behind=CH - 1)
            at.gpsimd(pool)

        @block.scalar
        def _(act):
            at.more["scalar_ahead"](act)
            pj.scalar(act)
            at.scalar(act)

        @block.vector
        def _(dve):
            at.more["vector_ahead"](dve)
            pj.more["vector_norm"](dve)
            pj.vector(dve)
            at.vector(dve)

        @block.tensor
        def _(pe):
            at.more["tensor_ahead"](pe)
            pj.tensor(pe)
            at.tensor(pe)


def build(nc, ins, out):
    dram = {
        "q_parts": nc.dram_tensor("q_parts", (B // QUAD, 3, CH, P, QUAD * T), BF16, kind="Internal").ap(),
        "k_parts": nc.dram_tensor("k_parts", (B // QUAD, 3, CH, P, QUAD * T), BF16, kind="Internal").ap(),
        "gate": nc.dram_tensor("gate_rows", (B, 2, C), F32, kind="Internal").ap(),
    }
    with ExitStack() as ctx:
        sh = allocate(nc, ctx, dram)
        first_layer(nc, sh, ins)
        self_attention(nc, sh, ins)
        cross_attention(nc, sh, ins)
        phase_mlp(nc, sh, ins, out)


_OUT = ((B, T, C), "float32")


def kernel(**inputs):
    import numpy as _np
    import concourse.bacc as _bacc
    from concourse import mybir as _mybir
    from concourse.bass_utils import run_bass_kernel_spmd as _run

    nc = _bacc.Bacc("TRN2", target_bir_lowering=False, num_devices=1)
    arrays, ins = {}, {}
    for name, value in inputs.items():
        a = _np.ascontiguousarray(value)
        arrays[f"in_{name}_dram"] = a
        ins[name] = nc.dram_tensor(f"in_{name}_dram", a.shape, _mybir.dt.from_np(a.dtype), kind="ExternalInput").ap()
    out = nc.dram_tensor("out_0_dram", _OUT[0], _mybir.dt.from_np(_np.dtype(_OUT[1])), kind="ExternalOutput").ap()
    build(nc, ins, out)
    r = _run(nc, [arrays], core_ids=[0])
    return r.results[0]["out_0_dram"]
```

```python
from contextlib import ExitStack

import numpy as np

import concourse.bass as bass
from concourse import mybir

F32 = mybir.dt.float32
BF16 = mybir.dt.bfloat16
ALU = mybir.AluOpType
ACT = mybir.ActivationFunctionType
AX_X = mybir.AxisListType.X

P = 128
B, T, L, C = 8, 112, 375, 256
H, D = 16, 16
CH = C // P
HC = P // D
HID = 4 * C
KEYS = [min(P, L - k) for k in range(0, L, P)]
NT = len(KEYS)
PAIRS = B // 2
SCALE = float(D) ** -0.5

TERMS_K = [0, 1, 0, 1, 2, 0]
TERMS_Q = [0, 0, 1, 1, 0, 2]
NTERM = len(TERMS_K)
WIDE = B * T + P - T
QUAD = 4
DEEP = NTERM * D
AUG = DEEP + 3

MODS = [("q_scale", 1.0), ("q_bias", 0.0), ("kv_scale", 1.0), ("kv_bias", 0.0),
        ("shift_msa", 0.0), ("scale_msa", 1.0), ("shift_mlp", 0.0), ("scale_mlp", 1.0)]


def wait(eng, sem, count):
    if isinstance(count, int) and count <= 0:
        return
    eng.wait_ge(sem, count)


def wait_all(eng, pairs):
    for sem, count in pairs:
        eng.wait_ge(sem, count)


class Parts:

    def __init__(self, tensor, vector, scalar, gpsimd, sync, **more):
        self.tensor, self.vector, self.scalar, self.gpsimd, self.sync = tensor, vector, scalar, gpsimd, sync
        self.more = more


class Room:

    def __init__(self, space):
        self.space, self.at = space, 0

    def take(self, shape, dt=F32):
        words = int(np.prod(shape[1:])) * (2 if dt == BF16 else 4) // 4
        view = self.space[0:shape[0], self.at:self.at + words]
        self.at += words
        if dt == BF16:
            view = view.bitcast(BF16)
        names = "abcd"[:len(shape) - 1]
        if len(names) == 1:
            return view
        return view.rearrange(f"p ({' '.join(names)}) -> p {' '.join(names)}", **dict(zip(names[1:], shape[2:])))


class Semaphores:

    def __init__(self, nc):
        self.nc, self.all = nc, []

    def new(self, name):
        self.all.append(self.nc.alloc_semaphore(name))
        return self.all[-1]

    def __enter__(self):
        return self

    def __exit__(self, *_):
        self.nc.clear_and_free_semaphores(self.all)
        self.nc.all_engine_barrier()


class Shared:
    pass


def allocate(nc, ctx, dram):
    sh = Shared()

    def sb(name, shape, dt=F32):
        return ctx.enter_context(nc.sbuf_tensor(name, shape, dt))

    sh.dram = dram
    sh.bank = [ctx.enter_context(nc.psum_tensor(f"bank{i}", [P, 512], F32)) for i in range(8)]
    sh.ident = sb("ident", [P, P])
    sh.ident_bf = sb("ident_bf", [P, P], BF16)
    sh.x = sb("x_tokens", [T, B, C])
    sh.ctx = sb("ctx_tokens", [P, B, NT, C])
    sh.ctx_mean = sb("ctx_mean", [P, B, NT])
    sh.ctx_rstd = sb("ctx_rstd", [P, B, NT])
    sh.silu_t = sb("silu_t", [P, CH, B])
    sh.mod = sb("mod", [P, len(MODS), CH, B])
    gates = [sb(f"gate{g}", [P, B * C]) for g in range(2)]
    sh.gate_space = gates
    sh.gate = [g[0:T, :].rearrange("t (b c) -> t b c", c=C) for g in gates]
    sh.wq0 = sb("wq0", [P, CH, C])
    sh.wkv0 = sb("wkv0", [P, CH, 2 * C])
    sh.wo0 = sb("wo0", [P, CH, C])
    sh.wqkv1 = sb("wqkv1", [P, CH, 3 * C])
    sh.wo1 = sb("wo1", [P, CH, C])
    sh.wq2 = sb("wq2", [P, CH, C])
    sh.wkv2 = sb("wkv2", [P, CH, 2 * C])
    sh.wo2 = sb("wo2", [P, CH, C])
    sh.bcol = sb("bias_columns", [P, 8, CH])
    sh.bhid = sb("bias_hidden", [P, HID // P])
    sh.brow = sb("bias_rows", [P, 7, C])
    sh.q_all = sb("q_stack_all", [AUG, H, WIDE], BF16)
    k_space = sb("k_stack_all", [P, H, WIDE], BF16)
    sh.k_all = k_space[0:AUG]
    mod_w = k_space[:, :, :].rearrange("p h n -> p (h n)").bitcast(F32)
    sh.wss = mod_w[:, 0:CH * 4 * C].rearrange("p (k n) -> p k n", k=CH)
    sh.ctx_t = [mod_w[:, i * CH * L:(i + 1) * CH * L].rearrange("p (c n) -> p c n", c=CH) for i in range(4)]
    at = 4 * CH * L
    sh.w1 = mod_w[:, at:at + CH * HID].rearrange("p (k n) -> p k n", k=CH)
    sh.w2 = mod_w[:, at + CH * HID:at + 2 * CH * HID].rearrange("p (k n) -> p k n", n=C)
    sh.wada = mod_w[:, at:at + CH * 6 * C].rearrange("p (k n) -> p k n", k=CH)
    sh.v_space = sb("v_all", [P, B * H * (D + 1)])
    sh.v_all = sh.v_space[0:T, :].rearrange("t (b h e) -> t b h e", b=B, h=H)
    sh.k_space = sb("k_stack", [P, 2 * H * NT * P // 2])
    stack = Room(sh.k_space)
    sh.k_st = [stack.take([AUG, H, NT * P], BF16) for i in range(2)]
    sh.v_sb = [sb(f"v_tokens{i}", [P, NT, H, D + 1]) for i in range(2)]
    return sh


BIAS_COLS = ["bq0", "bk0", "bq1", "bk1", "g2", "b2", "bq2", "bk2"]
BIAS_ROWS = ["bv0", "bp0", "bv1", "bo1", "bv2", "bo2", "bmlp2"]


def load(nc, sh, ctx, sems, ins):
    def sb(name, shape, dt=F32):
        return ctx.enter_context(nc.sbuf_tensor(name, shape, dt))

    cond, e, den, sig, silu = (sb(n, [B, C]) for n in ("cond", "cond_exp", "cond_den", "cond_sig", "cond_silu"))
    stats = sb("ctx_stats", [P, B, NT, 6])
    mv = sb("ctx_mv", [P, B, NT, 2])
    veps = sb("ctx_veps", [P, B, NT])
    half = sb("ctx_half", [P, B, NT])
    bmod = sb("bmod0", [P, 4, CH])

    cond_in, ctx_zero, zeroed, ident_set, half_set = (
        sems.new(n) for n in ("cond_in", "ctx_zero", "zeroed", "ident_set", "half_set"))
    exp_done, silu_step, silu_ready, silu_t_psum, silu_t_ready, mod_psum = (
        sems.new(n) for n in ("exp_done", "silu_step", "silu_ready", "silu_t_psum", "silu_t_ready", "mod_psum"))
    stats_done, aggr_done, veps_done = (sems.new(n) for n in ("stats_done", "aggr_done", "veps_done"))
    sh.mod_in = sems.new("mod_in")
    sh.x_in = sems.new("x_in")
    sh.wq_in = sems.new("wq_in")
    sh.ctx_in = sems.new("ctx_in")
    sh.w_in = sems.new("w_in")
    sh.ada_in = sems.new("ada_in")
    sh.late_in = sems.new("late_in")
    sh.mod_done = sems.new("mod_done")
    sh.ctx_stats_done = sems.new("ctx_stats_done")
    sh.consts_done = sems.new("consts_done")

    def chunks(w):
        return w.rearrange("(k p) n -> p k n", p=P)

    def col(v):
        return v.rearrange("(k p) -> p k", p=P)

    def sync(sp):
        sp.dma_start(cond[:, :], ins["cond_1024"]).then_inc(cond_in, 16)
        sp.dma_start(sh.wss[:, :, 0:2 * C], chunks(ins["L0_xcond_Wss_q"])).then_inc(sh.mod_in, 16)
        sp.dma_start(sh.x[:, 0:QUAD, :], ins["x"][0:QUAD].rearrange("b n c -> n b c")).then_inc(sh.x_in, 16)
        sp.dma_start(sh.x[:, QUAD:B, :], ins["x"][QUAD:B].rearrange("b n c -> n b c")).then_inc(sh.x_in, 16)
        sp.dma_start(sh.wss[:, :, 2 * C:4 * C], chunks(ins["L0_xcond_Wss_kv"])).then_inc(sh.mod_in, 16)
        with nc.allow_non_contiguous_dma(reason="biases, a few KB in all"):
            for m, v in enumerate([ins["L0_xcond_bss_q"][0:C], ins["L0_xcond_bss_q"][C:2 * C],
                                   ins["L0_xcond_bss_kv"][0:C], ins["L0_xcond_bss_kv"][C:2 * C]]):
                sp.dma_start(bmod[:, m, :], col(v)).then_inc(sh.mod_in, 16)
            sp.dma_start(sh.wq0[:, :, :], chunks(ins["L0_xcond_Wq"])).then_inc(sh.wq_in, 16)
            for n, v in (("bq0", ins["L0_xcond_bq"]), ("bq1", ins["L1_xcond_qkv_b"][0:C]), ("bk1", ins["L1_xcond_qkv_b"][C:2 * C]),
                         ("g2", ins["L1_xcond_norm2_g"]), ("b2", ins["L1_xcond_norm2_b"]), ("bq2", ins["L1_xcond_q_b"])):
                sp.dma_start(sh.bcol[:, BIAS_COLS.index(n), :], col(v)).then_inc(sh.wq_in, 16)
            sp.dma_start(sh.bhid[:, :], col(ins["L1_xcond_mlp_b1"])).then_inc(sh.wq_in, 16)
        sp.wait_ge(ctx_zero, 1)
        for t, rows in enumerate(KEYS):
            sp.dma_start(sh.ctx[0:rows, :, t, :],
                         ins["ctx_1024"][:, t * P:t * P + rows, :].rearrange("b p c -> p b c")).then_inc(sh.ctx_in, 16)
        sp.dma_start(sh.wkv0[:, :, :], chunks(ins["L0_xcond_Wkv"])).then_inc(sh.w_in, 16)
        sp.dma_start(sh.wo0[:, :, :], chunks(ins["L0_xcond_Wp"])).then_inc(sh.w_in, 16)
        for i, v in enumerate([ins["L0_xcond_bkv"][C:2 * C], ins["L0_xcond_bp"], ins["L1_xcond_qkv_b"][2 * C:3 * C],
                               ins["L1_xcond_self_o_b"], ins["L1_xcond_kv_b"][C:2 * C], ins["L1_xcond_cross_o_b"],
                               ins["L1_xcond_mlp_b2"]]):
            sp.dma_start(sh.brow[:, i, :], v.partition_broadcast(P)).then_inc(sh.w_in, 16)
        with nc.allow_non_contiguous_dma(reason="biases, a few KB in all"):
            for n, v in (("bk0", ins["L0_xcond_bkv"]), ("bk2", ins["L1_xcond_kv_b"])):
                for k in range(CH):
                    sp.dma_start(sh.bcol[:, BIAS_COLS.index(n), k:k + 1],
                                 v[k * P:(k + 1) * P].rearrange("(h d) -> d h", d=D)).then_inc(sh.w_in, 16)
        sp.dma_start(sh.wada, chunks(ins["L1_xcond_ada_w"])).then_inc(sh.ada_in, 16)
        for w, name in ((sh.wqkv1, "L1_xcond_qkv_w"), (sh.wo1, "L1_xcond_self_o_w"),
                        (sh.wq2, "L1_xcond_q_w"), (sh.wkv2, "L1_xcond_kv_w"), (sh.wo2, "L1_xcond_cross_o_w")):
            sp.dma_start(w[:, :, :], chunks(ins[name])).then_inc(sh.late_in, 16)

    def gpsimd(pool):
        pool.memset(sh.ident[:, :], 0.0).then_inc(zeroed, 1)
        pool.memset(sh.ident_bf[:, :], 0.0).then_inc(zeroed, 1)
        pool.wait_ge(zeroed, 2)
        for m in (sh.ident, sh.ident_bf):
            pool.affine_select(out=m[:, :], in_=m[:, :], compare_op=ALU.not_equal, fill=1.0,
                               base=0, pattern=[[-1, P]], channel_multiplier=1).then_inc(ident_set, 1)
        pool.memset(half[:, :, :], -0.5).then_inc(half_set, 1)

    def gpsimd_late(pool):
        for s in range(2):
            pool.memset(sh.v_sb[s][:, :, :, D:D + 1], 1.0).then_inc(sh.consts_done, 1)
        pool.memset(sh.q_all[:, :, B * T:], 0.0).then_inc(sh.consts_done, 1)
        pool.wait_ge(half_set, 1)
        pool.wait_ge(veps_done, 1)
        pool.tensor_tensor(sh.ctx_rstd[:, :, :], veps[:, :, :], half[:, :, :], ALU.pow).then_inc(sh.ctx_stats_done, 1)

    def scalar(act):
        act.wait_ge(cond_in, 16)
        act.activation(e[:, :], cond[:, :], ACT.Exp, scale=-1.0).then_inc(exp_done, 1)

    def vector(dve):
        dve.memset(sh.ctx[96:P, :, NT - 1, :], 0.0).then_inc(ctx_zero, 1)
        dve.wait_ge(exp_done, 1)
        dve.tensor_scalar(den[:, :], e[:, :], 1.0, None, ALU.add).then_inc(silu_step, 1)
        dve.wait_ge(silu_step, 1)
        dve.reciprocal(sig[:, :], den[:, :]).then_inc(silu_step, 1)
        dve.wait_ge(silu_step, 2)
        dve.tensor_tensor(silu[:, :], cond[:, :], sig[:, :], ALU.mult).then_inc(silu_ready, 1)
        dve.wait_ge(silu_t_psum, 1)
        dve.tensor_copy(sh.silu_t[:, :, :], sh.bank[6][:, 0:CH * B].rearrange("p (k b) -> p k b", b=B)).then_inc(silu_t_ready, 1)

    def vector_mod(dve):
        dve.wait_ge(mod_psum, 1)
        mp = sh.bank[7][:, 0:4 * CH * B].rearrange("p (m k b) -> p m k b", k=CH, b=B)
        for m in range(4):
            for k in range(CH):
                dve.tensor_scalar(sh.mod[:, m, k, :], mp[:, m, k, :], bmod[:, m, k:k + 1], MODS[m][1], ALU.add, ALU.add).then_inc(sh.mod_done, 1)

    def vector_late(dve):
        dve.memset(sh.bank[4][:, :], 0.0).then_inc(sh.consts_done, 1)
        dve.wait_ge(sh.ctx_in, 16 * NT)
        for b in range(B):
            for t in range(NT):
                dve.bn_stats(stats[:, b, t, :], sh.ctx[:, b, t, :]).then_inc(stats_done, 1)
        dve.wait_ge(stats_done, B * NT)
        for b in range(B):
            for t in range(NT):
                dve.bn_aggr(mv[:, b, t, :], stats[:, b, t, :]).then_inc(aggr_done, 1)
        dve.wait_ge(aggr_done, B * NT)
        dve.tensor_scalar(veps[:, :, :], mv[:, :, :, 1], 1e-5, None, ALU.add).then_inc(veps_done, 1)
        dve.tensor_copy(sh.ctx_mean[:, :, :], mv[:, :, :, 0]).then_inc(sh.ctx_stats_done, 1)

    def tensor(pe):
        pe.wait_ge(silu_ready, 1)
        pe.wait_ge(ident_set, 2)
        for k in range(CH):
            last = pe.transpose(sh.bank[6][:, k * B:(k + 1) * B], silu[:, k * P:(k + 1) * P], sh.ident[0:B, 0:B])
        last.then_inc(silu_t_psum, 1)
        pe.wait_ge(silu_t_ready, 1)
        pe.wait_ge(sh.mod_in, 16 * 6)
        for m in range(4):
            for k in range(CH):
                o = (m * CH + k) * B
                for kk in range(CH):
                    last = pe.matmul(sh.bank[7][:, o:o + B], sh.wss[:, kk, m * C + k * P:m * C + (k + 1) * P],
                                     sh.silu_t[:, kk, :], start=kk == 0, stop=kk == CH - 1)
        last.then_inc(mod_psum, 1)

    return Parts(tensor, vector, scalar, gpsimd, sync, gpsimd_late=gpsimd_late, vector_mod=vector_mod, vector_late=vector_late)


def modulate_second(nc, sh, ctx, sems, ins):
    def sb(name, shape, dt=F32):
        return ctx.enter_context(nc.sbuf_tensor(name, shape, dt))

    bmod = sb("bmod1", [P, 4, CH])
    bgate = sb("bgate", [B, 2, C])
    gates = sb("gates", [B, 2, C])
    bias_in, mod_psum, gate_psum, gates_ready, gate_dram = (
        sems.new(n) for n in ("ada_bias_in", "ada_mod_psum", "gate_psum", "gates_ready", "gate_dram"))
    mod1_done = sems.new("mod1_done")
    ada_b = ins["L1_xcond_ada_b"]
    part_at = [0, C, 3 * C, 4 * C]
    gate_at = [2 * C, 5 * C]

    def sync(sp):
        with nc.allow_non_contiguous_dma(reason="biases, a few KB in all"):
            for m, at in enumerate(part_at):
                sp.dma_start(bmod[:, m, :], ada_b[at:at + C].rearrange("(k p) -> p k", p=P)).then_inc(bias_in, 16)
            for g, at in enumerate(gate_at):
                sp.dma_start(bgate[:, g, :], ada_b[at:at + C].partition_broadcast(B)).then_inc(bias_in, 16)

    def sync_gates(sp):
        sp.wait_ge(gates_ready, 2)
        sp.dma_start(sh.dram["gate"], gates[:, :, :]).then_inc(gate_dram, 16)

    def vector(dve):
        dve.wait_ge(bias_in, 16 * 6)
        dve.wait_ge(mod_psum, 1)
        mp = sh.bank[6][:, 0:4 * CH * B].rearrange("p (m k b) -> p m k b", k=CH, b=B)
        for m in range(4):
            for k in range(CH):
                dve.tensor_scalar(sh.mod[:, 4 + m, k, :], mp[:, m, k, :], bmod[:, m, k:k + 1], MODS[4 + m][1], ALU.add, ALU.add).then_inc(mod1_done, 1)
        dve.wait_ge(gate_psum, 1)
        for g in range(2):
            dve.tensor_tensor(gates[:, g, :], sh.bank[7][0:B, g * C:(g + 1) * C], bgate[:, g, :], ALU.add).then_inc(gates_ready, 1)

    def tensor(pe):
        pe.wait_ge(sh.ada_in, 16)
        for m in range(4):
            for k in range(CH):
                o = (m * CH + k) * B
                for kk in range(CH):
                    last = pe.matmul(sh.bank[6][:, o:o + B], sh.wada[:, kk, part_at[m] + k * P:part_at[m] + (k + 1) * P],
                                     sh.silu_t[:, kk, :], start=kk == 0, stop=kk == CH - 1)
        last.then_inc(mod_psum, 1)
        for g in range(2):
            for kk in range(CH):
                last = pe.matmul(sh.bank[7][0:B, g * C:(g + 1) * C], sh.silu_t[:, kk, :],
                                 sh.wada[:, kk, gate_at[g]:gate_at[g] + C], start=kk == 0, stop=kk == CH - 1)
        last.then_inc(gate_psum, 1)

    return Parts(tensor, vector, None, None, sync, sync_gates=sync_gates, gate_dram=gate_dram,
                 banks_read=[(mod1_done, 4 * CH), (gates_ready, 2)])


def project(nc, sh, ctx, sems, name, eps, scale_of, bias_of, wq, bq, qkv, rooms, tensor_first=(), mod_first=(), bank_first=()):
    N4 = QUAD * T
    QUADS = B // QUAD

    def sb(n, shape, dt=F32):
        return ctx.enter_context(nc.sbuf_tensor(f"{name}_{n}", shape, dt))

    def sem(n):
        return sems.new(f"{name}_{n}")

    stats, mv = sb("stats", [T, B, 6]), sb("mv", [T, B, 2])
    veps, half, rstd = (sb(n, [T, B]) for n in ("veps", "half", "rstd"))
    def place(n, shape, dt=F32):
        room = rooms.get(n.split("_")[-1].rstrip("01"))
        return room.take(shape, dt) if room else sb(n, shape, dt)

    xn = place("xn", [T, B, C])
    xt = [place(f"xt{i}", [P, CH, N4]) for i in range(QUADS)]
    kinds = ["q", "k"] if qkv else ["q"]
    NK = len(kinds)
    full = {k: place(f"{k}_full", [P, CH, N4]) for k in kinds}
    rest = place("rest", [P, CH, N4])
    part = {k: place(f"{k}_part", [P, 3, CH, N4], BF16) for k in kinds}
    qb = sb("qb", [P, CH])
    half_set, qb_set, stats_done, aggr_done, veps_done, rstd_done, xn_done = (
        sem(n) for n in ("half_set", "qb_set", "stats_done", "aggr_done", "veps_done", "rstd_done", "xn_done"))
    xt_done = [sem(f"xt_done{c}") for c in range(CH)]
    xt_psum, proj_psum, v_psum, full_done, v_done, split = (
        sem(n) for n in ("xt_psum", "proj_psum", "v_psum", "full_done", "v_done", "split"))
    written = sem("written")
    stacked = [sem(f"stacked{i}") for i in range(QUADS)]
    all_of = {"q": sh.q_all, "k": sh.k_all}

    def xt_bank(i, c):
        return sh.bank[6 * i + c]

    banks_of = {"q": sh.bank[2:4], "k": sh.bank[4:6]}
    bias_col = {"q": qb, "k": sh.bcol[:, 3, :]}
    terms = {"q": TERMS_Q, "k": TERMS_K}

    def vector_norm(dve, first=()):
        wait_all(dve, first)
        for i in range(QUADS):
            quad = slice(QUAD * i, QUAD * (i + 1))
            for b in range(B)[quad]:
                dve.bn_stats(stats[:, b, :], sh.x[:, b, :]).then_inc(stats_done, 1)
            dve.wait_ge(stats_done, QUAD * (i + 1))
            for b in range(B)[quad]:
                dve.bn_aggr(mv[:, b, :], stats[:, b, :]).then_inc(aggr_done, 1)
            dve.wait_ge(aggr_done, QUAD * (i + 1))
            dve.tensor_scalar(veps[:, quad], mv[:, quad, 1], eps, None, ALU.add).then_inc(veps_done, 1)
        dve.tensor_scalar(qb[:, :], bq, SCALE, None, ALU.mult).then_inc(qb_set, 1)
        for b in range(B):
            if b % QUAD == 0:
                dve.wait_ge(rstd_done, b // QUAD + 1)
            dve.tensor_scalar(xn[:, b, :], sh.x[:, b, :], mv[:, b, 0:1], rstd[:, b:b + 1],
                              ALU.subtract, ALU.mult).then_inc(xn_done, 1)

    def vector_modulate(dve):
        c = CH - 1
        wait_all(dve, mod_first)
        for b in range(B):
            i, j = b // QUAD, b % QUAD
            dve.wait_ge(xt_psum, CH * i + c + 1)
            dve.tensor_scalar(xt[i][:, c, j * T:(j + 1) * T], xt_bank(i, c)[:, j * T:(j + 1) * T], scale_of(c, b), bias_of(c, b),
                              ALU.mult, ALU.add).then_inc(xt_done[c], 1)

    def vector(dve, quads=range(QUADS)):
        for i in quads:
            for n, k in enumerate(kinds):
                at = NK * i + n
                dve.wait_ge(full_done, CH * (at + 1))
                wait(dve, written, 16 * (at - NK + 1))
                dve.tensor_copy(part[k][:, 0, :, :], full[k][:, :, :]).then_inc(split, 1)
                dve.wait_ge(split, 4 * at + 1)
                dve.tensor_tensor(rest[:, :, :], full[k][:, :, :], part[k][:, 0, :, :], ALU.subtract).then_inc(split, 1)
                dve.wait_ge(split, 4 * at + 2)
                dve.tensor_copy(part[k][:, 1, :, :], rest[:, :, :]).then_inc(split, 1)
                dve.wait_ge(split, 4 * at + 3)
                dve.tensor_tensor(part[k][:, 2, :, :], rest[:, :, :], part[k][:, 1, :, :], ALU.subtract).then_inc(split, 1)
            if qkv:
                for j in range(0, QUAD, 2):
                    n = 2 * i + j // 2
                    dve.wait_ge(v_psum, n + 1)
                    b = QUAD * i + j
                    dve.tensor_tensor(sh.v_all[:, b:b + 2, :, 0:D],
                                      sh.bank[6 + j // 2][0:T, :].rearrange("t (j h d) -> t j h d", j=2, d=D),
                                      sh.brow[0:T, 2:3, :].rearrange("t o (h d) -> t o h d", d=D).broadcast_to([T, 2, H, D]),
                                      ALU.add).then_inc(v_done, 1)

    def gpsimd(pool):
        pool.memset(half[:, :], -0.5).then_inc(half_set, 1)
        pool.wait_ge(half_set, 1)
        for i in range(QUADS):
            quad = slice(QUAD * i, QUAD * (i + 1))
            pool.wait_ge(veps_done, i + 1)
            pool.tensor_tensor(rstd[:, quad], veps[:, quad], half[:, quad], ALU.pow).then_inc(rstd_done, 1)

    def scalar(act):
        act.wait_ge(qb_set, 1)
        wait_all(act, mod_first)
        for i in range(QUADS):
            act.wait_ge(xt_psum, CH * i + 1)
            for j in range(QUAD):
                b = QUAD * i + j
                act.activation(xt[i][:, 0, j * T:(j + 1) * T], xt_bank(i, 0)[:, j * T:(j + 1) * T], ACT.Identity,
                               bias=bias_of(0, b), scale=scale_of(0, b)).then_inc(xt_done[0], 1)
        for i in range(QUADS):
            for n, k in enumerate(kinds):
                at = NK * i + n
                wait(act, split, 4 * (at - NK + 1))
                for m in range(CH):
                    act.wait_ge(proj_psum, CH * at + m + 1)
                    act.activation(full[k][:, m, :], banks_of[k][m][:, 0:N4], ACT.Identity,
                                   bias=bias_col[k][:, m:m + 1], scale=SCALE if k == "q" else 1.0).then_inc(full_done, 1)

    def tensor(pe):
        for i in range(QUADS):
            pe.wait_ge(xn_done, QUAD * (i + 1))
            if i == 1:
                wait_all(pe, bank_first)
            for c in range(CH):
                for j in range(QUAD):
                    last = pe.transpose(xt_bank(i, c)[:, j * T:(j + 1) * T], xn[:, QUAD * i + j, c * P:(c + 1) * P], sh.ident[0:T, 0:T])
                last.then_inc(xt_psum, 1)
        wait_all(pe, tensor_first)
        for i in range(QUADS):
            for c in range(CH):
                pe.wait_ge(xt_done[c], QUAD * (i + 1))
            for n, k in enumerate(kinds):
                for m in range(CH):
                    wait(pe, full_done, CH * (NK * (i - 1) + n) + m + 1)
                    for c in range(CH):
                        last = pe.matmul(banks_of[k][m][:, 0:N4], wq[:, c, n * C + m * P:n * C + (m + 1) * P], xt[i][:, c, :],
                                         start=c == 0, stop=c == CH - 1)
                    last.then_inc(proj_psum, 1)
            if qkv:
                if i == 0:
                    for c in range(CH):
                        pe.wait_ge(xt_done[c], QUAD * QUADS)
                for j in range(0, QUAD, 2):
                    wait(pe, v_done, 2 * (i - 1) + j // 2 + 1)
                    for jj in (j, j + 1):
                        for c in range(CH):
                            last = pe.matmul(sh.bank[6 + j // 2][0:T, (jj - j) * C:(jj - j + 1) * C], xt[i][:, c, jj * T:(jj + 1) * T],
                                             wq[:, c, 2 * C:3 * C], start=c == 0, stop=c == CH - 1)
                    last.then_inc(v_psum, 1)

    def sync(sp):
        for i in range(QUADS):
            for n, k in enumerate(kinds):
                at = NK * i + n
                sp.wait_ge(split, 4 * (at + 1))
                d = sh.dram[f"{k}_parts"]
                sp.dma_start(d[i].rearrange("t c p n -> p t c n"), part[k][:, :, :, :]).then_inc(written, 16)
                sp.wait_ge(written, 16 * (at + 1))
                for t, w in enumerate(terms[k]):
                    sp.dma_start(all_of[k][t * D:(t + 1) * D, :, i * N4:(i + 1) * N4],
                                 d[i, w].rearrange("c (h d) n -> d (c h) n", d=D)).then_inc(stacked[i], 16)

    return Parts(tensor, vector, scalar, gpsimd, sync, vector_norm=vector_norm, vector_modulate=vector_modulate,
                 stacked=stacked, stacked_count=16 * NTERM * NK,
                 banks_read=[(full_done, CH * NK * QUADS)] + ([(v_done, 2 * QUADS)] if qkv else []),
                 x_read=[(xn_done, B)])


def attend(nc, sh, ctx, sems, name, cross, ln, wkv, bk, bv_row, wo, bo_row, gate, stacks, first, ahead=None):
    keys = KEYS if cross else [T]
    nt = len(keys)
    GH = 4
    NG = H // GH
    NU = NG * nt
    HS = 1 if cross else 4
    NS = H // HS
    LAG = 1 if cross else 2
    S_AT = [0, 3, 6, 8, 11, 14, 16, 16, 16, 16, 16, 16, 16, 16] if cross else [0, 2, 4, 4, 4, 4]
    K0, K1, V0, V1, T0, T1 = range(6)
    FILL_AT = {1: K0, 3: K1, 7: V0, 9: V1, 10: T0, 12: T1} if cross else {}
    MID_AT = {4: 0, 6: 1}
    LOAD_MAX_AT = 8
    MAX_AT = 7 if cross else 3
    TAIL_AT = {1: 0, 3: 1, 5: 2} if cross else {1: 0, 2: 1, 4: 2}

    def sb(n, shape, dt=F32):
        return ctx.enter_context(nc.sbuf_tensor(f"{name}_{n}", shape, dt))

    def sem(n):
        return sems.new(f"{name}_{n}")

    score, score_t, pv, cx, tb = [sh.bank[0], sh.bank[1], sh.bank[7]], [sh.bank[2], sh.bank[3]], sh.bank[4], sh.bank[5], sh.bank[6]
    nm_bank = (tb if cross else cx)[:, CH * T:CH * T + T // 2].bitcast(BF16)
    prob = [sb(f"prob{i}", [P, GH * T]) for i in range(2)]
    nmax, nrest, nparts = sb("nmax", [T, H]), sb("nrest", [T, H]), sb("nparts", [T, P // H, H], BF16)
    nm_t = [sb(f"nm_t{i}", [3 * H, T], BF16) for i in range(2)]
    pv_sb = sb("pv_sb", [P, NG * T])
    rden = sb("rden", [T, H])
    on = sb("on", [T, C])
    ot = sb("ot", [P, CH, T])
    if gate is not None:
        gated, bog = sb("gated", [T, C]), sb("bog", [T, C])
    if cross:
        xn = sb("xn", [P, NT, C])
        ct, kf, kr = sh.ctx_t[0:2], sh.ctx_t[2], sh.ctx_t[3]
        kp = [sb("kp", [P, 3, CH, L], BF16), Room(sh.v_space).take([P, 3, CH, L], BF16)]
    xn_done, fill_psum, fill_read, rest_done, mid_done = (
        sem(n) for n in ("xn_done", "fill_psum", "fill_read", "rest_done", "mid_done"))
    split = [sem(f"split{c}") for c in range(CH)]
    stacked = [[sem(f"stacked{s}{c}") for c in range(CH)] for s in range(2)]
    v_done, w_copied, w_ordered = sem("v_done"), sem("w_copied"), sem("w_ordered")
    v_loaded = [sem(f"v_loaded{s}") for s in range(2)]
    s_psum, max_done, nm_step, nm_psum, nm_done = (sem(n) for n in ("s_psum", "max_done", "nm_step", "nm_psum", "nm_done"))
    nparts_set, pad_set, ones_set = sem("nparts_set"), sem("pad_set"), sem("ones_set")
    nm_in = [sem(f"nm_in{s}") for s in range(2)]
    st_psum, exp_done, pv_psum, pv_read = (sem(n) for n in ("st_psum", "exp_done", "pv_psum", "pv_read"))
    tail1, rden_done, on_done, tail2, ot_done, tail3, tb_free, base_done, bog_done, gated_done = (
        sem(n) for n in ("tail1", "rden_done", "on_done", "tail2", "ot_done", "tail3", "tb_free", "base_done", "bog_done", "gated_done"))

    def has_fill(slot, k):
        b = slot + (2 if k in (K0, K1) else 1 if k in (V0, V1) else 3)
        return not isinstance(slot, int) or 0 <= b < B

    def fill_no(slot, k):
        if isinstance(slot, int):
            return sum(has_fill(s, j) for s in range(-3, slot) for j in range(6)) + sum(has_fill(slot, j) for j in range(k))
        return 6 * slot + 12 + k


    def pe_fill(pe, slot, k, par):
        wait(pe, fill_read, fill_no(slot, k))
        if k in (K0, K1):
            m = k - K0
            for c in range(CH):
                last = pe.matmul(cx[:, 0:L], wkv[:, c, m * P:(m + 1) * P], ct[par][:, c, :], start=c == 0, stop=c == CH - 1)
        elif k in (V0, V1):
            for t in ((0, 1) if k == V0 else (2,)):
                rows = keys[t]
                for c in range(CH):
                    last = pe.matmul(cx[0:rows, (t % 2) * C:(t % 2 + 1) * C], ct[1 - par][:, c, t * P:t * P + rows], wkv[:, c, C:2 * C],
                                     start=c == 0, stop=c == CH - 1)
        else:
            c = k - T0
            if c == 0:
                wait(pe, xn_done, NT * (slot + 4))
            for t, rows in enumerate(keys):
                last = pe.transpose(cx[:, t * P:t * P + rows], xn[0:rows, t, c * P:(c + 1) * P], sh.ident[0:rows, 0:rows])
        last.then_inc(fill_psum, 1)

    def pe_scores(pe, b, par, lo, hi, cnt):
        for i in range(lo, hi):
            if i == 0 and isinstance(b, int) and b == 0:
                pe.wait_ge(stacks.more["stacked"][0], stacks.more["stacked_count"])
            if cross and i == 0:
                pe.wait_ge(stacked[par][0], cnt * 16 * NTERM)
            if cross and i * HS == HC:
                pe.wait_ge(stacked[par][1], cnt * 16 * NTERM)
            wait(pe, max_done, NS * b + (i - 2 if i else 0))
            for h in range(i * HS, (i + 1) * HS):
                o = (h - i * HS) * T
                w = L if cross else T
                keys_h = sh.k_st[par][0:DEEP, h, 0:w] if cross else sh.k_all[0:DEEP, h, bass.ds(b * T, T)]
                last = pe.matmul(score[i % 3][:, o:o + w], sh.q_all[0:DEEP, h, bass.ds(b * T, P)], keys_h, start=True, stop=True)
            last.then_inc(s_psum, 1)

    def pe_max_t(pe, b):
        pe.wait_ge(nm_step, 4 * b + 4)
        wait(pe, nm_done, b)
        pe.transpose(nm_bank, nparts[:, :, :].rearrange("t a h -> t (a h)"),
                     sh.ident_bf[0:T, 0:T]).then_inc(nm_psum, 1)

    def pe_scores_t(pe, b, par, u, cnt):
        g, t = u // nt, u % nt
        if u == 0:
            pe.wait_ge(nm_in[par], 16 * cnt)
        wait(pe, exp_done, NU * b + u - 1)
        for j in range(GH):
            h = g * GH + j
            keys_h = sh.k_st[par][0:AUG, h, t * P:(t + 1) * P] if cross else sh.k_all[0:AUG, h, bass.ds(b * T, P)]
            last = pe.matmul(score_t[u % 2][:, j * T:(j + 1) * T], keys_h, sh.q_all[0:AUG, h, bass.ds(b * T, T)],
                             start=True, stop=True)
        last.then_inc(st_psum, 1)

    def pe_values(pe, b, par, u, cnt):
        g, t = u // nt, u % nt
        if u == 0:
            wait(pe, pv_read, b)
            if cross:
                pe.wait_ge(v_done, NT * (b + 1))
            else:
                pe.wait_ge(v_loaded[par], 16 * cnt)
        pe.wait_ge(exp_done, NU * b + u + 1)
        rows = keys[t]
        for j in range(GH):
            h = g * GH + j
            last = pe.matmul(pv[32 * j:32 * j + D + 1, g * T:(g + 1) * T], sh.v_sb[par][0:rows, t, h, :],
                             prob[u % 2][0:rows, j * T:(j + 1) * T], start=t == 0, stop=t == nt - 1)
        last.then_inc(pv_psum, 1)

    def pe_tail(pe, b, step):
        if step == 0:
            pe.wait_ge(pv_read, b + 1)
            pe.wait_ge(tb_free, b + 1)
            if cross:
                pe.wait_ge(nm_done, min(b + 2, B) if isinstance(b, int) else b + 2)
            for g in range(NG):
                last = pe.transpose(tb[0:T, g * P:(g + 1) * P], pv_sb[:, g * T:(g + 1) * T], sh.ident[:, :])
            last.then_inc(tail1, 1)
        elif step == 1:
            pe.wait_ge(on_done, b + 1)
            for c in range(CH):
                last = pe.transpose(tb[:, c * T:(c + 1) * T], on[:, c * P:(c + 1) * P], sh.ident[0:T, 0:T])
            last.then_inc(tail2, 1)
        else:
            pe.wait_ge(ot_done, b + 1)
            for c in range(CH):
                last = pe.matmul(tb[0:T, 0:C], ot[:, c, :], wo[:, c, :], start=c == 0, stop=c == CH - 1)
            last.then_inc(tail3, 1)

    def pe_slot(pe, b, par, cnt, has_e, has_s, has_tail):
        for u in range(NU + 1):
            if has_e and u < NU:
                pe_scores_t(pe, b, par, u, cnt[0])
            if has_tail and u in TAIL_AT:
                pe_tail(pe, b - 1, TAIL_AT[u])
            if u in FILL_AT and has_fill(b, FILL_AT[u]):
                pe_fill(pe, b, FILL_AT[u], par)
            if has_s:
                pe_scores(pe, b + LAG, (par + LAG) % 2, S_AT[u], S_AT[u + 1], cnt[1])
                if u == MAX_AT:
                    pe_max_t(pe, b + LAG)
            if has_e and u > 0:
                pe_values(pe, b, par, u - 1, cnt[0])

    def act_slot(act, b, par, cnt, has_e, has_s, has_tail):
        for u in range(NU + 1):
            if has_e and u < NU:
                rows = keys[u % nt]
                act.wait_ge(st_psum, NU * b + u + 1)
                wait(act, pv_psum, NU * b + u - 1)
                act.activation(prob[u % 2][0:rows, :], score_t[u % 2][0:rows, 0:GH * T], ACT.Exp).then_inc(exp_done, 1)
            if has_s and cross and u == LOAD_MAX_AT:
                load_max(act, b + LAG, (par + LAG) % 2)
            if has_tail and TAIL_AT.get(u) == 1:
                act.wait_ge(tail2, b)
                act.activation(ot[:, :, :], tb[:, 0:CH * T].rearrange("p (c n) -> p c n", c=CH), ACT.Copy).then_inc(ot_done, 1)
            if FILL_AT.get(u) in (K0, K1) and has_fill(b, K0):
                m = FILL_AT[u] - K0
                act.wait_ge(fill_psum, fill_no(b, K0 + m) + 1)
                act.activation(kf[:, m, :], cx[:, 0:L], ACT.Identity, bias=bk[:, m:m + 1])
                wait(act, stacked[par][m], 16 * NTERM * cnt[0])
                act.activation(kp[par][:, 0, m, :], cx[:, 0:L], ACT.Identity, bias=bk[:, m:m + 1]).then_inc(fill_read, 1)
            if cross and u in MID_AT and has_fill(b, K0):
                m = MID_AT[u]
                act.wait_ge(rest_done, CH * (b + 2) + m + 1)
                act.activation(kp[par][:, 1, m, :], kr[:, m, :], ACT.Copy).then_inc(mid_done, 1)
            if FILL_AT.get(u) in (V0, V1) and has_fill(b, V0):
                k = FILL_AT[u]
                act.wait_ge(fill_psum, fill_no(b, k) + 1)
                wait(act, pv_psum, NU * b)
                for t in ((0, 1) if k == V0 else (2,)):
                    rows = keys[t]
                    last = act.activation(sh.v_sb[1 - par][0:rows, t, :, 0:D],
                                          cx[0:rows, (t % 2) * C:(t % 2 + 1) * C].rearrange("p (h d) -> p h d", d=D), ACT.Copy)
                last.then_inc(fill_read, 1)
            if FILL_AT.get(u) in (T0, T1) and has_fill(b, T0):
                c = FILL_AT[u] - T0
                act.wait_ge(fill_psum, fill_no(b, T0 + c) + 1)
                if ln:
                    act.activation(ct[1 - par][:, c, :], cx[:, 0:L], ACT.Identity, bias=sh.mod[:, 3, c, bass.ds(b + 3, 1)],
                                   scale=sh.mod[:, 2, c, bass.ds(b + 3, 1)]).then_inc(fill_read, 1)
                else:
                    act.activation(ct[1 - par][:, c, :], cx[:, 0:L], ACT.Copy).then_inc(fill_read, 1)
        if has_e:
            act.wait_ge(pv_psum, NU * b + NU)
            wait(act, tail1, b)
            act.activation(pv_sb[:, :], pv[:, 0:NG * T], ACT.Copy).then_inc(pv_read, 1)

    def dve_norm_context(dve, b):
        if not isinstance(b, int) or b > 0:
            dve.wait_ge(fill_psum, fill_no(b - 4, T1) + 1)
        for t in range(NT):
            x_in = sh.ctx[:, bass.ds(b, 1), t, :]
            if ln:
                dve.tensor_scalar(xn[:, t, :], x_in, sh.ctx_mean[:, bass.ds(b, 1), t], sh.ctx_rstd[:, bass.ds(b, 1), t],
                                  ALU.subtract, ALU.mult).then_inc(xn_done, 1)
            else:
                dve.tensor_copy(xn[:, t, :], x_in).then_inc(xn_done, 1)

    def dve_slot(dve, b, par, cnt, has_s, has_tail, norm_next):
        for u in range(NU + 1):
            if has_tail and TAIL_AT.get(u) == 0:
                dve.wait_ge(tail1, b)
                tp = tb[0:T, :].rearrange("t (h e) -> t h e", e=32)
                dve.reciprocal(rden[:, :], tp[:, :, D]).then_inc(rden_done, 1)
                dve.wait_ge(rden_done, b)
                dve.tensor_tensor(on[:, :].rearrange("t (h d) -> t h d", d=D), tp[:, :, 0:D],
                                  rden[:, :].rearrange("t (h o) -> t h o", o=1).broadcast_to([T, H, D]), ALU.mult).then_inc(on_done, 1)
            if has_tail and TAIL_AT.get(u) == 2:
                xb = sh.x[:, bass.ds(b - 1, 1), :].rearrange("t o c -> t (o c)")
                dve.wait_ge(tail3, b)
                dve.wait_ge(base_done, b)
                if gate is None:
                    dve.tensor_tensor(xb, tb[0:T, 0:C], xb, ALU.add).then_inc(tb_free, 1)
                else:
                    dve.tensor_tensor(gated[:, :], tb[0:T, 0:C], sh.gate[gate][:, bass.ds(b - 1, 1), :].rearrange("t o c -> t (o c)"),
                                      ALU.mult).then_inc(gated_done, 1)
                    dve.wait_ge(gated_done, b)
                    dve.tensor_tensor(xb, gated[:, :], xb, ALU.add).then_inc(tb_free, 1)
            if has_s:
                n = b + LAG
                for i in range(S_AT[u], S_AT[u + 1]):
                    dve.wait_ge(s_psum, NS * n + i + 1)
                    if i == 0:
                        wait(dve, nm_step, 4 * n)
                    w = L if cross else T
                    dve.tensor_reduce(nmax[:, i * HS:(i + 1) * HS], score[i % 3][0:T, 0:HS * w].rearrange("t (h k) -> t h k", k=w),
                                      AX_X, ALU.max, negate=True).then_inc(max_done, 1)
            if has_s and u == MAX_AT:
                dve.wait_ge(max_done, NS * (n + 1))
                wait(dve, nm_psum, n)
                dve.tensor_copy(nparts[:, 0, :], nmax[:, :]).then_inc(nm_step, 1)
                dve.wait_ge(nm_step, 4 * n + 1)
                dve.tensor_tensor(nrest[:, :], nmax[:, :], nparts[:, 0, :], ALU.subtract).then_inc(nm_step, 1)
                dve.wait_ge(nm_step, 4 * n + 2)
                dve.tensor_copy(nparts[:, 1, :], nrest[:, :]).then_inc(nm_step, 1)
                dve.wait_ge(nm_step, 4 * n + 3)
                dve.tensor_tensor(nparts[:, 2, :], nrest[:, :], nparts[:, 1, :], ALU.subtract).then_inc(nm_step, 1)
                dve.wait_ge(nm_psum, n + 1)
                wait(dve, nm_in[(par + LAG) % 2], 16 * (cnt[1] - 1))
                dve.tensor_copy(nm_t[(par + LAG) % 2][:, :], nm_bank[0:3 * H, :]).then_inc(nm_done, 1)
            if norm_next and u == MAX_AT:
                dve_norm_context(dve, b + 3)

    def pool_slot(pool, b, par, has_e):
        if has_e:
            xb = sh.x[:, bass.ds(b, 1), :].rearrange("t o c -> t (o c)")
            if gate is None:
                pool.tensor_tensor(xb, xb, sh.brow[0:T, bo_row, :], ALU.add).then_inc(base_done, 1)
            else:
                wait(pool, base_done, b)
                pool.tensor_tensor(bog[:, :], sh.gate[gate][:, bass.ds(b, 1), :].rearrange("t o c -> t (o c)"),
                                   sh.brow[0:T, bo_row, :], ALU.mult).then_inc(bog_done, 1)
                pool.wait_ge(bog_done, b + 1)
                pool.tensor_tensor(xb, xb, bog[:, :], ALU.add).then_inc(base_done, 1)
        if cross and has_fill(b, K0):
            for m in range(CH):
                n = CH * (b + 2) + m
                pool.wait_ge(fill_read, fill_no(b, K0 + m) + 1)
                pool.tensor_tensor(kr[:, m, :], kf[:, m, :], kp[par][:, 0, m, :], ALU.subtract).then_inc(rest_done, 1)
                pool.wait_ge(mid_done, n + 1)
                pool.tensor_tensor(kp[par][:, 2, m, :], kr[:, m, :], kp[par][:, 1, m, :], ALU.subtract).then_inc(split[m], 3)
        if cross and has_fill(b, V0):
            for t, k in enumerate((V0, V0, V1)):
                if t != 1:
                    pool.wait_ge(fill_read, fill_no(b, k) + 1)
                v = sh.v_sb[1 - par][0:keys[t], t, :, 0:D]
                pool.tensor_tensor(v, v, sh.brow[0:keys[t], bv_row, :].rearrange("p (h d) -> p h d", d=D), ALU.add).then_inc(v_done, 1)

    def sp_load_half(sp, b, par, c):
        wait(sp, st_psum, NU * (b - 2) + (NU // 2) * (c + 1))
        sp.wait_ge(split[c], 3 * (b + 1))
        for s, w in enumerate(TERMS_K):
            sp.dma_start(sh.k_st[par][s * D:(s + 1) * D, c * HC:(c + 1) * HC, 0:L], kp[par][:, w, c, :]).then_inc(stacked[par][c], 16)

    def load_max(eng, b, par):
        eng.wait_ge(nm_done, b + 1)
        eng.dma_start(sh.q_all[DEEP:AUG, :, bass.ds(b * T, T)], nm_t[par][:, :]).then_inc(nm_in[par], 16)

    def sp_load_values(sp, b, par):
        wait(sp, pv_psum, NU * (b - 1))
        sp.dma_start(sh.v_sb[par][0:T, 0, :, :], sh.v_all[:, bass.ds(b, 1), :, :]).then_inc(v_loaded[par], 16)

    def sp_slot(sp, b, par, has_s, has_load):
        if has_load and cross:
            sp_load_half(sp, b + 2, par, 0)
        elif has_load:
            sp_load_values(sp, b + 2, par)
        if has_s and not cross:
            load_max(sp, b + LAG, (par + LAG) % 2)
        if has_load and cross:
            sp_load_half(sp, b + 2, par, 1)

    AHEAD = (-3, -2) if cross else ()

    def within(b, ahead):
        return not isinstance(b, int) or 0 <= b + ahead < B

    def run(slot, slots):
        for b in slots:
            slot(b, b % 2, (b // 2 + 1, (b + LAG) // 2 + 1))

    def run_main(eng, slot, before_loop=()):
        run(slot, range(-1 if cross else -2, 1))
        wait_all(eng, before_loop)
        with eng.Fori(0, 2) as i:
            slot(2 * i + 1, 1, (i + 1, i + 2))
            slot(2 * i + 2, 0, (i + 2, i + 1 + LAG))
        run(slot, range(5, B + 1))

    def on_tensor(pe):
        return lambda b, par, cnt: pe_slot(pe, b, par, cnt, within(b, 0), within(b, LAG), within(b, -1))

    def on_scalar(act):
        return lambda b, par, cnt: act_slot(act, b, par, cnt, within(b, 0), within(b, LAG), within(b, -1))

    def on_vector(dve):
        return lambda b, par, cnt: dve_slot(dve, b, par, cnt, within(b, LAG), within(b, -1), cross and within(b, 3))

    def on_gpsimd(pool):
        return lambda b, par, cnt: pool_slot(pool, b, par, within(b, 0))

    def on_sync(sp):
        return lambda b, par, cnt: sp_slot(sp, b, par, within(b, LAG), within(b, 2))


    def tensor_ahead(pe):
        wait_all(pe, ahead["tensor"])
        pe.wait_ge(w_ordered, CH)
        run(on_tensor(pe), AHEAD)

    def scalar_ahead(act):
        wait_all(act, ahead["scalar"])
        run(on_scalar(act), AHEAD)

    def vector_ahead(dve):
        wait_all(dve, ahead["vector"])
        w_heads = kr[:, :, 0:C]
        dve.tensor_copy(w_heads, wkv[:, :, 0:C]).then_inc(w_copied, 1)
        dve.wait_ge(w_copied, 1)
        for c in range(CH):
            dve.tensor_copy(wkv[:, c, 0:C].rearrange("p (m d h) -> p m d h", m=CH, h=HC),
                            w_heads[:, c, :].rearrange("p (m h d) -> p m d h", m=CH, d=D)).then_inc(w_ordered, 1)
        run(on_vector(dve), AHEAD)

    def gpsimd_pads(pool):
        for s in range(2):
            pool.memset(sh.k_st[s][:, :, L:], 0.0).then_inc(pad_set, 1)
        pool.wait_ge(pad_set, 2)

    def gpsimd_ones(pool, behind=None):
        if behind is not None:
            pool.wait_ge(split[behind], 3)
        for s in range(2):
            pool.memset(sh.k_st[s][DEEP:AUG, :, :], 1.0).then_inc(ones_set, 1)
        pool.wait_ge(ones_set, 2)

    def gpsimd_ahead(pool):
        run(on_gpsimd(pool), AHEAD)

    def sync_ahead(sp):
        sp.wait_ge(pad_set, 2)
        run(on_sync(sp), AHEAD)


    def tensor(pe):
        wait_all(pe, first["tensor"])
        pe.wait_ge(nparts_set, 1)
        if cross:
            pe.wait_ge(ones_set, 2)
        run_main(pe, on_tensor(pe), [(stacks.more["stacked"][1], stacks.more["stacked_count"])])

    def scalar(act):
        run_main(act, on_scalar(act))

    def vector(dve):
        dve.memset(nparts[:, 3:5, :], 0.0).then_inc(nparts_set, 1)
        dve.memset(nparts[:, 5:, :], 0.0).then_inc(tb_free, 1)
        run_main(dve, on_vector(dve))

    def gpsimd(pool):
        wait_all(pool, first["gpsimd"])
        run_main(pool, on_gpsimd(pool))

    def sync(sp):
        wait_all(sp, first["sync"])
        run_main(sp, on_sync(sp))

    return Parts(tensor, vector, scalar, gpsimd, sync, tensor_ahead=tensor_ahead, vector_ahead=vector_ahead,
                 scalar_ahead=scalar_ahead, gpsimd_ahead=gpsimd_ahead, sync_ahead=sync_ahead,
                 gpsimd_pads=gpsimd_pads, gpsimd_ones=gpsimd_ones)


def phase_mlp(nc, sh, out):
    N2 = 2 * T
    NH = HID // P
    with ExitStack() as ctx:
        semaphores = ctx.enter_context(Semaphores(nc))

        def sb(n, shape, dt=F32):
            return ctx.enter_context(nc.sbuf_tensor(f"mlp_{n}", shape, dt))

        def sem(n):
            return semaphores.new(f"mlp_{n}")

        w1, w2 = sh.w1, sh.w2
        stats, mv, veps, half, rstd, pause = sb("stats", [T, 2, 6]), sb("mv", [T, 2, 2]), sb("veps", [T, 2]), sb("half", [T, 2]), sb("rstd", [T, 2]), sb("pause", [T, 1])
        xn = sb("xn", [T, 2, C])
        xt = sb("xt", [P, CH, N2])
        hid = sb("hid", [P, NH, N2])
        y, yg, yo = sb("y", [T, 2, C]), sb("yg", [T, 2, C]), sb("yo", [T, 2, C])
        half_set, stats_done, aggr_done, veps_done, rstd_done, xn_done = (
            sem(n) for n in ("half_set", "stats_done", "aggr_done", "veps_done", "rstd_done", "xn_done"))
        xt_psum, xt_done, h_psum, hid_done, y_psum, y_step, stored = (
            sem(n) for n in ("xt_psum", "xt_done", "h_psum", "hid_done", "y_psum", "y_step", "stored"))
        xt_bank, y_bank = sh.bank[0], sh.bank[5:7]

        def norm(dve, p):
            for j in range(2):
                dve.bn_stats(stats[:, j, :], sh.x[:, bass.ds(2 * p + j, 1), :]).then_inc(stats_done, 1)
            dve.wait_ge(stats_done, 2 * p + 2)
            dve.memset(pause[:, :], 0.0)
            for j in range(2):
                dve.bn_aggr(mv[:, j, :], stats[:, j, :]).then_inc(aggr_done, 1)
            dve.wait_ge(aggr_done, 2 * p + 2)
            dve.tensor_scalar(veps[:, :], mv[:, :, 1], 1e-6, None, ALU.add).then_inc(veps_done, 1)
            dve.wait_ge(rstd_done, p + 1)
            wait(dve, xt_psum, p)
            for j in range(2):
                dve.tensor_scalar(xn[:, j, :], sh.x[:, bass.ds(2 * p + j, 1), :], mv[:, j, 0:1], rstd[:, j:j + 1],
                                  ALU.subtract, ALU.mult).then_inc(xn_done, 1)

        def modulate(dve, p):
            dve.wait_ge(xt_psum, p + 1)
            for c in range(CH):
                for j in range(2):
                    o = (c * 2 + j) * T
                    dve.tensor_scalar(xt[:, c, j * T:(j + 1) * T], xt_bank[:, o:o + T], sh.mod[:, 7, c, bass.ds(2 * p + j, 1)],
                                      sh.mod[:, 6, c, bass.ds(2 * p + j, 1)], ALU.mult, ALU.add).then_inc(xt_done, 1)

        def finish(dve, p):
            for j in range(2):
                n = 6 * p + 3 * j
                b = bass.ds(2 * p + j, 1)
                dve.wait_ge(y_psum, 2 * p + j + 1)
                dve.tensor_tensor(y[:, j, :], y_bank[j][0:T, 0:C], sh.brow[0:T, 6, :], ALU.add).then_inc(y_step, 1)
                dve.wait_ge(y_step, n + 1)
                dve.tensor_tensor(yg[:, j, :], y[:, j, :], sh.gate[1][:, b, :].rearrange("t o c -> t (o c)"), ALU.mult).then_inc(y_step, 1)
                dve.wait_ge(y_step, n + 2)
                if j == 0:
                    wait(dve, stored, 32 * p)
                dve.tensor_tensor(yo[:, j, :], yg[:, j, :], sh.x[:, b, :].rearrange("t o c -> t (o c)"), ALU.add).then_inc(y_step, 1)

        def transposes(pe, p):
            pe.wait_ge(xn_done, 2 * p + 2)
            wait(pe, xt_done, 4 * p)
            for c in range(CH):
                for j in range(2):
                    o = (c * 2 + j) * T
                    last = pe.transpose(xt_bank[:, o:o + T], xn[:, j, c * P:(c + 1) * P], sh.ident[0:T, 0:T])
            last.then_inc(xt_psum, 1)

        def first_matmuls(pe, p):
            pe.wait_ge(xt_done, 4 * p + 4)
            for m in range(NH):
                wait(pe, hid_done, NH * p + m - 3)
                for c in range(CH):
                    last = pe.matmul(sh.bank[1 + m % 4][:, 0:N2], w1[:, c, m * P:(m + 1) * P], xt[:, c, :],
                                     start=c == 0, stop=c == CH - 1)
                last.then_inc(h_psum, 1)

        def second_matmuls(pe, p):
            wait(pe, y_step, 6 * p - 2)
            for j in range(2):
                for m in range(NH):
                    if j == 0:
                        pe.wait_ge(hid_done, NH * p + m + 1)
                    last = pe.matmul(y_bank[j][0:T, 0:C], hid[:, m, j * T:(j + 1) * T], w2[:, m, :],
                                     start=m == 0, stop=m == NH - 1)
                last.then_inc(y_psum, 1)

        with nc.Block() as block:
            @block.sync
            def _(sp):
                with sp.Fori(0, PAIRS) as p:
                    for j in range(2):
                        sp.wait_ge(y_step, 6 * p + 3 * j + 3)
                        sp.dma_start(out[bass.ds(2 * p + j, 1)].rearrange("o n c -> n (o c)"), yo[:, j, :]).then_inc(stored, 16)
                sp.wait_ge(stored, 16 * B)

            @block.gpsimd
            def _(pool):
                pool.memset(half[:, :], -0.5).then_inc(half_set, 1)
                pool.wait_ge(half_set, 1)
                with pool.Fori(0, PAIRS) as p:
                    pool.wait_ge(veps_done, p + 1)
                    pool.tensor_tensor(rstd[:, :], veps[:, :], half[:, :], ALU.pow).then_inc(rstd_done, 1)

            @block.vector
            def _(dve):
                norm(dve, 0)
                modulate(dve, 0)
                norm(dve, 1)
                modulate(dve, 1)
                finish(dve, 0)
                with dve.Fori(1, PAIRS - 1) as p:
                    norm(dve, p + 1)
                    modulate(dve, p + 1)
                    finish(dve, p)
                finish(dve, PAIRS - 1)

            @block.scalar
            def _(act):
                def hidden(p):
                    for m in range(NH):
                        act.wait_ge(h_psum, NH * p + m + 1)
                        if m == 0:
                            wait(act, y_psum, 2 * p)
                        act.activation(hid[:, m, :], sh.bank[1 + m % 4][:, 0:N2], ACT.Gelu_apprx_tanh,
                                       bias=sh.bhid[:, m:m + 1]).then_inc(hid_done, 1)
                hidden(0)
                with act.Fori(1, PAIRS) as p:
                    hidden(p)

            @block.tensor
            def _(pe):
                transposes(pe, 0)
                first_matmuls(pe, 0)
                transposes(pe, 1)
                second_matmuls(pe, 0)
                with pe.Fori(1, PAIRS - 1) as p:
                    first_matmuls(pe, p)
                    transposes(pe, p + 1)
                    second_matmuls(pe, p)
                first_matmuls(pe, PAIRS - 1)
                second_matmuls(pe, PAIRS - 1)


def modulation(sh, m):
    return lambda c, b: sh.mod[:, m, c, b:b + 1]


def first_layer(nc, sh, ins):
    with ExitStack() as ctx:
        sems = ctx.enter_context(Semaphores(nc))
        ld = load(nc, sh, ctx, sems, ins)
        md = modulate_second(nc, sh, ctx, sems, ins)
        NM = 4 * CH
        pj = project(nc, sh, ctx, sems, "p0", 1e-5, modulation(sh, 0), modulation(sh, 1), sh.wq0, sh.bcol[:, 0, :], False,
                     {"xn": Room(sh.v_space), "xt": Room(sh.gate_space[0]), "full": Room(sh.gate_space[1]), "rest": Room(sh.gate_space[1][:, 1024:])},
                     tensor_first=[(sh.wq_in, 16 * 8)], mod_first=[(sh.mod_done, NM)], bank_first=[(sh.mod_done, NM)])
        w_all = 16 * 13
        at = attend(nc, sh, ctx, sems, "a0", True, True, sh.wkv0, sh.bcol[:, 1, :], 0, sh.wo0, 1, None, pj, {
            "tensor": pj.more["banks_read"] + md.more["banks_read"] + [(sh.consts_done, 4)],
            "gpsimd": pj.more["x_read"], "sync": []}, {
            "tensor": [(sh.w_in, w_all), (sh.mod_done, NM)], "scalar": [(sh.mod_done, NM), (sh.w_in, w_all)],
            "vector": [(sh.ctx_stats_done, 2), (sh.w_in, w_all)]})
        block = ctx.enter_context(nc.Block())

        @block.sync
        def _(sp):
            ld.sync(sp)
            md.sync(sp)
            pj.sync(sp)
            at.more["sync_ahead"](sp)
            md.more["sync_gates"](sp)
            at.sync(sp)
            sp.wait_ge(md.more["gate_dram"], 16)
            sp.wait_ge(sh.late_in, 16 * 5)

        @block.gpsimd
        def _(pool):
            ld.gpsimd(pool)
            at.more["gpsimd_pads"](pool)
            at.more["gpsimd_ones"](pool)
            pj.gpsimd(pool)
            ld.more["gpsimd_late"](pool)
            at.more["gpsimd_ahead"](pool)
            at.gpsimd(pool)

        @block.scalar
        def _(act):
            ld.scalar(act)
            pj.scalar(act)
            at.more["scalar_ahead"](act)
            at.scalar(act)

        @block.vector
        def _(dve):
            ld.vector(dve)
            pj.more["vector_norm"](dve, [(sh.wq_in, 16 * 8), (sh.x_in, 32)])
            ld.more["vector_mod"](dve)
            pj.more["vector_modulate"](dve)
            ld.more["vector_late"](dve)
            pj.vector(dve, [0])
            at.more["vector_ahead"](dve)
            pj.vector(dve, [1])
            md.vector(dve)
            at.vector(dve)

        @block.tensor
        def _(pe):
            ld.tensor(pe)
            pj.tensor(pe)
            md.tensor(pe)
            at.more["tensor_ahead"](pe)
            at.tensor(pe)


def self_attention(nc, sh):
    with ExitStack() as ctx:
        sems = ctx.enter_context(Semaphores(nc))
        gate_in = sems.new("gate_in")
        stack = Room(sh.k_space)
        pj = project(nc, sh, ctx, sems, "p1", 1e-6, modulation(sh, 5), modulation(sh, 4), sh.wqkv1, sh.bcol[:, 2, :], True,
                     {n: stack for n in ("full", "rest", "part")})
        pad_set = sems.new("pad_set")
        at = attend(nc, sh, ctx, sems, "a1", False, False, None, None, 2, sh.wo1, 3, 0, pj, {
            "tensor": pj.more["banks_read"], "gpsimd": pj.more["x_read"] + [(gate_in, 32)],
            "sync": pj.more["banks_read"] + [(pad_set, 3)]})
        block = ctx.enter_context(nc.Block())

        @block.sync
        def _(sp):
            for g in range(2):
                sp.dma_start(sh.gate[g], sh.dram["gate"][:, g, :].partition_broadcast(T)).then_inc(gate_in, 16)
            pj.sync(sp)
            at.sync(sp)

        @block.gpsimd
        def _(pool):
            pj.gpsimd(pool)
            pool.memset(sh.k_all[:, :, B * T:], 0.0).then_inc(pad_set, 1)
            pool.memset(sh.v_all[:, :, :, D:D + 1], 1.0).then_inc(pad_set, 1)
            pool.wait_ge(pad_set, 2)
            pool.memset(sh.k_all[96:AUG, :, :], 1.0).then_inc(pad_set, 1)
            pool.wait_ge(pad_set, 3)
            at.gpsimd(pool)

        @block.scalar
        def _(act):
            pj.scalar(act)
            at.scalar(act)

        @block.vector
        def _(dve):
            pj.more["vector_norm"](dve)
            pj.more["vector_modulate"](dve)
            pj.vector(dve)
            at.vector(dve)

        @block.tensor
        def _(pe):
            pj.tensor(pe)
            pe.wait_ge(pad_set, 3)
            at.tensor(pe)


def cross_attention(nc, sh, ins):
    with ExitStack() as ctx:
        sems = ctx.enter_context(Semaphores(nc))
        mlp_in = sems.new("mlp_in")
        pj = project(nc, sh, ctx, sems, "p2", 1e-6, lambda c, b: sh.bcol[:, 4, c:c + 1], lambda c, b: sh.bcol[:, 5, c:c + 1],
                     sh.wq2, sh.bcol[:, 6, :], False, {"xn": Room(sh.v_space), "xt": Room(sh.gate_space[0])})
        at = attend(nc, sh, ctx, sems, "a2", True, False, sh.wkv2, sh.bcol[:, 7, :], 4, sh.wo2, 5, None, pj, {
            "tensor": pj.more["banks_read"], "gpsimd": pj.more["x_read"], "sync": []}, {"tensor": [], "scalar": [], "vector": []})
        block = ctx.enter_context(nc.Block())

        @block.sync
        def _(sp):
            sp.dma_start(sh.w1, ins["L1_xcond_mlp_w1"].rearrange("(k p) n -> p k n", p=P)).then_inc(mlp_in, 16)
            sp.dma_start(sh.w2, ins["L1_xcond_mlp_w2"].rearrange("(k p) n -> p k n", p=P)).then_inc(mlp_in, 16)
            at.more["sync_ahead"](sp)
            pj.sync(sp)
            at.sync(sp)
            sp.wait_ge(mlp_in, 32)

        @block.gpsimd
        def _(pool):
            at.more["gpsimd_pads"](pool)
            pj.gpsimd(pool)
            at.more["gpsimd_ahead"](pool)
            at.more["gpsimd_ones"](pool, behind=CH - 1)
            at.gpsimd(pool)

        @block.scalar
        def _(act):
            at.more["scalar_ahead"](act)
            pj.scalar(act)
            at.scalar(act)

        @block.vector
        def _(dve):
            at.more["vector_ahead"](dve)
            pj.more["vector_norm"](dve)
            pj.more["vector_modulate"](dve)
            pj.vector(dve)
            at.vector(dve)

        @block.tensor
        def _(pe):
            at.more["tensor_ahead"](pe)
            pj.tensor(pe)
            at.tensor(pe)


def build(nc, ins, out):
    dram = {
        "q_parts": nc.dram_tensor("q_parts", (B // QUAD, 3, CH, P, QUAD * T), BF16, kind="Internal").ap(),
        "k_parts": nc.dram_tensor("k_parts", (B // QUAD, 3, CH, P, QUAD * T), BF16, kind="Internal").ap(),
        "gate": nc.dram_tensor("gate_rows", (B, 2, C), F32, kind="Internal").ap(),
    }
    with ExitStack() as ctx:
        sh = allocate(nc, ctx, dram)
        first_layer(nc, sh, ins)
        self_attention(nc, sh)
        cross_attention(nc, sh, ins)
        phase_mlp(nc, sh, out)


_OUT = ((B, T, C), "float32")


def kernel(**inputs):
    import numpy as _np
    import concourse.bacc as _bacc
    from concourse import mybir as _mybir
    from concourse.bass_utils import run_bass_kernel_spmd as _run

    nc = _bacc.Bacc("TRN2", target_bir_lowering=False, num_devices=1)
    arrays, ins = {}, {}
    for name, value in inputs.items():
        a = _np.ascontiguousarray(value)
        arrays[f"in_{name}_dram"] = a
        ins[name] = nc.dram_tensor(f"in_{name}_dram", a.shape, _mybir.dt.from_np(a.dtype), kind="ExternalInput").ap()
    out = nc.dram_tensor("out_0_dram", _OUT[0], _mybir.dt.from_np(_np.dtype(_OUT[1])), kind="ExternalOutput").ap()
    build(nc, ins, out)
    r = _run(nc, [arrays], core_ids=[0])
    return r.results[0]["out_0_dram"]
```
